# Optimizing a Trainium2 kernel written in Bass

```python
import numpy as np
import jax
import jax.numpy as jnp

def _softmax(x, axis=-1):
    return jax.nn.softmax(x, axis=axis)

def _gelu(x):
    return jax.nn.gelu(x, approximate=True)

def _silu(x):
    return jax.nn.silu(x)

def _sigmoid(x):
    return jax.nn.sigmoid(x)

def _layernorm(x, axis=-1, eps=1e-05):
    m = jnp.mean(x, axis=axis, keepdims=True)
    v = jnp.var(x, axis=axis, keepdims=True)
    return (x - m) / jnp.sqrt(v + eps)

def _scatter_add(tgt, idx, src, axis=0):
    return tgt.at[idx].add(src)

def _segment_sum(src, seg, n):
    return jax.ops.segment_sum(src, seg, n)
kernel_name = 'mk_conv_attn_hybrid_d4_conv_nchw1024_r4_160d8e'

def setup_inputs(seed: int=0):
    np.random.seed(seed)
    _w = jnp.asarray

    def _rec_inputs():
        import jax
        import jax.numpy as jnp
        _gk = jax.random.key(seed)
        x = -0.0003957 + 1 * jax.random.normal(jax.random.fold_in(_gk, 1), (16, 256, 14, 14), jnp.float32)
        return x
    x = _rec_inputs()

    def _L0_conv_setup():
        import jax, jax.numpy as jnp
        import numpy as np
        EPS = 1e-05

        def _conv(x, w, b, stride, pad):
            y = jax.lax.conv_general_dilated(x, w, window_strides=(stride, stride), padding=[(pad, pad), (pad, pad)], dimension_numbers=('NCHW', 'OIHW', 'NCHW'))
            return y + b.reshape(1, -1, 1, 1)

        def _bn(x, gamma, beta):
            mean = jnp.mean(x, axis=(0, 2, 3), keepdims=True)
            var = jnp.var(x, axis=(0, 2, 3), keepdims=True)
            xn = (x - mean) * jax.lax.rsqrt(var + EPS)
            return gamma.reshape(1, -1, 1, 1) * xn + beta.reshape(1, -1, 1, 1)
        key = jax.random.key(seed)
        ks = jax.random.split(key, 8)
        N, Cin, H, W = (16, 256, 14, 14)
        P = 64
        Cout = P * 4

        def kaiming(k, shape):
            fan_in = shape[1] * shape[2] * shape[3]
            return jax.random.normal(k, shape, jnp.float32) * np.float32(np.sqrt(2.0 / fan_in))
        return {'x': jax.random.normal(ks[0], (N, Cin, H, W), jnp.float32), 'w1': kaiming(ks[1], (P, Cin, 1, 1)), 'b1': jnp.zeros((P,), jnp.float32), 'g1': jnp.ones((P,), jnp.float32), 'be1': jnp.zeros((P,), jnp.float32), 'w2': kaiming(ks[2], (P, P, 3, 3)), 'b2': jnp.zeros((P,), jnp.float32), 'g2': jnp.ones((P,), jnp.float32), 'be2': jnp.zeros((P,), jnp.float32), 'w3': kaiming(ks[3], (Cout, P, 1, 1)), 'b3': jnp.zeros((Cout,), jnp.float32), 'g3': jnp.ones((Cout,), jnp.float32), 'be3': jnp.zeros((Cout,), jnp.float32), 'residual_scale': jnp.zeros((1,), jnp.float32)}
    _L0_conv_all = _L0_conv_setup()
    _L0_conv_in = {k: v for k, v in _L0_conv_all.items() if k in ('w1', 'b1', 'g1', 'be1', 'w2', 'b2', 'g2', 'be2', 'w3', 'b3', 'g3', 'be3', 'residual_scale')}
    del _L0_conv_all

    def _L1_conv_setup():
        import jax, jax.numpy as jnp
        import numpy as np
        EPS = 1e-05

        def conv1x1(x, W, b):
            return jnp.einsum('bchw,oc->bohw', x, W) + b[None, :, None, None]

        def bn(x, gamma, beta, mean, var):
            inv = gamma / jnp.sqrt(var + EPS)
            return x * inv[None, :, None, None] + (beta - mean * inv)[None, :, None, None]
        key = jax.random.key(seed)
        ks = jax.random.split(key, 16)
        B, C, H, W = (16, 256, 48, 48)
        mid = C // 4
        s = 1.0 / np.sqrt(C)
        inp = {'x': jax.random.normal(ks[0], (B, C, H, W), jnp.float32), 'Wf': jax.random.normal(ks[1], (mid, C), jnp.float32) * s, 'bf': jnp.zeros((mid,), jnp.float32), 'gf': jnp.ones((mid,), jnp.float32), 'btf': jnp.zeros((mid,), jnp.float32), 'mf': jax.random.normal(ks[2], (mid,), jnp.float32) * 0.1, 'vf': jax.random.uniform(ks[3], (mid,), jnp.float32, 0.5, 1.5), 'Wg': jax.random.normal(ks[4], (mid, C), jnp.float32) * s, 'bg': jnp.zeros((mid,), jnp.float32), 'gg': jnp.ones((mid,), jnp.float32), 'btg': jnp.zeros((mid,), jnp.float32), 'mg': jax.random.normal(ks[5], (mid,), jnp.float32) * 0.1, 'vg': jax.random.uniform(ks[6], (mid,), jnp.float32, 0.5, 1.5), 'Wh': jax.random.normal(ks[7], (mid, C), jnp.float32) * s, 'bh': jnp.zeros((mid,), jnp.float32), 'Wv': jax.random.normal(ks[8], (C, mid), jnp.float32) * (1.0 / np.sqrt(mid)), 'bv': jnp.zeros((C,), jnp.float32)}
        return inp
    _L1_conv_all = _L1_conv_setup()
    _L1_conv_in = {k: v for k, v in _L1_conv_all.items() if k in ('Wf', 'bf', 'gf', 'btf', 'mf', 'vf', 'Wg', 'bg', 'gg', 'btg', 'mg', 'vg', 'Wh', 'bh', 'Wv', 'bv')}
    del _L1_conv_all

    def _L2_attn_setup():
        import jax, jax.numpy as jnp
        import numpy as np
        N_HEAD = 16
        N_EMBED = 256
        key = jax.random.key(seed)
        k0, k1, k2 = jax.random.split(key, 3)
        B, T, C = (4, 512, N_EMBED)
        x = jax.random.normal(k0, (B, T, C), jnp.float32)
        w_attn = jax.random.normal(k1, (C, 3 * C), jnp.float32) * 0.02
        b_attn = jnp.zeros((3 * C,), jnp.float32)
        w_proj = jax.random.normal(k2, (C, C), jnp.float32) * 0.02
        b_proj = jnp.zeros((C,), jnp.float32)
        return {'x': x, 'w_attn': w_attn, 'b_attn': b_attn, 'w_proj': w_proj, 'b_proj': b_proj}
    _L2_attn_all = _L2_attn_setup()
    _L2_attn_in = {k: v for k, v in _L2_attn_all.items() if k in ('w_attn', 'b_attn', 'w_proj', 'b_proj')}
    del _L2_attn_all

    def _L2_ffn_setup():
        import jax, jax.numpy as jnp
        import numpy as np
        EPS = 1e-05
        HEADS = 8
        DIM_KEY = 32
        K = 16
        NUM_KEYS = 64
        key = jax.random.key(seed)
        ks = jax.random.split(key, 5)
        B, T, D = (1, 256, 256)
        x = jax.random.normal(ks[0], (B, T, D), dtype=jnp.float32)
        norm_w = jnp.ones((D,), dtype=jnp.float32)
        wq = jax.random.normal(ks[1], (D, DIM_KEY * HEADS * 2), dtype=jnp.float32) * 0.02
        keys = jax.random.normal(ks[2], (HEADS, NUM_KEYS, 2, DIM_KEY), dtype=jnp.float32) * 0.02
        expert_down = jax.random.normal(ks[3], (NUM_KEYS * NUM_KEYS, D), dtype=jnp.float32) * 0.02
        expert_up = jax.random.normal(ks[4], (NUM_KEYS * NUM_KEYS, D), dtype=jnp.float32) * 0.02
        return {'x': x, 'norm_w': norm_w, 'wq': wq, 'keys': keys, 'expert_down': expert_down, 'expert_up': expert_up}
    _L2_ffn_all = _L2_ffn_setup()
    _L2_ffn_in = {k: v for k, v in _L2_ffn_all.items() if k in ('norm_w', 'wq', 'keys', 'expert_down', 'expert_up')}
    del _L2_ffn_all

    def _L3_attn_setup():
        import jax, jax.numpy as jnp
        import numpy as np
        HEADS = 8
        DIM_HEAD = 16
        SCALE = DIM_HEAD ** (-0.5)
        key = jax.random.key(seed)
        ks = jax.random.split(key, 6)
        b, n, d = (2, 1024, 256)
        inner = HEADS * DIM_HEAD
        x = jax.random.normal(ks[0], (b, n, d), dtype=jnp.float32)
        Wq = jax.random.normal(ks[1], (d, inner), dtype=jnp.float32) * d ** (-0.5)
        Wk = jax.random.normal(ks[2], (d, inner), dtype=jnp.float32) * d ** (-0.5)
        Wv = jax.random.normal(ks[3], (d, inner), dtype=jnp.float32) * d ** (-0.5)
        Wout = jax.random.normal(ks[4], (inner, d), dtype=jnp.float32) * inner ** (-0.5)
        bout = jnp.zeros((d,), dtype=jnp.float32)
        return {'x': x, 'Wq': Wq, 'Wk': Wk, 'Wv': Wv, 'Wout': Wout, 'bout': bout}
    _L3_attn_all = _L3_attn_setup()
    _L3_attn_in = {k: v for k, v in _L3_attn_all.items() if k in ('Wq', 'Wk', 'Wv', 'Wout', 'bout')}
    del _L3_attn_all

    def _L3_ffn_setup():
        import jax, jax.numpy as jnp
        import numpy as np
        MIN_EXPERT_CAPACITY = 4
        CAPACITY_FACTOR = 1.0

        def _moe_forward(x, router_w, w1, b1, w2, b2):
            B, S, D = x.shape
            E = router_w.shape[1]
            G = 1
            T = B * S
            C = max(int(round(CAPACITY_FACTOR * T / E)), MIN_EXPERT_CAPACITY)
            xt = x.reshape(G, T, D)
            logits = jnp.einsum('gtd,de->gte', xt, router_w)
            probs = jax.nn.softmax(logits, axis=-1)
            gate = jnp.max(probs, axis=-1)
            idx = jnp.argmax(probs, axis=-1)
            emask = jax.nn.one_hot(idx, E, dtype=x.dtype)
            pos = jnp.cumsum(emask, axis=1) * emask - 1.0
            pos = pos.astype(jnp.int32)
            slot = jax.nn.one_hot(pos, C, dtype=x.dtype)
            dispatch = emask[..., None] * slot
            combine = dispatch * gate[..., None, None]
            expert_inputs = jnp.einsum('gtd,gtec->gecd', xt, dispatch)
            h = jax.nn.relu(jnp.einsum('gecd,edf->gecf', expert_inputs, w1) + b1[None, :, None, :])
            expert_outputs = jnp.einsum('gecf,efd->gecd', h, w2) + b2[None, :, None, :]
            out = jnp.einsum('gecd,gtec->gtd', expert_outputs, combine)
            return out.reshape(B, S, D)
        key = jax.random.key(seed)
        k0, k1, k2, k3 = jax.random.split(key, 4)
        B, S, D, E, F = (4, 512, 256, 8, 1024)
        x = jax.random.normal(k0, (B, S, D), dtype=jnp.float32)
        router_w = jax.random.normal(k1, (D, E), dtype=jnp.float32) * D ** (-0.5)
        w1 = jax.random.normal(k2, (E, D, F), dtype=jnp.float32) * D ** (-0.5)
        b1 = jnp.zeros((E, F), dtype=jnp.float32)
        w2 = jax.random.normal(k3, (E, F, D), dtype=jnp.float32) * F ** (-0.5)
        b2 = jnp.zeros((E, D), dtype=jnp.float32)
        return {'x': x, 'router_w': router_w, 'w1': w1, 'b1': b1, 'w2': w2, 'b2': b2}
    _L3_ffn_all = _L3_ffn_setup()
    _L3_ffn_in = {k: v for k, v in _L3_ffn_all.items() if k in ('router_w', 'w1', 'b1', 'w2', 'b2')}
    del _L3_ffn_all
    return {'x': x, 'L0_conv_w1': _L0_conv_in['w1'], 'L0_conv_b1': _L0_conv_in['b1'], 'L0_conv_g1': _L0_conv_in['g1'], 'L0_conv_be1': _L0_conv_in['be1'], 'L0_conv_w2': _L0_conv_in['w2'], 'L0_conv_b2': _L0_conv_in['b2'], 'L0_conv_g2': _L0_conv_in['g2'], 'L0_conv_be2': _L0_conv_in['be2'], 'L0_conv_w3': _L0_conv_in['w3'], 'L0_conv_b3': _L0_conv_in['b3'], 'L0_conv_g3': _L0_conv_in['g3'], 'L0_conv_be3': _L0_conv_in['be3'], 'L0_conv_residual_scale': _L0_conv_in['residual_scale'], 'L1_conv_Wf': _L1_conv_in['Wf'], 'L1_conv_bf': _L1_conv_in['bf'], 'L1_conv_gf': _L1_conv_in['gf'], 'L1_conv_btf': _L1_conv_in['btf'], 'L1_conv_mf': _L1_conv_in['mf'], 'L1_conv_vf': _L1_conv_in['vf'], 'L1_conv_Wg': _L1_conv_in['Wg'], 'L1_conv_bg': _L1_conv_in['bg'], 'L1_conv_gg': _L1_conv_in['gg'], 'L1_conv_btg': _L1_conv_in['btg'], 'L1_conv_mg': _L1_conv_in['mg'], 'L1_conv_vg': _L1_conv_in['vg'], 'L1_conv_Wh': _L1_conv_in['Wh'], 'L1_conv_bh': _L1_conv_in['bh'], 'L1_conv_Wv': _L1_conv_in['Wv'], 'L1_conv_bv': _L1_conv_in['bv'], 'L2_attn_w_attn': _L2_attn_in['w_attn'], 'L2_attn_b_attn': _L2_attn_in['b_attn'], 'L2_attn_w_proj': _L2_attn_in['w_proj'], 'L2_attn_b_proj': _L2_attn_in['b_proj'], 'L2_ffn_norm_w': _L2_ffn_in['norm_w'], 'L2_ffn_wq': _L2_ffn_in['wq'], 'L2_ffn_keys': _L2_ffn_in['keys'], 'L2_ffn_expert_down': _L2_ffn_in['expert_down'], 'L2_ffn_expert_up': _L2_ffn_in['expert_up'], 'L3_attn_Wq': _L3_attn_in['Wq'], 'L3_attn_Wk': _L3_attn_in['Wk'], 'L3_attn_Wv': _L3_attn_in['Wv'], 'L3_attn_Wout': _L3_attn_in['Wout'], 'L3_attn_bout': _L3_attn_in['bout'], 'L3_ffn_router_w': _L3_ffn_in['router_w'], 'L3_ffn_w1': _L3_ffn_in['w1'], 'L3_ffn_b1': _L3_ffn_in['b1'], 'L3_ffn_w2': _L3_ffn_in['w2'], 'L3_ffn_b2': _L3_ffn_in['b2']}

def reference(x, L0_conv_w1, L0_conv_b1, L0_conv_g1, L0_conv_be1, L0_conv_w2, L0_conv_b2, L0_conv_g2, L0_conv_be2, L0_conv_w3, L0_conv_b3, L0_conv_g3, L0_conv_be3, L0_conv_residual_scale, L1_conv_Wf, L1_conv_bf, L1_conv_gf, L1_conv_btf, L1_conv_mf, L1_conv_vf, L1_conv_Wg, L1_conv_bg, L1_conv_gg, L1_conv_btg, L1_conv_mg, L1_conv_vg, L1_conv_Wh, L1_conv_bh, L1_conv_Wv, L1_conv_bv, L2_attn_w_attn, L2_attn_b_attn, L2_attn_w_proj, L2_attn_b_proj, L2_ffn_norm_w, L2_ffn_wq, L2_ffn_keys, L2_ffn_expert_down, L2_ffn_expert_up, L3_attn_Wq, L3_attn_Wk, L3_attn_Wv, L3_attn_Wout, L3_attn_bout, L3_ffn_router_w, L3_ffn_w1, L3_ffn_b1, L3_ffn_w2, L3_ffn_b2):
    import jax
    import jax.numpy as jnp

    def _L0_conv_ref(x, w1, b1, g1, be1, w2, b2, g2, be2, w3, b3, g3, be3, residual_scale):
        import jax, jax.numpy as jnp
        import numpy as np
        EPS = 1e-05

        def _conv(x, w, b, stride, pad):
            y = jax.lax.conv_general_dilated(x, w, window_strides=(stride, stride), padding=[(pad, pad), (pad, pad)], dimension_numbers=('NCHW', 'OIHW', 'NCHW'))
            return y + b.reshape(1, -1, 1, 1)

        def _bn(x, gamma, beta):
            mean = jnp.mean(x, axis=(0, 2, 3), keepdims=True)
            var = jnp.var(x, axis=(0, 2, 3), keepdims=True)
            xn = (x - mean) * jax.lax.rsqrt(var + EPS)
            return gamma.reshape(1, -1, 1, 1) * xn + beta.reshape(1, -1, 1, 1)
        out = jax.nn.relu(_bn(_conv(x, w1, b1, 1, 0), g1, be1))
        out = jax.nn.relu(_bn(_conv(out, w2, b2, 1, 1), g2, be2))
        out = _bn(_conv(out, w3, b3, 1, 0), g3, be3)
        out = jax.nn.softplus(residual_scale)[0] * out
        out = x + out
        return jax.nn.relu(out)

    def _L1_conv_ref(x, Wf, bf, gf, btf, mf, vf, Wg, bg, gg, btg, mg, vg, Wh, bh, Wv, bv):
        import jax, jax.numpy as jnp
        import numpy as np
        EPS = 1e-05

        def conv1x1(x, W, b):
            return jnp.einsum('bchw,oc->bohw', x, W) + b[None, :, None, None]

        def bn(x, gamma, beta, mean, var):
            inv = gamma / jnp.sqrt(var + EPS)
            return x * inv[None, :, None, None] + (beta - mean * inv)[None, :, None, None]
        B, C, H, W = x.shape
        mid = Wf.shape[0]
        HW = H * W
        f_x = jax.nn.relu(bn(conv1x1(x, Wf, bf), gf, btf, mf, vf)).reshape(B, mid, HW)
        g_x = jax.nn.relu(bn(conv1x1(x, Wg, bg), gg, btg, mg, vg)).reshape(B, mid, HW)
        h_x = conv1x1(x, Wh, bh).reshape(B, mid, HW)
        scale = mid ** (-0.5)
        z = jnp.einsum('bci,bcj->bij', f_x, g_x)
        attn = jax.nn.softmax(scale * z, axis=-1)
        z = jnp.einsum('bij,bcj->bci', attn, h_x)
        z = z.reshape(B, mid, H, W)
        z = conv1x1(z, Wv, bv)
        return z + x

    def _L2_attn_ref(x, w_attn, b_attn, w_proj, b_proj):
        import jax, jax.numpy as jnp
        import numpy as np
        N_HEAD = 16
        N_EMBED = 256
        B, T, C = x.shape
        H = N_HEAD
        attn = x @ w_attn + b_attn
        q, k, v = jnp.split(attn, 3, axis=-1)
        q = q.reshape(B, T, H, -1).transpose(0, 2, 1, 3)
        k = k.reshape(B, T, H, -1).transpose(0, 2, 1, 3)
        v = v.reshape(B, T, H, -1).transpose(0, 2, 1, 3)
        qk = jnp.einsum('bhqd,bhkd->bhqk', q, k)
        causal = jnp.tril(jnp.ones((T, T), dtype=bool))
        qk = jnp.where(causal, qk, -jnp.inf)
        p = jax.nn.softmax(qk, axis=-1) * C ** (-0.5)
        o = jnp.einsum('bhqk,bhkd->bhqd', p, v)
        o = o.transpose(0, 2, 1, 3).reshape(B, T, C)
        return o @ w_proj + b_proj

    def _L2_ffn_ref(x, norm_w, wq, keys, expert_down, expert_up):
        import jax, jax.numpy as jnp
        import numpy as np
        EPS = 1e-05
        HEADS = 8
        DIM_KEY = 32
        K = 16
        NUM_KEYS = 64
        B, T, D = x.shape
        inv = jax.lax.rsqrt(jnp.mean(x * x, axis=-1, keepdims=True) + EPS)
        x_norm = x * inv * norm_w
        q = (x_norm @ wq).reshape(B, T, HEADS, 2, DIM_KEY)
        sim = jnp.einsum('bthpd,hkpd->pbthk', q, keys)
        s1, i1 = jax.lax.top_k(sim[0], K)
        s2, i2 = jax.lax.top_k(sim[1], K)
        all_idx = (i1[..., :, None] * NUM_KEYS + i2[..., None, :]).reshape(B, T, HEADS, K * K)
        all_scores = (s1[..., :, None] + s2[..., None, :]).reshape(B, T, HEADS, K * K)
        final_scores, pk = jax.lax.top_k(all_scores, K)
        final_idx = jnp.take_along_axis(all_idx, pk, axis=-1)
        wd = expert_down[final_idx]
        wu = expert_up[final_idx]
        hidden = jnp.einsum('btd,bthkd->bthk', x_norm, wd)
        hidden = jax.nn.gelu(hidden, approximate=False)
        hidden = hidden * jax.nn.relu(final_scores)
        out = jnp.einsum('bthk,bthkd->btd', hidden, wu)
        return out

    def _L3_attn_ref(x, Wq, Wk, Wv, Wout, bout):
        import jax, jax.numpy as jnp
        import numpy as np
        HEADS = 8
        DIM_HEAD = 16
        SCALE = DIM_HEAD ** (-0.5)
        b, n, _ = x.shape
        h, dh = (HEADS, DIM_HEAD)
        q = (x @ Wq).reshape(b, n, h, dh).transpose(0, 2, 1, 3)
        k = (x @ Wk).reshape(b, n, h, dh).transpose(0, 2, 1, 3)
        v = (x @ Wv).reshape(b, n, h, dh).transpose(0, 2, 1, 3)
        sim = jnp.einsum('bhid,bhjd->bhij', q, k) * SCALE
        attn = jax.nn.softmax(sim, axis=-1)
        out = jnp.einsum('bhij,bhjd->bhid', attn, v)
        out = out.transpose(0, 2, 1, 3).reshape(b, n, h * dh)
        return out @ Wout + bout

    def _L3_ffn_ref(x, router_w, w1, b1, w2, b2):
        import jax, jax.numpy as jnp
        import numpy as np
        MIN_EXPERT_CAPACITY = 4
        CAPACITY_FACTOR = 1.0

        def _moe_forward(x, router_w, w1, b1, w2, b2):
            B, S, D = x.shape
            E = router_w.shape[1]
            G = 1
            T = B * S
            C = max(int(round(CAPACITY_FACTOR * T / E)), MIN_EXPERT_CAPACITY)
            xt = x.reshape(G, T, D)
            logits = jnp.einsum('gtd,de->gte', xt, router_w)
            probs = jax.nn.softmax(logits, axis=-1)
            gate = jnp.max(probs, axis=-1)
            idx = jnp.argmax(probs, axis=-1)
            emask = jax.nn.one_hot(idx, E, dtype=x.dtype)
            pos = jnp.cumsum(emask, axis=1) * emask - 1.0
            pos = pos.astype(jnp.int32)
            slot = jax.nn.one_hot(pos, C, dtype=x.dtype)
            dispatch = emask[..., None] * slot
            combine = dispatch * gate[..., None, None]
            expert_inputs = jnp.einsum('gtd,gtec->gecd', xt, dispatch)
            h = jax.nn.relu(jnp.einsum('gecd,edf->gecf', expert_inputs, w1) + b1[None, :, None, :])
            expert_outputs = jnp.einsum('gecf,efd->gecd', h, w2) + b2[None, :, None, :]
            out = jnp.einsum('gecd,gtec->gtd', expert_outputs, combine)
            return out.reshape(B, S, D)
        return _moe_forward(x, router_w, w1, b1, w2, b2)

    def _gn(v, G=32, eps=1e-05):
        B_, C_, H_, W_ = v.shape
        g = v.reshape(B_, G, C_ // G, H_, W_)
        m = jnp.mean(g, axis=(2, 3, 4), keepdims=True)
        s = jnp.var(g, axis=(2, 3, 4), keepdims=True)
        return ((g - m) / jnp.sqrt(s + eps)).reshape(v.shape)

    def _ln_c(v, eps=1e-06):
        m = jnp.mean(v, axis=1, keepdims=True)
        s = jnp.var(v, axis=1, keepdims=True)
        return (v - m) / jnp.sqrt(s + eps)

    def _ln_t(v, eps=1e-05):
        m = jnp.mean(v, axis=-1, keepdims=True)
        s = jnp.var(v, axis=-1, keepdims=True)
        return (v - m) / jnp.sqrt(s + eps)

    def _to_tokens(v):
        B_, C_, H_, W_ = v.shape
        return v.reshape(B_, C_, H_ * W_).transpose(0, 2, 1)

    def _from_tokens(t, like):
        B_, C_, H_, W_ = like.shape
        return t.transpose(0, 2, 1).reshape(B_, C_, H_, W_)
    x = _L0_conv_ref(x, L0_conv_w1, L0_conv_b1, L0_conv_g1, L0_conv_be1, L0_conv_w2, L0_conv_b2, L0_conv_g2, L0_conv_be2, L0_conv_w3, L0_conv_b3, L0_conv_g3, L0_conv_be3, L0_conv_residual_scale)
    x = _L1_conv_ref(x, L1_conv_Wf, L1_conv_bf, L1_conv_gf, L1_conv_btf, L1_conv_mf, L1_conv_vf, L1_conv_Wg, L1_conv_bg, L1_conv_gg, L1_conv_btg, L1_conv_mg, L1_conv_vg, L1_conv_Wh, L1_conv_bh, L1_conv_Wv, L1_conv_bv)
    t = _to_tokens(x)
    t = t + _L2_attn_ref(_ln_t(t), L2_attn_w_attn, L2_attn_b_attn, L2_attn_w_proj, L2_attn_b_proj)
    t = t + _L2_ffn_ref(_ln_t(t), L2_ffn_norm_w, L2_ffn_wq, L2_ffn_keys, L2_ffn_expert_down, L2_ffn_expert_up)
    t = t + _L3_attn_ref(_ln_t(t), L3_attn_Wq, L3_attn_Wk, L3_attn_Wv, L3_attn_Wout, L3_attn_bout)
    t = t + _L3_ffn_ref(_ln_t(t), L3_ffn_router_w, L3_ffn_w1, L3_ffn_b1, L3_ffn_w2, L3_ffn_b2)
    x = _from_tokens(t, x)
    return x

_drawn_inputs = setup_inputs


def setup_inputs(seed=0):
    import zlib

    import numpy as np

    out = dict(_drawn_inputs(seed))
    spreads = {'L0_conv_b1': (0.0, 2.0),
     'L0_conv_g1': (1.0, 0.2),
     'L0_conv_be1': (0.0, 0.1),
     'L0_conv_b2': (0.0, 2.0),
     'L0_conv_g2': (1.0, 0.2),
     'L0_conv_be2': (0.0, 0.1),
     'L0_conv_b3': (0.0, 2.0),
     'L0_conv_g3': (1.0, 0.2),
     'L0_conv_be3': (0.0, 0.1),
     'L1_conv_bf': (0.0, 0.8),
     'L1_conv_gf': (1.0, 0.6),
     'L1_conv_btf': (0.0, 0.8),
     'L1_conv_bg': (0.0, 0.8),
     'L1_conv_gg': (1.0, 0.6),
     'L1_conv_btg': (0.0, 0.8),
     'L1_conv_bh': (0.0, 0.1),
     'L1_conv_bv': (0.0, 0.1),
     'L2_attn_b_attn': (0.0, 0.604),
     'L2_attn_b_proj': (0.0, 0.1),
     'L2_ffn_norm_w': (1.0, 0.6),
     'L3_attn_bout': (0.0, 0.603),
     'L3_ffn_b1': (0.0, 2.0),
     'L3_ffn_b2': (0.0, 1.786)}
    factors = {'L1_conv_mf': 5.959,
     'L1_conv_vf': 4.484,
     'L1_conv_mg': 5.536,
     'L1_conv_vg': 5.396,
     'L2_attn_w_attn': 3.289,
     'L2_attn_w_proj': 4.248,
     'L2_ffn_wq': 4.866,
     'L2_ffn_keys': 5.514,
     'L2_ffn_expert_down': 4.668,
     'L2_ffn_expert_up': 4.755,
     'L3_attn_Wq': 3.844,
     'L3_attn_Wk': 3.874}
    for name, (base, spread) in spreads.items():
        noise = np.random.default_rng([zlib.crc32(name.encode()), seed]).standard_normal(out[name].shape)
        drawn = base * np.exp(spread * noise) if base else spread * noise
        out[name] = jnp.asarray(drawn.astype(out[name].dtype))
    for name, factor in factors.items():
        out[name] = (out[name] * factor).astype(out[name].dtype)
    return out
```

```python
import concourse.bass as bass
from concourse import mybir
from contextlib import ExitStack

F32 = mybir.dt.float32
BF16 = mybir.dt.bfloat16
U32 = mybir.dt.uint32
ALU = mybir.AluOpType
ACT = mybir.ActivationFunctionType
LN_EXP = "natural_log_exp_and_others"
AX_X = mybir.AxisListType.X

LN_EPS = 1e-5

P = 128
B, C, HI, WI = 16, 256, 14, 14
HW = HI * WI
NT = B * HW
KC = C // P
TH = HW // 2


def wait(eng, semaphore, value):
    if isinstance(value, int) and value <= 0:
        return
    eng.wait_ge(semaphore, value)


def steps(eng, n, body):
    body(0)
    if n > 1:
        with eng.Fori(1, n) as i:
            body(i)


class Chain:

    def __init__(self, eng, semaphore):
        self.eng, self.sem = eng, semaphore
        self.base, self.k, self.start, self.per = 0, 0, 0, None

    def turn(self, i):
        if isinstance(i, int) and i == 0:
            self.start, self.k = self.k, 0
            self.base = self.start
        else:
            if self.per is None:
                self.per = self.k
            assert self.k == self.per
            self.base, self.k = self.start + i * self.per, 0

    def step(self, ins):
        ins.then_inc(self.sem, 1)
        self.k += 1

    def wait(self):
        self.eng.wait_ge(self.sem, self.base + self.k)


class Scope:

    def __init__(self, nc, name):
        self.nc, self.name, self.ctx, self.sems = nc, name, ExitStack(), []

    def __enter__(self):
        self.ctx.__enter__()
        return self

    def __exit__(self, *e):
        self.ctx.__exit__(*e)
        if self.sems and e[0] is None:
            self.nc.clear_and_free_semaphores(self.sems)
            self.nc.all_engine_barrier()

    def sb(self, name, shape, dt=F32):
        return self.ctx.enter_context(self.nc.sbuf_tensor(f"{self.name}_{name}", shape, dt))

    def ps(self, name, shape=(P, 512), dt=F32):
        return self.ctx.enter_context(self.nc.psum_tensor(f"{self.name}_{name}_ps", list(shape), dt))

    def sem(self, name):
        s = self.nc.alloc_semaphore(f"{self.name}_{name}")
        self.sems.append(s)
        return s

    def block(self):
        return self.ctx.enter_context(self.nc.Block())


def part(w, prefix):
    return {name[len(prefix):]: dram for name, dram in w.items() if name.startswith(prefix)}


def constants(nc, S):
    ident = S.sb("ident", [P, P])
    mean_w = S.sb("mean_w", [P, P])
    filled, done = S.sem("filled"), S.sem("ident_done")
    with nc.Block() as block:
        @block.gpsimd
        def _(pool):
            nc.gpsimd.memset(ident[:, :], 0.0).then_inc(filled, 1)
            nc.gpsimd.memset(mean_w[:, :], 1.0 / C).then_inc(done, 1)
            pool.wait_ge(filled, 1)
            nc.gpsimd.affine_select(out=ident[:, :], in_=ident[:, :], compare_op=ALU.not_equal, fill=1.0,
                                    base=0, pattern=[[-1, P]], channel_multiplier=1).then_inc(done, 1)
            pool.wait_ge(done, 2)
    return ident, mean_w


def layer_norm(nc, name, x, xn, mean_w, eps, norm_w=None):
    N = 392
    with Scope(nc, name) as S:
        eps_col = S.sb("eps", [P, 1])
        sq = [S.sb(f"sq{p}", [P, KC, N]) for p in range(2)]
        lnv = [S.sb(f"lnv{p}", [P, N]) for p in range(2)]
        rs = [S.sb(f"rs{p}", [P, N]) for p in range(2)]
        mean_ps = [S.ps(f"mean{p}") for p in range(2)]
        var_ps = [S.ps(f"var{p}") for p in range(2)]
        mean_ready, centred, squared = S.sem("mean_ready"), S.sem("centred"), S.sem("squared")
        var_ready, ln_ready, rs_ready, normed = S.sem("var_ready"), S.sem("ln_ready"), S.sem("rs_ready"), S.sem("normed")
        nw_loaded, consts = S.sem("nw_loaded"), S.sem("consts")
        rounds = 2 if norm_w is not None else 1
        if norm_w is not None:
            nw = S.sb("nw", [P, KC])
        n_steps = NT // N // 2
        block = S.block()

        def tok(t, n):
            return t[:, :, bass.ds(n * N, N)] if not isinstance(n, int) else t[:, :, n * N:(n + 1) * N]

        @block.sync
        def _(sp):
            if norm_w is not None:
                sp.dma_start(nw[:, :], norm_w.rearrange("(k p) -> p k", p=P),
                             allow_slow_non_contiguous=True).then_inc(nw_loaded, 16)

        @block.tensor
        def _(pe):
            def body(i):
                for p in range(2):
                    n = 2 * i + p
                    wait(pe, centred, n - 1)
                    for k in range(KC):
                        mm = nc.tensor.matmul(mean_ps[p][:, 0:N], mean_w[:, :], tok(x, n)[:, k, :],
                                              start=(k == 0), stop=(k == KC - 1))
                    mm.then_inc(mean_ready, 1)
                for r in range(rounds):
                    for p in range(2):
                        m = (2 * i + p) if rounds == 1 else (4 * i + 2 * r + p)
                        pe.wait_ge(squared, m + 1)
                        wait(pe, ln_ready, m - 1)
                        for k in range(KC):
                            mm = nc.tensor.matmul(var_ps[p][:, 0:N], mean_w[:, :], sq[p][:, k, :],
                                                  start=(k == 0), stop=(k == KC - 1))
                        mm.then_inc(var_ready, 1)
            steps(pe, n_steps, body)

        @block.scalar
        def _(act):
            act.preload_act_table_set(LN_EXP)

            def body(i):
                for r in range(rounds):
                    for p in range(2):
                        n = 2 * i + p
                        m = n if rounds == 1 else (4 * i + 2 * r + p)
                        act.wait_ge(consts, 1)
                        if r == 0:
                            act.wait_ge(centred, n + 1)
                        else:
                            act.wait_ge(normed, 4 * i + p + 1)
                        wait(act, var_ready, m - 1)
                        nc.scalar.activation(sq[p][:, :, :], tok(xn, n), ACT.Square).then_inc(squared, 1)
                    for p in range(2):
                        m = (2 * i + p) if rounds == 1 else (4 * i + 2 * r + p)
                        act.wait_ge(var_ready, m + 1)
                        nc.scalar.activation(lnv[p][:, :], var_ps[p][:, 0:N], ACT.Ln,
                                             bias=eps_col[:, 0:1]).then_inc(ln_ready, 1)
                    for p in range(2):
                        m = (2 * i + p) if rounds == 1 else (4 * i + 2 * r + p)
                        act.wait_ge(ln_ready, m + 1)
                        wait(act, normed, m - 1)
                        nc.scalar.activation(rs[p][:, :], lnv[p][:, :], ACT.Exp, scale=-0.5).then_inc(rs_ready, 1)
            steps(act, n_steps, body)

        @block.vector
        def _(dve):
            nc.vector.memset(eps_col[:, :], eps).then_inc(consts, 1)
            if norm_w is not None:
                dve.wait_ge(nw_loaded, 16)

            def body(i):
                for p in range(2):
                    n = 2 * i + p
                    dve.wait_ge(mean_ready, n + 1)
                    nc.vector.tensor_tensor(tok(xn, n), tok(x, n), mean_ps[p][:, 0:N].unsqueeze(1).broadcast_to([P, KC, N]),
                                            ALU.subtract).then_inc(centred, 1)
                for r in range(rounds):
                    for p in range(2):
                        n = 2 * i + p
                        m = n if rounds == 1 else (4 * i + 2 * r + p)
                        dve.wait_ge(rs_ready, m + 1)
                        dve.wait_ge(squared, m + 1)
                        for k in range(KC):
                            if r == 0:
                                ins = nc.vector.tensor_tensor(tok(xn, n)[:, k, :], tok(xn, n)[:, k, :], rs[p][:, :],
                                                              ALU.mult)
                            else:
                                ins = nc.vector.scalar_tensor_tensor(tok(xn, n)[:, k, :], tok(xn, n)[:, k, :],
                                                                     nw[:, k:k + 1], rs[p][:, :], ALU.mult, ALU.mult)
                        ins.then_inc(normed, 1)
            steps(dve, n_steps, body)


def l0_conv(nc, x_dram, w, x, ident):
    MID = 64
    IPC = 2
    NCH = B // IPC
    N = IPC * HW
    PW = WI + 2
    EPS = 1e-5
    N_COL = 16
    with Scope(nc, "l0") as S:
        w1n, w3n = S.sb("w1n", [MID, C]), S.sb("w3n", [P, KC, MID])
        w2n = S.sb("w2n", [MID, 9 * MID])
        w2r = S.sb("w2r", [MID, 9, MID])
        w1t = S.sb("w1t", [P, KC, P])
        w2t = S.sb("w2t", [P, 3, P])
        w2s = S.sb("w2s", [MID, 3, P])
        w3t = S.sb("w3t", [MID, C])
        bias1, gam1, bet1 = S.sb("b1", [P, 1]), S.sb("g1", [P, 1]), S.sb("be1", [P, 1])
        bias2, gam2, bet2 = S.sb("b2", [P, 1]), S.sb("g2", [P, 1]), S.sb("be2", [P, 1])
        bias3, gam3, bet3 = S.sb("b3", [P, KC]), S.sb("g3", [P, KC]), S.sb("be3", [P, KC])
        rsc = S.sb("rsc", [P, 5])
        eps_col = S.sb("eps", [P, 1])
        y1 = S.sb("y1", [P, NT])
        ypad = S.sb("ypad", [P, B, PW, PW])
        y2 = S.sb("y2", [MID, NT])
        y3 = S.sb("y3", [P, KC, NT])
        stats = S.sb("stats", [P, 4, NCH, 6])
        mv = S.sb("mv", [P, 4, 2])
        lnv, rstd = S.sb("lnv", [P, 4]), S.sb("rstd", [P, 4])
        scale, shift, mscale = S.sb("scale", [P, 4]), S.sb("shift", [P, 4]), S.sb("mscale", [P, 4])
        scale3, shift3 = S.sb("scale3", [P, KC]), S.sb("shift3", [P, KC])
        wps = [S.ps(f"w{p}") for p in range(2)]
        cps = [S.ps(f"c{p}") for p in range(4)]
        col_in = S.sem("col_in")
        w_in, x_in = S.sem("w_in"), [S.sem(f"x_in{c}") for c in range(NCH)]
        w_turned, w_ready, cleared = S.sem("w_turned"), S.sem("w_ready"), S.sem("cleared")
        conv1_done, conv2_done, conv3_done = S.sem("conv1_done"), S.sem("conv2_done"), S.sem("conv3_done")
        y1_ready, y2_ready, y3_ready = S.sem("y1_ready"), S.sem("y2_ready"), S.sem("y3_ready")
        var_ready, ln_ready, rstd_ready, aff_ready = S.sem("var_ready"), S.sem("ln_ready"), S.sem("rstd_ready"), S.sem("aff_ready")
        padded, act2_done, sum_done, res_done = S.sem("padded"), S.sem("act2_done"), S.sem("sum_done"), S.sem("res_done")
        soft_in, w2_ordered, dve_link = S.sem("soft_in"), S.sem("w2_ordered"), S.sem("dve_link")
        block = S.block()
        HALF = [slice(0, MID), slice(MID, P)]

        def chunk(t, c):
            return t[:, bass.ds(c * N, N)]

        @block.sync
        def _(sp):
            sp.dma_start(w1n[:, :], w["w1"].rearrange("o c h w -> o (c h w)")).then_inc(w_in, 16)
            sp.dma_start(w2n[:, :], w["w2"].rearrange("o i h w -> o (i h w)")).then_inc(w_in, 16)
            sp.dma_start(w3n[:, :, :], w["w3"].rearrange("(k o) c h w -> o k (c h w)", k=KC)).then_inc(w_in, 16)
            for c in range(NCH):
                for k in range(KC):
                    sp.dma_start(x[:, k, c * N:(c + 1) * N].rearrange("p (b t) -> p b t", b=IPC),
                                 x_dram[c * IPC:(c + 1) * IPC, k * P:(k + 1) * P].rearrange("b p t -> p b t")).then_inc(x_in[c], 16)

        @block.gpsimd
        def _(pool):
            def column(dst, src):
                pool.dma_start(dst, src.rearrange("(p a) -> p a", a=1)).then_inc(col_in, 16)
            for dst, v in ((bias1, "b1"), (gam1, "g1"), (bet1, "be1")):
                for h in HALF:
                    column(dst[h, 0:1], w[v])
            for dst, v in ((bias2, "b2"), (gam2, "g2"), (bet2, "be2")):
                column(dst[0:MID, 0:1], w[v])
            for dst, v in ((bias3, "b3"), (gam3, "g3"), (bet3, "be3")):
                for k in range(KC):
                    column(dst[:, k:k + 1], w[v][k * P:(k + 1) * P])
            pool.dma_start(rsc[:, 0:1], w["residual_scale"].partition_broadcast(P)).then_inc(col_in, 16)
            nc.gpsimd.memset(eps_col[:, :], EPS).then_inc(cleared, 1)
            nc.gpsimd.memset(ypad[:, :, :, :], 0.0).then_inc(cleared, 1)

        @block.tensor
        def _(pe):
            pe.wait_ge(w_in, 16 * 3)
            for k in range(KC):
                for h in range(2):
                    nc.tensor.transpose(wps[0][:, (2 * k + h) * MID:(2 * k + h + 1) * MID], w1n[:, k * P:(k + 1) * P],
                                        ident[0:MID, 0:MID])
            for k in range(KC):
                mm = nc.tensor.transpose(wps[0][0:MID, 256 + k * P:256 + (k + 1) * P], w3n[:, k, :], ident[:, :])
            mm.then_inc(w_turned, 1)
            pe.wait_ge(w2_ordered, 1)
            for ky in range(3):
                nc.tensor.transpose(wps[1][:, ky * MID:(ky + 1) * MID], w2r[:, 3 * ky:3 * ky + 2, :].rearrange("o t i -> o (t i)"), ident[0:MID, 0:MID])
            for ky in range(3):
                mm = nc.tensor.transpose(wps[1][0:MID, (3 + ky) * MID:(4 + ky) * MID], w2r[:, 3 * ky + 2, :], ident[0:MID, 0:MID])
            mm.then_inc(w_turned, 1)
            pe.wait_ge(w_ready, 1)
            for c in range(NCH):
                pe.wait_ge(x_in[c], 32)
                wait(pe, y1_ready, c - 3)
                for k in range(KC):
                    mm = nc.tensor.matmul(cps[c % 4][:, 0:N], w1t[:, k, :], x[:, k, c * N:(c + 1) * N],
                                          start=(k == 0), stop=(k == KC - 1))
                mm.then_inc(conv1_done, 1)
            pe.wait_ge(w_ready, 2)
            pe.wait_ge(y1_ready, NCH)

            def conv2(i):
                for p in range(2):
                    c = 2 * i + p
                    pe.wait_ge(padded, c + 1)
                    wait(pe, y2_ready, c - 1)
                    src = ypad[:, bass.ds(c * IPC, IPC), :, :]
                    out = cps[p][:, 0:N].rearrange("o (b h w) -> o b h w", b=IPC, h=HI)
                    for ky in range(3):
                        nc.tensor.matmul(out, w2t[:, ky, :], src[:, :, ky:ky + HI, 0:WI], start=(ky == 0), stop=False)
                        mm = nc.tensor.matmul(out, w2s[:, ky, :], src[0:MID, :, ky:ky + HI, 2:2 + WI], start=False, stop=(ky == 2))
                    mm.then_inc(conv2_done, 1)
            steps(pe, NCH // 2, conv2)
            pe.wait_ge(y2_ready, NCH)

            def conv3(i):
                for p in range(2):
                    c = 2 * i + p
                    pe.wait_ge(act2_done, c + 1)
                    wait(pe, y3_ready, 2 * c - 2)
                    for k in range(KC):
                        nc.tensor.matmul(cps[2 * p + k][:, 0:N], w3t[:, k * P:(k + 1) * P], chunk(y2, c),
                                         start=True, stop=True).then_inc(conv3_done, 1)
            steps(pe, NCH // 2, conv3)

        @block.scalar
        def _(act):
            act.preload_act_table_set(LN_EXP)
            act.wait_ge(col_in, 16 * N_COL)
            act.wait_ge(cleared, 2)
            nc.scalar.activation(rsc[:, 1:2], rsc[:, 0:1], ACT.Abs).then_inc(soft_in, 1)
            act.wait_ge(soft_in, 1)
            nc.scalar.activation(rsc[:, 2:3], rsc[:, 1:2], ACT.Exp, scale=-1.0).then_inc(soft_in, 1)
            act.wait_ge(soft_in, 2)
            nc.scalar.activation(rsc[:, 3:4], rsc[:, 2:3], ACT.Ln, bias=1.0).then_inc(soft_in, 1)
            for c in range(NCH):
                act.wait_ge(conv1_done, c + 1)
                nc.scalar.activation(y1[:, c * N:(c + 1) * N], cps[c % 4][:, 0:N], ACT.Identity, bias=bias1[:, 0:1]).then_inc(y1_ready, 1)

            def rstd_of(n, s, h):
                act.wait_ge(var_ready, n + 1)
                nc.scalar.activation(lnv[0:h, s], mv[0:h, s, 1], ACT.Ln, bias=eps_col[0:h, 0:1]).then_inc(ln_ready, 1)
                act.wait_ge(ln_ready, n + 1)
                nc.scalar.activation(rstd[0:h, s], lnv[0:h, s], ACT.Exp, scale=-0.5).then_inc(rstd_ready, 1)
                act.wait_ge(aff_ready, n + 1)

            rstd_of(0, slice(0, 1), P)

            def pad(c):
                for h, off in ((0, 1), (1, 0)):
                    dst = ypad[HALF[h], bass.ds(c * IPC, IPC), 1:1 + HI, off:off + WI]
                    ins = nc.scalar.activation(dst, chunk(y1, c)[HALF[h], :].rearrange("p (b h w) -> p b h w", b=IPC, h=HI),
                                               ACT.Relu, scale=scale[HALF[h], 0:1], bias=shift[HALF[h], 0:1])
                ins.then_inc(padded, 1)
            steps(act, NCH, pad)

            def out2(i):
                for p in range(2):
                    c = 2 * i + p
                    act.wait_ge(conv2_done, c + 1)
                    nc.scalar.activation(chunk(y2, c), cps[p][0:MID, 0:N], ACT.Identity, bias=bias2[0:MID, 0:1]).then_inc(y2_ready, 1)
            steps(act, NCH // 2, out2)
            rstd_of(1, slice(1, 2), MID)

            def relu2(c):
                nc.scalar.activation(chunk(y2, c), chunk(y2, c), ACT.Relu, scale=scale[0:MID, 1:2], bias=shift[0:MID, 1:2]).then_inc(act2_done, 1)
            steps(act, NCH, relu2)

            def out3(i):
                for p in range(2):
                    c = 2 * i + p
                    for k in range(KC):
                        act.wait_ge(conv3_done, 2 * c + k + 1)
                        nc.scalar.activation(chunk(y3[:, k, :], c), cps[2 * p + k][:, 0:N], ACT.Identity, bias=bias3[:, k:k + 1]).then_inc(y3_ready, 1)
            steps(act, NCH // 2, out3)
            rstd_of(2, slice(2, 4), P)

            def relu3(c):
                act.wait_ge(sum_done, c + 1)
                for k in range(KC):
                    nc.scalar.activation(chunk(x[:, k, :], c), chunk(y3[:, k, :], c), ACT.Relu, bias=shift3[:, k:k + 1]).then_inc(res_done, 1)
            steps(act, NCH, relu3)

        @block.vector
        def _(dve):
            links = [0]

            def link(ins):
                links[0] += 1
                ins.then_inc(dve_link, 1)
                dve.wait_ge(dve_link, links[0])

            dve.wait_ge(w_in, 16 * 3)
            dve.wait_ge(col_in, 16 * N_COL)
            nc.vector.tensor_copy(w2r[:, :, :], w2n[:, :].rearrange("o (i t) -> o t i", t=9)).then_inc(w2_ordered, 1)
            dve.wait_ge(w_turned, 1)
            nc.vector.tensor_copy(w1t[:, :, :], wps[0][:, 0:256].rearrange("p (k m) -> p k m", k=KC))
            nc.vector.tensor_copy(w3t[:, :], wps[0][0:MID, 256:512]).then_inc(w_ready, 1)
            dve.wait_ge(w_turned, 2)
            for h in HALF:
                nc.vector.tensor_copy(w2t[:, :, h], wps[1][:, 0:3 * MID].rearrange("p (y m) -> p y m", y=3))
                ins = nc.vector.tensor_copy(w2s[:, :, h], wps[1][0:MID, 3 * MID:6 * MID].rearrange("p (y m) -> p y m", y=3))
            ins.then_inc(w_ready, 1)

            def affine(n, s, h, g, b):
                dve.wait_ge(rstd_ready, n + 1)
                link(nc.vector.tensor_tensor(scale[0:h, s], g[0:h, :], rstd[0:h, s], ALU.mult))
                link(nc.vector.tensor_tensor(mscale[0:h, s], mv[0:h, s, 0], scale[0:h, s], ALU.mult))
                return nc.vector.tensor_tensor(shift[0:h, s], b[0:h, :], mscale[0:h, s], ALU.subtract)

            for c in range(NCH):
                dve.wait_ge(y1_ready, c + 1)
                ins = nc.vector.bn_stats(stats[:, 0, c, :], y1[:, c * N:(c + 1) * N])
            link(ins)
            nc.vector.bn_aggr(mv[:, 0, :], stats[:, 0, :, :]).then_inc(var_ready, 1)
            affine(0, slice(0, 1), P, gam1, bet1).then_inc(aff_ready, 1)
            for c in range(NCH):
                dve.wait_ge(y2_ready, c + 1)
                ins = nc.vector.bn_stats(stats[0:MID, 1, c, :], y2[:, c * N:(c + 1) * N])
            link(ins)
            nc.vector.bn_aggr(mv[0:MID, 1, :], stats[0:MID, 1, :, :]).then_inc(var_ready, 1)
            affine(1, slice(1, 2), MID, gam2, bet2).then_inc(aff_ready, 1)
            for c in range(NCH):
                for k in range(KC):
                    dve.wait_ge(y3_ready, 2 * c + k + 1)
                    ins = nc.vector.bn_stats(stats[:, 2 + k, c, :], y3[:, k, c * N:(c + 1) * N])
            link(ins)
            for k in range(KC):
                ins = nc.vector.bn_aggr(mv[:, 2 + k, :], stats[:, 2 + k, :, :])
            ins.then_inc(var_ready, 1)
            link(affine(2, slice(2, 4), P, gam3, bet3))
            dve.wait_ge(soft_in, 3)
            link(nc.vector.scalar_tensor_tensor(rsc[:, 4:5], rsc[:, 0:1], 0.0, rsc[:, 3:4], ALU.max, ALU.add))
            nc.vector.tensor_scalar(scale3[:, :], scale[:, 2:4], rsc[:, 4:5], None, ALU.mult)
            nc.vector.tensor_scalar(shift3[:, :], shift[:, 2:4], rsc[:, 4:5], None, ALU.mult).then_inc(aff_ready, 1)
            dve.wait_ge(aff_ready, 3)

            def residual(c):
                for k in range(KC):
                    ins = nc.vector.scalar_tensor_tensor(chunk(y3[:, k, :], c), chunk(y3[:, k, :], c), scale3[:, k:k + 1],
                                                         chunk(x[:, k, :], c), ALU.mult, ALU.add)
                ins.then_inc(sum_done, 1)
            steps(dve, NCH, residual)


def l1_attention(nc, x, w, ident):
    MID = 64
    EPS = 1e-5
    SCALE = MID ** -0.5
    with Scope(nc, "l1") as S:
        wn = S.sb("wn", [MID, 3, C])
        wvn = S.sb("wvn", [P, KC, MID])
        wt = S.sb("wt", [P, KC, 3, MID])
        wvt = S.sb("wvt", [MID, C])
        col = S.sb("col", [MID, 2, 5])
        bh = S.sb("bh", [MID, 1])
        bv = S.sb("bv", [P, KC])
        eps_col = S.sb("eps", [MID, 1])
        lnv, rstd = S.sb("lnv", [MID, 2]), S.sb("rstd", [MID, 2])
        scale, shift, tmp = S.sb("scale", [MID, 2]), S.sb("shift", [MID, 2]), S.sb("tmp", [MID, 2])
        xi = [S.sb(f"xi{p}", [P, KC, HW]) for p in range(2)]
        fg = [S.sb(f"fg{p}", [MID, 2, HW]) for p in range(2)]
        ht = [S.sb(f"ht{p}", [TH, 2, MID]) for p in range(2)]
        nm = [S.sb(f"nm{p}", [TH, 2]) for p in range(2)]
        ex = [S.sb(f"ex{p}", [TH, 2, HW]) for p in range(2)]
        total = [S.sb(f"total{p}", [TH, 2]) for p in range(2)]
        inv = [S.sb(f"inv{p}", [TH, 2]) for p in range(2)]
        pn = [S.sb(f"pn{p}", [TH, 2, HW]) for p in range(2)]
        pt = [S.sb(f"pt{p}", [TH, 2, HW]) for p in range(2)]
        z = [S.sb(f"z{p}", [MID, HW]) for p in range(2)]
        a_ps = [S.ps(f"a{p}") for p in range(2)]
        s_ps = [S.ps(f"s{p}") for p in range(2)]
        h_ps, pt_ps = S.ps("h"), [S.ps(f"pt{p}") for p in range(2)]
        z_ps = S.ps("z")
        w_in, consts, w_turned, w_ready = S.sem("w_in"), S.sem("consts"), S.sem("w_turned"), S.sem("w_ready")
        ln_ready, rstd_ready, aff_ready, link_s = S.sem("ln_ready"), S.sem("rstd_ready"), S.sem("aff_ready"), S.sem("link")
        xi_in = [S.sem(f"xi_in{p}") for p in range(2)]
        fg_done, h_done, fg_ready, h_ready = S.sem("fg_done"), S.sem("h_done"), S.sem("fg_ready"), S.sem("h_ready")
        s_done, max_done, exp_done, inv_done, pn_ready = S.sem("s_done"), S.sem("max_done"), S.sem("exp_done"), S.sem("inv_done"), S.sem("pn_ready")
        t_done, pt_ready, z_done, z_ready, o_done, x_done = S.sem("t_done"), S.sem("pt_ready"), S.sem("z_done"), S.sem("z_ready"), S.sem("o_done"), S.sem("x_done")
        N_W = 4 + 10 + 2
        block = S.block()

        def image(t, n):
            return t[:, :, bass.ds(n * HW, HW)]

        def pairs(eng, body):
            def both(i):
                for p in range(2):
                    body(2 * i + p, p)
            steps(eng, B // 2, both)

        @block.sync
        def _(sp):
            for j, v in enumerate(("Wf", "Wg", "Wh")):
                sp.dma_start(wn[:, j, :], w[v]).then_inc(w_in, 16)
            sp.dma_start(wvn[:, :, :], w["Wv"].rearrange("(k p) c -> p k c", p=P)).then_inc(w_in, 16)
            for j, s in enumerate("fg"):
                for n, v in enumerate(("b", "g", "bt", "m", "v")):
                    sp.dma_start(col[:, j, n:n + 1], w[v + s].rearrange("(p a) -> p a", a=1)).then_inc(w_in, 16)
            sp.dma_start(bh[:, :], w["bh"].rearrange("(p a) -> p a", a=1)).then_inc(w_in, 16)
            sp.dma_start(bv[:, :], w["bv"].rearrange("(k p) -> p k", p=P), allow_slow_non_contiguous=True).then_inc(w_in, 16)

            def body(n, p):
                wait(sp, x_done, n - 1)
                sp.dma_start(xi[p][:, :, :], image(x, n)).then_inc(xi_in[p], 16)
            pairs(sp, body)

        @block.gpsimd
        def _(pool):
            nc.gpsimd.memset(eps_col[:, :], EPS).then_inc(consts, 1)

        @block.tensor
        def _(pe):
            pe.wait_ge(w_in, 16 * N_W)
            for j in range(3):
                for k in range(KC):
                    mm = nc.tensor.transpose(a_ps[0][:, (3 * k + j) * MID:(3 * k + j + 1) * MID], wn[:, j, k * P:(k + 1) * P], ident[0:MID, 0:MID])
            for k in range(KC):
                mm = nc.tensor.transpose(a_ps[1][0:MID, k * P:(k + 1) * P], wvn[:, k, :], ident[:, :])
            mm.then_inc(w_turned, 1)
            pe.wait_ge(w_ready, 1)

            def project_in(n, p):
                pe.wait_ge(xi_in[p], 8 * (n - p) + 16)
                wait(pe, fg_ready, n - 1)
                for j in range(2):
                    for k in range(KC):
                        mm = nc.tensor.matmul(a_ps[p][0:MID, j * HW:(j + 1) * HW], wt[:, k, j, :], xi[p][:, k, :],
                                              start=(k == 0), stop=(k == KC - 1))
                mm.then_inc(fg_done, 1)
                wait(pe, h_ready, n)
                for t in range(2):
                    for k in range(KC):
                        mm = nc.tensor.matmul(h_ps[0:TH, t * MID:(t + 1) * MID], xi[p][:, k, t * TH:(t + 1) * TH], wt[:, k, 2, :],
                                              start=(k == 0), stop=(k == KC - 1))
                mm.then_inc(h_done, 1)

            def scores(n, p):
                pe.wait_ge(fg_ready, n + 1)
                wait(pe, x_done, n - 1)
                for t in range(2):
                    mm = nc.tensor.matmul(s_ps[p][0:TH, t * HW:(t + 1) * HW], fg[p][:, 0, t * TH:(t + 1) * TH], fg[p][:, 1, :],
                                          start=True, stop=True)
                mm.then_inc(s_done, 1)

            def turn(n, p):
                pe.wait_ge(pn_ready, n + 1)
                wait(pe, pt_ready, n - 1)
                for t in range(2):
                    for u in range(2):
                        mm = nc.tensor.transpose(pt_ps[p][0:TH, u * HW + t * TH:u * HW + (t + 1) * TH], pn[p][:, t, u * TH:(u + 1) * TH],
                                                 ident[0:TH, 0:TH])
                mm.then_inc(t_done, 1)

            def mix(n, p):
                pe.wait_ge(pt_ready, n + 1)
                pe.wait_ge(h_ready, n + 1)
                wait(pe, z_ready, n)
                for u in range(2):
                    mm = nc.tensor.matmul(z_ps[0:MID, 0:HW], ht[p][:, u, :], pt[p][:, u, :], start=(u == 0), stop=(u == 1))
                mm.then_inc(z_done, 1)

            def project_out(n, p):
                pe.wait_ge(z_ready, n + 1)
                for k in range(KC):
                    mm = nc.tensor.matmul(s_ps[p][:, k * HW:(k + 1) * HW], wvt[:, k * P:(k + 1) * P], z[p][:, :], start=True, stop=True)
                mm.then_inc(o_done, 1)

            def both(i):
                for stage in (project_in, scores, turn, mix, project_out):
                    for p in range(2):
                        stage(2 * i + p, p)
            steps(pe, B // 2, both)

        @block.scalar
        def _(act):
            act.preload_act_table_set(LN_EXP)
            act.wait_ge(w_in, 16 * N_W)
            act.wait_ge(consts, 1)
            nc.scalar.activation(lnv[:, :], col[:, :, 4], ACT.Ln, bias=eps_col[:, 0:1]).then_inc(ln_ready, 1)
            act.wait_ge(ln_ready, 1)
            nc.scalar.activation(rstd[:, :], lnv[:, :], ACT.Exp, scale=-0.5).then_inc(rstd_ready, 1)
            act.wait_ge(aff_ready, 1)

            def both(i):
                for p in range(2):
                    n = 2 * i + p
                    act.wait_ge(fg_done, n + 1)
                    wait(act, s_done, n - 1)
                    for j in range(2):
                        ins = nc.scalar.activation(fg[p][:, j, :], a_ps[p][0:MID, j * HW:(j + 1) * HW], ACT.Relu,
                                                   scale=scale[:, j:j + 1], bias=shift[:, j:j + 1])
                    ins.then_inc(fg_ready, 1)
                    act.wait_ge(h_done, n + 1)
                    wait(act, z_done, n - 1)
                    nc.scalar.activation(ht[p][:, :, :], h_ps[0:TH, 0:2 * MID].rearrange("p (t m) -> p t m", t=2), ACT.Copy).then_inc(h_ready, 1)
                for p in range(2):
                    n = 2 * i + p
                    act.wait_ge(max_done, n + 1)
                    wait(act, pn_ready, n - 1)
                    for t in range(2):
                        ins = nc.scalar.activation(ex[p][:, t, :], s_ps[p][0:TH, t * HW:(t + 1) * HW], ACT.Exp, scale=SCALE,
                                                   bias=nm[p][:, t:t + 1], accum_out=total[p][:, t:t + 1])
                    ins.then_inc(exp_done, 1)
                for p in range(2):
                    n = 2 * i + p
                    act.wait_ge(t_done, n + 1)
                    wait(act, z_done, n - 1)
                    nc.scalar.activation(pt[p][:, :, :], pt_ps[p][0:TH, 0:2 * HW].rearrange("p (u t) -> p u t", u=2), ACT.Copy).then_inc(pt_ready, 1)
                for p in range(2):
                    n = 2 * i + p
                    act.wait_ge(z_done, n + 1)
                    wait(act, o_done, n - 1)
                    nc.scalar.activation(z[p][:, :], z_ps[0:MID, 0:HW], ACT.Identity, bias=bh[:, 0:1]).then_inc(z_ready, 1)
            steps(act, B // 2, both)

        @block.vector
        def _(dve):
            dve.wait_ge(w_turned, 1)
            nc.vector.tensor_copy(wt[:, :, :, :], a_ps[0][:, 0:KC * 3 * MID].rearrange("p (k j m) -> p k j m", k=KC, j=3))
            nc.vector.tensor_copy(wvt[:, :], a_ps[1][0:MID, 0:C]).then_inc(w_ready, 1)
            dve.wait_ge(w_in, 16 * N_W)
            dve.wait_ge(rstd_ready, 1)
            nc.vector.tensor_tensor(scale[:, :], col[:, :, 1], rstd[:, :], ALU.mult).then_inc(link_s, 1)
            nc.vector.tensor_tensor(tmp[:, :], col[:, :, 0], col[:, :, 3], ALU.subtract).then_inc(link_s, 1)
            dve.wait_ge(link_s, 2)
            nc.vector.tensor_tensor(tmp[:, :], tmp[:, :], scale[:, :], ALU.mult).then_inc(link_s, 1)
            dve.wait_ge(link_s, 3)
            nc.vector.tensor_tensor(shift[:, :], tmp[:, :], col[:, :, 2], ALU.add).then_inc(aff_ready, 1)

            def both(i):
                for p in range(2):
                    n = 2 * i + p
                    dve.wait_ge(s_done, n + 1)
                    nc.vector.tensor_reduce(inv[p][:, :], s_ps[p][0:TH, 0:2 * HW].rearrange("p (t j) -> p t j", t=2), AX_X, ALU.max).then_inc(link_s, 1)
                    dve.wait_ge(link_s, n + 4)
                    nc.vector.tensor_scalar(nm[p][:, :], inv[p][:, :], -SCALE, None, ALU.mult).then_inc(max_done, 1)
                for p in range(2):
                    n = 2 * i + p
                    dve.wait_ge(exp_done, n + 1)
                    nc.vector.reciprocal(inv[p][:, :], total[p][:, :]).then_inc(inv_done, 1)
                    dve.wait_ge(inv_done, n + 1)
                    wait(dve, t_done, n - 1)
                    for t in range(2):
                        ins = nc.vector.tensor_scalar(pn[p][:, t, :], ex[p][:, t, :], inv[p][:, t:t + 1], None, ALU.mult)
                    ins.then_inc(pn_ready, 1)
                for p in range(2):
                    n = 2 * i + p
                    dve.wait_ge(o_done, n + 1)
                    for k in range(KC):
                        ins = nc.vector.scalar_tensor_tensor(image(x, n)[:, k, :], s_ps[p][:, k * HW:(k + 1) * HW], bv[:, k:k + 1],
                                                             xi[p][:, k, :], ALU.add, ALU.add)
                    ins.then_inc(x_done, 1)
            steps(dve, B // 2, both)


def attention(nc, name, x, xn, ident, heads, causal, q_scale, out_scale, load_w, w_out, b_qkv, b_out):
    D = 16
    INNER = heads * D
    MT = INNER // P
    GH = P // D
    SW = 3 * TH if causal else 4 * TH
    blocks = [(0, 0, 0), (1, 0, 1), (1, 1, 2)] if causal else [(0, 0, 0), (0, 1, 1), (1, 0, 2), (1, 1, 3)]
    rows = [(0, 0, 1), (1, 1, 2)] if causal else [(0, 0, 2), (1, 2, 2)]
    with Scope(nc, name) as S:
        w_qkv = S.sb("w_qkv", [P, KC, 3 * INNER])
        w_o = S.sb("w_o", [P, MT, C])
        bq, bk = S.sb("bq", [P, MT]), S.sb("bk", [P, MT])
        bv = S.sb("bv", [1, INNER])
        bo = S.sb("bo", [P, KC])
        ones = S.sb("ones", [1, TH])
        side = S.sb("side", [P, 2])
        ident_b, mask_b = S.sb("ident_b", [TH, TH], BF16), S.sb("mask_b", [TH, 2, TH], BF16)
        xi = S.sb("xi", [P, KC, HW])
        qm = S.sb("qm", [P, 2, MT, HW])
        kt = S.sb("kt", [P, MT, HW])
        va = S.sb("va", [TH, 2, heads, D + 1])
        ex = [S.sb(f"ex{p}", [TH, SW]) for p in range(2)]
        pt = [S.sb(f"pt{p}", [TH, SW]) for p in range(2)]
        mn = S.sb("mn", [TH, heads, 2])
        rinv = S.sb("rinv", [TH, 2, heads])
        on = S.sb("on", [TH, 2, INNER])
        ot = S.sb("ot", [P, MT, HW])
        q_ps, k_ps, v_ps, pt_ps = S.ps("q"), S.ps("k"), S.ps("v"), S.ps("pt")
        s_ps = [S.ps(f"s{p}") for p in range(2)]
        o_ps = [S.ps(f"o{p}") for p in range(2)]
        w_in, c_in, consts, masked = S.sem("w_in"), S.sem("c_in"), S.sem("consts"), S.sem("masked")
        xi_in, q_done, k_done, v_done = S.sem("xi_in"), S.sem("q_done"), S.sem("k_done"), S.sem("v_done")
        q_ready, k_ready, v_ready = S.sem("q_ready"), S.sem("k_ready"), S.sem("v_ready")
        s_done, min_done, exp_done, t_done = S.sem("s_done"), S.sem("min_done"), S.sem("exp_done"), S.sem("t_done")
        pt_ready, pv_done, inv_done, on_ready = S.sem("pt_ready"), S.sem("pv_done"), S.sem("inv_done"), S.sem("on_ready")
        ot_done, ot_ready, proj_done, x_done = S.sem("ot_done"), S.sem("ot_ready"), S.sem("proj_done"), S.sem("x_done")
        n_w = load_w(None, None, None)
        n_c = (3 if b_qkv is not None else 0) + 1
        block = S.block()

        def image(t, n):
            return t[:, :, bass.ds(n * HW, HW)]

        def loop(eng, body):
            body(0, False)
            with eng.Fori(1, B - 1) as n:
                body(n, False)
            body(B - 1, True)

        @block.sync
        def _(sp):
            load_w(sp, w_qkv, w_in)
            sp.dma_start(w_o[:, :, :], w_out.rearrange("(m p) c -> p m c", p=P)).then_inc(w_in, 16)
            if b_qkv is not None:
                for j, dst in ((0, bq), (1, bk)):
                    sp.dma_start(dst[:, :], b_qkv[j * INNER:(j + 1) * INNER].rearrange("(m p) -> p m", p=P),
                                 allow_slow_non_contiguous=True).then_inc(c_in, 16)
                sp.dma_start(bv[:, :], b_qkv[2 * INNER:3 * INNER].rearrange("(a n) -> a n", a=1)).then_inc(c_in, 16)
            sp.dma_start(bo[:, :], b_out.rearrange("(k p) -> p k", p=P), allow_slow_non_contiguous=True).then_inc(c_in, 16)

            def body(n):
                wait(sp, v_done, n)
                sp.dma_start(xi[:, :, :], image(xn, n)).then_inc(xi_in, 16)
            steps(sp, B, body)

        @block.gpsimd
        def _(pool):
            nc.gpsimd.memset(ones[:, :], 1.0).then_inc(consts, 1)
            nc.gpsimd.memset(va[:, :, :, :], 1.0).then_inc(consts, 1)
            nc.gpsimd.tensor_copy(ident_b[:, :], ident[0:TH, 0:TH]).then_inc(consts, 1)
            nc.gpsimd.memset(mask_b[:, :, :], 0.0).then_inc(masked, 1)
            pool.wait_ge(masked, 1)
            nc.gpsimd.affine_select(out=mask_b[:, :, :], in_=mask_b[:, :, :], compare_op=ALU.is_ge, fill=1e30,
                                    base=0, pattern=[[0, 2], [-1, TH]], channel_multiplier=1).then_inc(consts, 1)

        @block.tensor
        def _(pe):
            def qkv(n):
                pe.wait_ge(xi_in, 16 * n + 16)
                wait(pe, q_ready, n)
                for m in range(MT):
                    for k in range(KC):
                        mm = nc.tensor.matmul(q_ps[:, m * HW:(m + 1) * HW], w_qkv[:, k, m * P:(m + 1) * P], xi[:, k, :],
                                              start=(k == 0), stop=(k == KC - 1))
                mm.then_inc(q_done, 1)
                wait(pe, k_ready, n)
                for m in range(MT):
                    for k in range(KC):
                        mm = nc.tensor.matmul(k_ps[:, m * HW:(m + 1) * HW], w_qkv[:, k, INNER + m * P:INNER + (m + 1) * P],
                                              xi[:, k, :], start=(k == 0), stop=(k == KC - 1))
                mm.then_inc(k_done, 1)
                wait(pe, v_ready, n)
                for t in range(2):
                    for k in range(KC):
                        mm = nc.tensor.matmul(v_ps[0:TH, t * INNER:(t + 1) * INNER], xi[:, k, t * TH:(t + 1) * TH],
                                              w_qkv[:, k, 2 * INNER:3 * INNER], start=(k == 0),
                                              stop=(k == KC - 1 and b_qkv is None))
                    if b_qkv is not None:
                        mm = nc.tensor.matmul(v_ps[0:TH, t * INNER:(t + 1) * INNER], ones[0:1, :], bv[0:1, :], start=False, stop=True)
                mm.then_inc(v_done, 1)

            def scores(n, h):
                m, row, side_h = h // GH, 32 * (h % GH // 2), h % 2
                wait(pe, exp_done, n * heads + h - 1)
                if h == 0:
                    pe.wait_ge(q_ready, n + 1)
                    pe.wait_ge(k_ready, n + 1)
                    wait(pe, ot_ready, n)
                if h == 1:
                    wait(pe, x_done, n)
                last = blocks[-1]
                for j, (t, b, nb) in enumerate(rows):
                    mm = nc.tensor.matmul(s_ps[h % 2][0:TH, b * TH:(b + nb) * TH],
                                          qm[row:row + 32, side_h, m, t * TH:(t + 1) * TH],
                                          kt[row:row + 32, m, 0:nb * TH], start=(j == 0), stop=(not causal and j == 1),
                                          skip_group_check=True)
                if causal:
                    out = s_ps[h % 2][0:TH, 0:2 * 2 * TH].rearrange("p (a c) -> p a c", a=2)[:, :, 0:TH]
                    mm = nc.tensor.matmul(out, ident_b[:, :], mask_b[:, :, :], start=False, stop=True, skip_group_check=True)
                mm.then_inc(s_done, 1)

            def turn(n, h):
                pe.wait_ge(exp_done, n * heads + h + 1)
                wait(pe, pt_ready, n * heads + h)
                for t, u, b in blocks:
                    mm = nc.tensor.transpose(pt_ps[0:TH, b * TH:(b + 1) * TH], ex[h % 2][:, b * TH:(b + 1) * TH], ident[0:TH, 0:TH])
                mm.then_inc(t_done, 1)

            def values(n, h):
                pe.wait_ge(pt_ready, n * heads + h + 1)
                if h == 0:
                    pe.wait_ge(v_ready, n + 1)
                    wait(pe, on_ready, n)
                for t, u, b in blocks:
                    last = u == (t if causal else 1)
                    mm = nc.tensor.matmul(o_ps[t][0:TH, h * (D + 1):(h + 1) * (D + 1)], pt[h % 2][:, b * TH:(b + 1) * TH],
                                          va[:, u, h, :], start=(u == 0), stop=last)
                mm.then_inc(pv_done, 1)

            def project(n):
                pe.wait_ge(on_ready, n + 1)
                pe.wait_ge(exp_done, (n + 1) * heads)
                for m in range(MT):
                    for t in range(2):
                        mm = nc.tensor.transpose(s_ps[0][:, m * HW + t * TH:m * HW + (t + 1) * TH], on[:, t, m * P:(m + 1) * P],
                                                 ident[0:TH, 0:TH])
                mm.then_inc(ot_done, 1)
                pe.wait_ge(ot_ready, n + 1)
                for k in range(KC):
                    for m in range(MT):
                        mm = nc.tensor.matmul(s_ps[1][:, k * HW:(k + 1) * HW], w_o[:, m, k * P:(k + 1) * P], ot[:, m, :],
                                              start=(m == 0), stop=(m == MT - 1))
                mm.then_inc(proj_done, 1)

            pe.wait_ge(w_in, 16 * (n_w + 1))
            pe.wait_ge(c_in, 16 * n_c)
            pe.wait_ge(consts, 4)
            qkv(0)

            def body(n, last):
                for s in range(heads + 2):
                    if s < heads:
                        scores(n, s)
                    if 1 <= s <= heads:
                        turn(n, s - 1)
                    if s >= 2:
                        values(n, s - 2)
                if not last:
                    qkv(n + 1)
                project(n)
            loop(pe, body)

        @block.scalar
        def _(act):
            act.preload_act_table_set(LN_EXP)

            def keys_values(n):
                act.wait_ge(k_done, n + 1)
                for m in range(MT):
                    if b_qkv is not None:
                        ins = nc.scalar.activation(kt[:, m, :], k_ps[:, m * HW:(m + 1) * HW], ACT.Identity, bias=bk[:, m:m + 1])
                    else:
                        ins = nc.scalar.activation(kt[:, m, :], k_ps[:, m * HW:(m + 1) * HW], ACT.Copy)
                ins.then_inc(k_ready, 1)
                act.wait_ge(v_done, n + 1)
                for t in range(2):
                    ins = nc.scalar.activation(va[:, t, :, 0:D], v_ps[0:TH, t * INNER:(t + 1) * INNER].rearrange("p (h d) -> p h d", d=D),
                                               ACT.Copy)
                ins.then_inc(v_ready, 1)

            def exps(n, h):
                act.wait_ge(min_done, n * heads + h + 1)
                wait(act, t_done, n * heads + h - 1)
                for t, b, nb in rows:
                    ins = nc.scalar.activation(ex[h % 2][:, b * TH:(b + nb) * TH], s_ps[h % 2][0:TH, b * TH:(b + nb) * TH],
                                               ACT.Exp, scale=-1.0, bias=mn[:, h, t:t + 1])
                ins.then_inc(exp_done, 1)

            act.wait_ge(c_in, 16 * n_c)
            act.wait_ge(consts, 4)
            keys_values(0)

            def body(n, last):
                for h in range(heads):
                    exps(n, h)
                if not last:
                    keys_values(n + 1)
                act.wait_ge(ot_done, n + 1)
                nc.scalar.activation(ot[:, :, :], s_ps[0][:, 0:MT * HW].rearrange("p (m t) -> p m t", m=MT), ACT.Copy).then_inc(ot_ready, 1)
            loop(act, body)

        @block.vector
        def _(dve):
            def queries(n):
                dve.wait_ge(q_done, n + 1)
                for e in range(2):
                    for m in range(MT):
                        if b_qkv is not None:
                            ins = nc.vector.tensor_scalar(qm[:, e, m, :], q_ps[:, m * HW:(m + 1) * HW], bq[:, m:m + 1],
                                                          side[:, e:e + 1], ALU.add, ALU.mult)
                        else:
                            ins = nc.vector.tensor_scalar(qm[:, e, m, :], q_ps[:, m * HW:(m + 1) * HW], side[:, e:e + 1],
                                                          None, ALU.mult)
                ins.then_inc(q_ready, 1)

            def row_min(n, h):
                dve.wait_ge(s_done, n * heads + h + 1)
                if causal:
                    for t, b, nb in rows:
                        ins = nc.vector.tensor_reduce(mn[:, h, t:t + 1], s_ps[h % 2][0:TH, b * TH:(b + nb) * TH], AX_X, ALU.min)
                else:
                    ins = nc.vector.tensor_reduce(mn[:, h, :], s_ps[h % 2][0:TH, 0:SW].rearrange("p (t j) -> p t j", t=2), AX_X, ALU.min)
                ins.then_inc(min_done, 1)

            def turned_out(n, h):
                dve.wait_ge(t_done, n * heads + h + 1)
                wait(dve, pv_done, n * heads + h - 1)
                nc.vector.tensor_copy(pt[h % 2][:, :], pt_ps[0:TH, 0:SW]).then_inc(pt_ready, 1)

            for e in range(2):
                src = ident[:, :].rearrange("p (g e d) -> p e g d", e=2, d=D)[:, e, :, :]
                nc.vector.tensor_reduce(side[:, e:e + 1], src, mybir.AxisListType.XY, ALU.add).then_inc(inv_done, 1)
            dve.wait_ge(inv_done, 2)
            nc.vector.tensor_scalar(side[:, :], side[:, :], -q_scale, None, ALU.mult).then_inc(inv_done, 1)
            dve.wait_ge(inv_done, 3)
            dve.wait_ge(c_in, 16 * n_c)
            queries(0)

            def body(n, last):
                for s in range(heads + 1):
                    if s < heads:
                        row_min(n, s)
                    if s >= 1:
                        turned_out(n, s - 1)
                dve.wait_ge(pv_done, (n + 1) * heads)
                for t in range(2):
                    ov = o_ps[t][0:TH, 0:heads * (D + 1)].rearrange("p (h d) -> p h d", d=D + 1)
                    ins = nc.vector.reciprocal(rinv[:, t, :], ov[:, :, D])
                ins.then_inc(inv_done, 1)
                dve.wait_ge(inv_done, n + 4)
                for t in range(2):
                    ov = o_ps[t][0:TH, 0:heads * (D + 1)].rearrange("p (h d) -> p h d", d=D + 1)
                    ins = nc.vector.scalar_tensor_tensor(on[:, t, :].rearrange("p (h d) -> p h d", d=D), ov[:, :, 0:D], out_scale,
                                                         rinv[:, t, :].unsqueeze(2).broadcast_to([TH, heads, D]), ALU.mult, ALU.mult)
                ins.then_inc(on_ready, 1)
                if not last:
                    queries(n + 1)
                dve.wait_ge(proj_done, n + 1)
                for k in range(KC):
                    ins = nc.vector.scalar_tensor_tensor(image(x, n)[:, k, :], s_ps[1][:, k * HW:(k + 1) * HW], bo[:, k:k + 1],
                                                         image(x, n)[:, k, :], ALU.add, ALU.add)
                ins.then_inc(x_done, 1)
            loop(dve, body)


def l2_weights(w_attn):
    def load(sp, w_qkv, w_in):
        if sp is None:
            return 1
        sp.dma_start(w_qkv[:, :, :], w_attn.rearrange("(k p) n -> p k n", p=P)).then_inc(w_in, 16)
    return load


def l3_weights(wq, wk, wv):
    def load(sp, w_qkv, w_in):
        if sp is None:
            return 3
        n = wq.shape[1]
        for j, w in enumerate((wq, wk, wv)):
            sp.dma_start(w_qkv[:, :, j * n:(j + 1) * n], w.rearrange("(k p) n -> p k n", p=P)).then_inc(w_in, 16)
    return load


def peer_ffn(nc, x, xn_dram, w, ident):
    NH, NK, DK, TOP = 8, 64, 32, 16
    G16 = 2 * NH
    NP = NH * TOP
    TT = 112
    NTILE = 2
    CT = NTILE * TT
    NCHUNK = NT // CT
    J = 32
    HT = TT // 2
    NHB = 2 * NTILE
    GT = HT // 4
    LOWEST = -3.4028235e38
    CAND = [(0, 1, 16), (1, 3, 8), (4, 4, 4), (8, 8, 1)]
    row_start = [off for a0, na, nb, o in ((0, 1, 16, 0), (1, 3, 8, 16), (4, 4, 4, 40), (8, 8, 1, 56)) for off in range(o, o + na * nb, nb)]
    with Scope(nc, "peer") as S:
        up = S.sb("up", [P, J, C])
        dt = S.sb("dt", [P, KC, J, P])
        g = S.sb("g", [P, J, CT])
        oh_a = [S.sb(f"oh_a{p}", [P, P, HT], BF16) for p in range(2)]
        oh_h = [S.sb(f"oh_h{p}", [P, J, HT], BF16) for p in range(2)]
        oh_l = [S.sb(f"oh_l{p}", [P, J, HT], BF16) for p in range(2)]
        iota_f = S.sb("iota_f", [P, P, GT], BF16)
        wq = S.sb("wq", [P, KC, 2 * NH * DK])
        keys_b = S.sb("keys_b", [P, 4, 4 * NK])
        xc = [S.sb(f"xc{p}", [P, KC, CT]) for p in range(2)]
        qt = S.sb("qt", [P, 4, CT])
        sc = [S.sb(f"sc{p}", [TT, G16, NK]) for p in range(NTILE)]
        keys_n = sc[1][0:NK, 0:NH, :].rearrange("k h r -> k (h r)")
        v16, i16 = S.sb("v16", [TT, G16, TOP]), S.sb("i16", [TT, G16, TOP], U32)
        i16f, step16 = S.sb("i16f", [TT, G16, TOP]), S.sb("step16", [TT, G16, TOP], BF16)
        cv = S.sb("cv", [TT, NH, 64])
        f16, p16 = S.sb("f16", [TT, NH, TOP]), S.sb("p16", [TT, NH, TOP], U32)
        pos_b, col_b = S.sb("pos_b", [TT, NP], BF16), S.sb("col_b", [TT, NP], BF16)
        t1, t2, t3 = S.sb("t1", [TT, NP]), S.sb("t2", [TT, NP]), S.sb("t3", [TT, NP])
        bits, col = S.sb("bits", [TT, NP], U32), S.sb("col", [TT, NP], U32)
        starts_b, ranks_b = S.sb("starts_b", [TT, TOP, TOP], BF16), S.sb("ranks_b", [TT, TOP, TOP], BF16)
        sel = S.sb("sel", [TT, TOP, NP], BF16)
        i1, i2 = S.sb("i1", [TT, NP]), S.sb("i2", [TT, NP])
        codes = [S.sb(f"codes{p}", [TT, 3, NP]) for p in range(NTILE)]
        a_t = S.sb("a_t", [P, CT], BF16)
        b_t = S.sb("b_t", [P, CT], BF16)
        wh_t, wl_t = S.sb("wh_t", [P, CT], BF16), S.sb("wl_t", [P, CT], BF16)
        x_ps = [S.ps(f"x{p}") for p in range(4)]
        sim_ps = [S.ps(f"sim{p}") for p in range(2)]
        tr_ps, out_ps = S.ps("tr"), S.ps("out")
        w_in, d_in, w_turned = S.sem("w_in"), S.sem("d_in"), S.sem("w_turned")
        w_out_a, w_out_d = S.sem("w_out_a"), S.sem("w_out_d")
        xc_in = [S.sem(f"xc_in{p}") for p in range(2)]
        q_done, q_ready, sim_done, sim_ready = S.sem("q_done"), S.sem("q_ready"), S.sem("sim_done"), S.sem("sim_ready")
        codes_ready, tr_done, tr_ready, wl_ready = S.sem("codes_ready"), S.sem("tr_done"), S.sem("tr_ready"), S.sem("wl_ready")
        oh_ready, h_done, gelu_done, m_done, g_done = S.sem("oh_ready"), S.sem("h_done"), S.sem("gelu_done"), S.sem("m_done"), S.sem("g_done")
        out_done, x_done, own, keys_ready = S.sem("out_done"), S.sem("x_done"), S.sem("own"), S.sem("keys_ready")
        iota_done = S.sem("iota_done")
        pad = S.sb("pad", [1, 1])
        block = S.block()
        NPAIR = J // 2
        JS = 8
        stage = [g[:, 0:10, :].rearrange("p j t -> p (j t)")[:, 0:JS * C], g[:, 10:20, :].rearrange("p j t -> p (j t)")[:, 0:JS * C]]

        def by_halves(dram, h):
            return dram.rearrange("(i h j) d -> h i j d", h=2, j=J)[h]

        def chunks(eng, chunk):
            for p in range(2):
                chunk(p, p, False)
            with eng.Fori(1, NCHUNK // 2 - 1) as i:
                for p in range(2):
                    chunk(2 * i + p, p, False)
            for p in range(2):
                chunk(NCHUNK - 2 + p, p, p == 1)

        @block.sync
        def _(sp):
            sp.dma_start(wq[:, :, :], w["wq"].rearrange("(k p) n -> p k n", p=P)).then_inc(w_in, 16)
            sp.dma_start(keys_n.rearrange("k (h r) -> k h r", h=NH), w["keys"].rearrange("h k p d -> k h (p d)")).then_inc(w_in, 16)
            for s in range(J // JS):
                if s >= 2:
                    sp.wait_ge(w_turned, 4 * (s - 1) + 1)
                for h in range(2):
                    sp.dma_start(stage[s % 2][64 * h:64 * h + 64, :].rearrange("p (j d) -> p j d", j=JS),
                                 by_halves(w["expert_down"], h)[:, s * JS:(s + 1) * JS, :]).then_inc(d_in, 16)
                if s == 0:
                    for p in range(2):
                        sp.dma_start(xc[p][:, :, :], xn_dram[:, :, p * CT:(p + 1) * CT].rearrange("k p t -> p k t")).then_inc(xc_in[p], 16)
                sp.wait_ge(d_in, 32 * (s + 1))
            for h in range(2):
                sp.dma_start(up[64 * h:64 * h + 64, :, :], by_halves(w["expert_up"], h)).then_inc(w_in, 16)

            def body(i):
                for p in range(2):
                    n = 2 * i + p
                    sp.wait_ge(h_done, NPAIR * (n + 1))
                    sp.dma_start(xc[p][:, :, :], xn_dram[:, :, bass.ds((n + 2) * CT, CT)].rearrange("k p t -> p k t")).then_inc(xc_in[p], 16)
            steps(sp, NCHUNK // 2 - 1, body)

        @block.gpsimd
        def _(pool):
            nc.gpsimd.iota(iota_f[:, :, :], [[1, P], [0, GT]], base=0, channel_multiplier=0,
                           allow_small_or_imprecise_dtypes=True).then_inc(iota_done, 1)
            nc.gpsimd.iota(ranks_b[:, :, :], [[1, TOP], [0, TOP]], base=0, channel_multiplier=0,
                           allow_small_or_imprecise_dtypes=True).then_inc(iota_done, 1)
            for a in range(TOP):
                nc.gpsimd.memset(starts_b[:, a, :], float(row_start[a])).then_inc(iota_done, 1)
            nc.gpsimd.memset(keys_b[:, :, :], 0.0).then_inc(iota_done, 1)

        @block.tensor
        def _(pe):
            def queries(n, p):
                pe.wait_ge(xc_in[p], 8 * (n - p) + 16)
                wait(pe, sim_ready, NTILE * n)
                for m in range(4):
                    for k in range(KC):
                        mm = nc.tensor.matmul(sim_ps[m // 2][:, (m % 2) * CT:(m % 2 + 1) * CT], wq[:, k, m * P:(m + 1) * P],
                                              xc[p][:, k, :], start=(k == 0), stop=(k == KC - 1))
                mm.then_inc(q_done, 1)

            def scores(n, t):
                pe.wait_ge(q_ready, n + 1)
                if t > 0:
                    pe.wait_ge(sim_ready, NTILE * n + t)
                for m in range(4):
                    mm = nc.tensor.matmul(sim_ps[m // 2][0:TT, (m % 2) * 4 * NK:(m % 2 + 1) * 4 * NK], qt[:, m, t * TT:(t + 1) * TT],
                                          keys_b[:, m, :], start=True, stop=True)
                mm.then_inc(sim_done, 1)

            def hidden(n, p):
                for jp in range(NPAIR):
                    b = jp % 4
                    if jp < 4:
                        wait(pe, g_done, 16 * n - 3 + jp)
                    else:
                        pe.wait_ge(gelu_done, NPAIR * n + jp - 3)
                    for jj in range(2):
                        for k in range(KC):
                            mm = nc.tensor.matmul(x_ps[b][:, jj * CT:(jj + 1) * CT], dt[:, k, 2 * jp + jj, :], xc[p][:, k, :],
                                                  start=(k == 0), stop=(k == KC - 1))
                    mm.then_inc(h_done, 1)

            def turn(n, t):
                pe.wait_ge(codes_ready, NTILE * n + t + 1)
                wait(pe, tr_ready, NTILE * n + t)
                wait(pe, wl_ready, NTILE * n + t)
                for s in range(3):
                    mm = nc.tensor.transpose(tr_ps[:, s * TT:(s + 1) * TT], codes[t][:, s, :], ident[0:TT, 0:TT])
                mm.then_inc(tr_done, 1)

            def scatter(n, hb):
                pe.wait_ge(oh_ready, NHB * n + hb + 1)
                for q in range(4):
                    if hb == 0:
                        pe.wait_ge(gelu_done, NPAIR * n + NPAIR - 3 + q)
                    else:
                        pe.wait_ge(g_done, 16 * n + 4 * (hb - 1) + q + 1)
                    for i in range(GT):
                        t = q * GT + i
                        nc.tensor.matmul(x_ps[q][:, i * J:(i + 1) * J], oh_a[hb % 2][:, :, t], oh_h[hb % 2][:, :, t], start=True, stop=False)
                        mm = nc.tensor.matmul(x_ps[q][:, i * J:(i + 1) * J], oh_a[hb % 2][:, :, t], oh_l[hb % 2][:, :, t], start=False, stop=True)
                    mm.then_inc(m_done, 1)

            def experts_out(n):
                pe.wait_ge(g_done, 16 * n + 16)
                wait(pe, x_done, n)
                for m in range(KC):
                    for j in range(J):
                        mm = nc.tensor.matmul(out_ps[:, m * CT:(m + 1) * CT], up[:, j, m * P:(m + 1) * P], g[:, j, :],
                                              start=(j == 0), stop=(j == J - 1))
                mm.then_inc(out_done, 1)

            pe.wait_ge(w_in, 16 * 2)
            for m in range(4):
                mm = nc.tensor.transpose(tr_ps[:, m * NK:(m + 1) * NK], keys_n[:, m * P:(m + 1) * P], ident[0:NK, 0:NK])
            mm.then_inc(w_turned, 1)
            for s in range(J // JS):
                pe.wait_ge(d_in, 32 * (s + 1))
                for r in range(4):
                    i = 4 * s + r
                    if i >= 4:
                        pe.wait_ge((w_out_a, w_out_d)[i % 2], (i - 4) // 2 + 1)
                    for jj in range(2):
                        for k in range(KC):
                            j = 2 * r + jj
                            mm = nc.tensor.transpose(x_ps[i % 4][:, (2 * jj + k) * P:(2 * jj + k + 1) * P],
                                                     stage[s % 2][:, j * C + k * P:j * C + (k + 1) * P], ident[:, :])
                    mm.then_inc(w_turned, 1)
            pe.wait_ge(w_out_a, 8)
            pe.wait_ge(w_out_d, 8)
            pe.wait_ge(keys_ready, 1)
            queries(0, 0)
            for t in range(NTILE):
                scores(0, t)
            pe.wait_ge(w_in, 16 * 4)

            def chunk(n, p, last):
                hidden(n, p)
                for t in range(NTILE):
                    turn(n, t)
                for hb in range(NHB):
                    scatter(n, hb)
                if not last:
                    queries(n + 1, 1 - p)
                    for t in range(NTILE):
                        scores(n + 1, t)
                experts_out(n)
            chunks(pe, chunk)

        @block.scalar
        def _(act):
            act.preload_act_table(ACT.Gelu)
            for i in range(0, 16, 2):
                act.wait_ge(w_turned, i + 2)
                nc.scalar.activation(dt[:, :, 2 * i:2 * i + 2, :].rearrange("p k j e -> p j k e"),
                                     x_ps[i % 4][:, :].rearrange("p (j k e) -> p j k e", j=2, k=KC), ACT.Copy).then_inc(w_out_a, 1)

            def query_out(n):
                act.wait_ge(q_done, n + 1)
                for b in range(2):
                    ins = nc.scalar.activation(qt[:, 2 * b:2 * b + 2, :], sim_ps[b][:, 0:2 * CT].rearrange("p (m t) -> p m t", m=2), ACT.Copy)
                ins.then_inc(q_ready, 1)

            def score_out(n, t):
                act.wait_ge(sim_done, NTILE * n + t + 1)
                for b in range(2):
                    ins = nc.scalar.activation(sc[t][:, 8 * b:8 * b + 8, :], sim_ps[b][0:TT, :].rearrange("p (g k) -> p g k", g=8), ACT.Copy)
                ins.then_inc(sim_ready, 1)

            query_out(0)
            for t in range(NTILE):
                score_out(0, t)

            def chunk(n, p, last):
                wait(act, out_done, n)
                for jp in range(NPAIR):
                    act.wait_ge(h_done, NPAIR * n + jp + 1)
                    nc.scalar.activation(g[:, 2 * jp:2 * jp + 2, :], x_ps[jp % 4][:, 0:2 * CT].rearrange("p (j t) -> p j t", j=2),
                                         ACT.Gelu).then_inc(gelu_done, 1)
                for t in range(NTILE):
                    act.wait_ge(tr_done, NTILE * n + t + 1)
                    ts = slice(t * TT, (t + 1) * TT)
                    if t == 0:
                        wait(act, oh_ready, NHB * n)
                    nc.scalar.activation(wh_t[:, ts], tr_ps[:, 2 * TT:3 * TT], ACT.Copy)
                    nc.scalar.activation(a_t[:, ts], tr_ps[:, 0:TT], ACT.Copy)
                    nc.scalar.activation(b_t[:, ts], tr_ps[:, TT:2 * TT], ACT.Copy).then_inc(tr_ready, 1)
                if not last:
                    query_out(n + 1)
                    for t in range(NTILE):
                        score_out(n + 1, t)
            chunks(act, chunk)

        @block.vector
        def _(dve):
            dve.wait_ge(w_turned, 1)
            dve.wait_ge(iota_done, TOP + 3)
            for q in range(4):
                rows = slice(32 * q, 32 * q + 32)
                ins = nc.vector.tensor_copy(keys_b[rows, :, q * NK:(q + 1) * NK], tr_ps[rows, 0:4 * NK].rearrange("p (m k) -> p m k", m=4))
            ins.then_inc(keys_ready, 1)
            for i in range(1, 16, 2):
                dve.wait_ge(w_turned, i + 2)
                nc.vector.tensor_copy(dt[:, :, 2 * i:2 * i + 2, :].rearrange("p k j e -> p j k e"),
                                      x_ps[i % 4][:, :].rearrange("p (j k e) -> p j k e", j=2, k=KC)).then_inc(w_out_d, 1)
            chain = Chain(dve, own)

            def top16(values, indices, source, groups):
                for half in range(2):
                    r = slice(8 * half, 8 * half + 8)
                    for q in range(groups):
                        ins = nc.vector.max(values[:, q, r], source[:, q, :])
                    chain.step(ins)
                    chain.wait()
                    nc.vector.memset(pad[:, :], 0.0)
                    for q in range(groups):
                        last = nc.vector.max_index(indices[:, q, r], values[:, q, r], source[:, q, :])
                        if half == 0:
                            ins = nc.vector.match_replace(source[:, q, :], values[:, q, r], source[:, q, :], LOWEST)
                    if half == 1:
                        ins = last
                    chain.step(ins)
                    if half == 0:
                        chain.wait()
                        nc.vector.memset(pad[:, :], 0.0)

            def pick(out, place, table, which):
                steps_v = step16[:, :, :].rearrange("t (h w) a -> t w a h", w=2)[:, which, :, :]
                sv = sel[:, :, :].rearrange("t a (h k) -> t a h k", k=TOP)
                places = place.rearrange("t (h k) -> t h k", k=TOP)
                chain.step(nc.vector.tensor_tensor(sv, places.unsqueeze(1).broadcast_to([TT, TOP, NH, TOP]),
                                                   table[:, :, :].unsqueeze(2).broadcast_to([TT, TOP, NH, TOP]), ALU.is_ge))
                chain.wait()
                chain.step(nc.vector.tensor_tensor(sv, sv, steps_v.unsqueeze(3).broadcast_to([TT, TOP, NH, TOP]), ALU.mult))
                n = TOP // 2
                while n > 1:
                    chain.wait()
                    chain.step(nc.vector.tensor_tensor(sel[:, 0:n, :], sel[:, 0:n, :], sel[:, n:2 * n, :], ALU.add))
                    n //= 2
                chain.wait()
                chain.step(nc.vector.tensor_tensor(out[:, :], sel[:, 0, :], sel[:, 1, :], ALU.add))

            def make_codes(n, t):
                dve.wait_ge(sim_ready, NTILE * n + t + 1)
                nc.vector.memset(pad[:, :], 0.0)
                top16(v16, i16, sc[t], G16)
                v = v16[:, :, :].rearrange("t (h w) a -> t w h a", w=2)
                o = 0
                for a0, na, nb in CAND:
                    out = cv[:, :, o:o + na * nb]
                    v1, v2 = v[:, 0, :, a0:a0 + na], v[:, 1, :, 0:nb]
                    if na == 1:
                        v1 = v1.broadcast_to([TT, NH, nb])
                    elif nb == 1:
                        v2 = v2.broadcast_to([TT, NH, na])
                    else:
                        out = out.rearrange("t h (a b) -> t h a b", a=na)
                        v1 = v1.unsqueeze(3).broadcast_to([TT, NH, na, nb])
                        v2 = v2.unsqueeze(2).broadcast_to([TT, NH, na, nb])
                    if o == 0:
                        chain.wait()
                    ins = nc.vector.tensor_tensor(out, v1, v2, ALU.add)
                    o += na * nb
                chain.step(ins)
                chain.step(nc.vector.tensor_copy(i16f[:, :, :], i16[:, :, :]))
                chain.wait()
                nc.vector.tensor_tensor(step16[:, :, 1:TOP], i16f[:, :, 1:TOP], i16f[:, :, 0:TOP - 1], ALU.subtract)
                chain.step(nc.vector.tensor_copy(step16[:, :, 0:1], i16f[:, :, 0:1]))
                chain.wait()
                nc.vector.memset(pad[:, :], 0.0)
                top16(f16, p16, cv, NH)
                fv = f16[:, :, :].rearrange("t h k -> t (h k)")
                pv = p16[:, :, :].rearrange("t h k -> t (h k)")
                chain.wait()
                wait(dve, tr_done, NTILE * (n - 1) + t + 1)
                chain.step(nc.vector.tensor_scalar(codes[t][:, 2, :], fv, 0.0, None, ALU.max))
                chain.step(nc.vector.tensor_copy(pos_b[:, :], pv))
                chain.wait()
                chain.step(nc.vector.tensor_scalar(t1[:, :], pos_b[:, :], 16.0, -8.0, ALU.is_ge, ALU.mult))
                chain.step(nc.vector.tensor_scalar(t2[:, :], pos_b[:, :], 40.0, -4.0, ALU.is_ge, ALU.mult))
                chain.step(nc.vector.tensor_scalar(t3[:, :], pos_b[:, :], 56.0, -3.0, ALU.is_ge, ALU.mult))
                chain.wait()
                chain.step(nc.vector.tensor_tensor(t1[:, :], t1[:, :], t2[:, :], ALU.add))
                chain.wait()
                chain.step(nc.vector.scalar_tensor_tensor(bits[:, :], t1[:, :], 15.0, t3[:, :], ALU.add, ALU.add))
                chain.wait()
                chain.step(nc.vector.tensor_tensor(col[:, :], pv, bits[:, :], ALU.bitwise_and))
                chain.wait()
                chain.step(nc.vector.tensor_copy(col_b[:, :], col[:, :]))
                pick(i1, pos_b[:, :], starts_b, 0)
                chain.wait()
                pick(i2, col_b[:, :], ranks_b, 1)
                chain.wait()
                chain.step(nc.vector.tensor_scalar(t1[:, :], i2[:, :], 32.0, 64.0, ALU.is_ge, ALU.mult))
                chain.wait()
                nc.vector.tensor_tensor(codes[t][:, 0, :], t1[:, :], i1[:, :], ALU.add)
                nc.vector.scalar_tensor_tensor(codes[t][:, 1, :], t1[:, :], -0.5, i2[:, :], ALU.mult, ALU.add).then_inc(codes_ready, 1)

            def low_weights(n, t):
                dve.wait_ge(tr_ready, NTILE * n + t + 1)
                ts = slice(t * TT, (t + 1) * TT)
                nc.vector.tensor_tensor(wl_t[:, ts], tr_ps[:, 2 * TT:3 * TT], wh_t[:, ts], ALU.subtract).then_inc(wl_ready, 1)

            def one_hots(n, hb):
                q = hb % 2
                wait(dve, m_done, 16 * n + 4 * (hb - 1))
                if hb % 2 == 0:
                    dve.wait_ge(wl_ready, NTILE * n + hb // 2 + 1)
                ts = slice(hb * HT, (hb + 1) * HT)

                def spread(v, rows):
                    return v[:, ts].rearrange("p (a b) -> p a b", b=GT).unsqueeze(1).broadcast_to([P, rows, HT // GT, GT])

                def number(rows):
                    return iota_f[:, 0:rows, :].unsqueeze(2).broadcast_to([P, rows, HT // GT, GT])

                def view(m):
                    return m[:, :, :].rearrange("p r (a b) -> p r a b", b=GT)
                nc.vector.tensor_tensor(view(oh_a[q]), spread(a_t, P), number(P), ALU.is_equal)
                chain.step(nc.vector.tensor_tensor(view(oh_l[q]), spread(b_t, J), number(J), ALU.is_equal))
                chain.wait()
                for dst, wt in ((oh_h, wh_t), (oh_l, wl_t)):
                    ins = nc.vector.tensor_tensor(dst[q][:, :, :], oh_l[q][:, :, :], wt[:, ts].unsqueeze(1).broadcast_to([P, J, HT]), ALU.mult)
                ins.then_inc(oh_ready, 1)

            def weigh(n, hb):
                for q in range(4):
                    dve.wait_ge(m_done, 16 * n + 4 * hb + q + 1)
                    ts = slice(hb * HT + q * GT, hb * HT + (q + 1) * GT)
                    nc.vector.tensor_tensor(g[:, :, ts], g[:, :, ts], x_ps[q][:, 0:GT * J].rearrange("p (t j) -> p j t", j=J),
                                            ALU.mult).then_inc(g_done, 1)

            for t in range(NTILE):
                make_codes(0, t)
            first = [True]

            def chunk(n, p, last):
                if p == 0:
                    chain.turn(0 if first[0] else n // 2 if isinstance(n, int) else turn_no[0])
                    first[0] = False
                for t in range(NTILE):
                    low_weights(n, t)
                one_hots(n, 0)
                for hb in range(NHB):
                    if hb + 1 < NHB:
                        one_hots(n, hb + 1)
                    weigh(n, hb)
                if not last:
                    for t in range(NTILE):
                        make_codes(n + 1, t)
                dve.wait_ge(out_done, n + 1)
                xs = x[:, :, bass.ds(n * CT, CT)]
                nc.vector.tensor_tensor(xs, xs, out_ps[:, 0:KC * CT].rearrange("p (k t) -> p k t", k=KC), ALU.add).then_inc(x_done, 1)

            turn_no = [0]
            for p in range(2):
                chunk(p, p, False)
            with dve.Fori(1, NCHUNK // 2 - 1) as i:
                turn_no[0] = i
                for p in range(2):
                    chunk(2 * i + p, p, False)
            for p in range(2):
                chunk(NCHUNK - 2 + p, p, p == 1)


def moe_ffn(nc, x, xn, y_dram, w, ident):
    E, F = 8, 1024
    CAP = NT // E
    TT = 112
    NTILES = NT // TT
    Q = 4
    KF = F // P
    ST = CAP // 4
    LW = C + E
    IMGS = 4
    with Scope(nc, "moe") as S:
        expert_in = nc.dram_tensor("moe_expert_in", [2 * NT, C], F32, kind="Internal").ap()
        expert_out = nc.dram_tensor("moe_expert_out", [NT, C], F32, kind="Internal").ap()
        router = S.sb("router", [P, KC, E])
        xs = [S.sb(f"xs{q}", [P, KC, TT]) for q in range(Q)]
        rows = S.sb("rows", [TT, NTILES, LW])
        marks = S.sb("marks", [1, NTILES // Q])
        zero = S.sb("zero", [TT, C])
        tri, ones = S.sb("tri", [TT, TT]), S.sb("ones", [TT, TT])
        e_num, spare = S.sb("e_num", [TT, NTILES, E]), S.sb("spare", [TT, NTILES])
        best, dist, expd = S.sb("best", [TT, NTILES]), S.sb("dist", [TT, NTILES, E]), S.sb("expd", [TT, NTILES, E])
        total, gate = S.sb("total", [TT, NTILES]), S.sb("gate", [TT, NTILES])
        cand, first, onehot = S.sb("cand", [TT, NTILES, E]), S.sb("first", [TT, NTILES]), S.sb("onehot", [TT, NTILES, E])
        before = [S.sb(f"before{p}", [TT, NTILES, E]) for p in range(2)]
        count, picked = S.sb("count", [TT, NTILES, E]), S.sb("picked", [TT, NTILES])
        kept, slot_f, sent_f = S.sb("kept", [TT, NTILES]), S.sb("slot_f", [TT, NTILES]), S.sb("sent_f", [TT, NTILES])
        slot, sent = S.sb("slot", [TT, NTILES], U32), S.sb("sent", [TT, NTILES], U32)
        w1 = [S.sb(f"w1_{p}", [P, KC, F]) for p in range(2)]
        w2 = [S.sb(f"w2_{p}", [P, KF, C]) for p in range(2)]
        b1_rows, b1, b2 = S.sb("b1_rows", [E * KF, P]), S.sb("b1", [P, E * KF]), S.sb("b2", [ST, E, C])
        ein = [S.sb(f"ein{p}", [ST, 4, C]) for p in range(2)]
        ein_t = [S.sb(f"ein_t{p}", [P, KC, CAP]) for p in range(2)]
        h = [S.sb(f"h{p}", [P, KF, CAP]) for p in range(2)]
        y = [S.sb(f"y{p}", [ST, 4, C]) for p in range(2)]
        scaled = [S.sb(f"scaled{q}", [TT, C]) for q in range(Q)]
        a_ps = [S.ps(f"a{q}") for q in range(4)]
        t_ps = [S.ps(f"t{k}") for k in range(2)]
        y_ps = [S.ps(f"y{k}") for k in range(2)]
        consts_in, consts = S.sem("consts_in"), S.sem("consts")
        w_in = [S.sem(f"w_in{p}") for p in range(2)]
        ein_in = [S.sem(f"ein_in{p}") for p in range(2)]
        y_out = [S.sem(f"y_out{p}") for p in range(2)]
        zeroed, scattered, x_out = S.sem("zeroed"), S.sem("scattered"), S.sem("x_out")
        copied, turned, rows_ready = S.sem("copied"), S.sem("turned"), S.sem("rows_ready")
        b1_turned, b1_ready = S.sem("b1_turned"), S.sem("b1_ready")
        own, dist_ready, exp_ready = S.sem("own"), S.sem("dist_ready"), S.sem("exp_ready")
        onehot_ready, counted, slots_ready = S.sem("onehot_ready"), S.sem("counted"), S.sem("slots_ready")
        ein_turned, ein_ready, h_done, h_ready = S.sem("ein_turned"), S.sem("ein_ready"), S.sem("h_done"), S.sem("h_ready")
        y_done, y_ready = S.sem("y_done"), S.sem("y_ready")
        gathered = [S.sem(f"gathered{p}") for p in range(2)]
        rows_back, scaled_ready, back_turned, x_done = S.sem("rows_back"), S.sem("scaled_ready"), S.sem("back_turned"), S.sem("x_done")
        block = S.block()
        ROUTED = 4 * (NTILES // Q)

        def slots_of(dram, e):
            return dram[bass.ds(e * CAP, CAP), :].rearrange("(s p) d -> p s d", p=ST)

        @block.sync
        def _(sp):
            sp.dma_start(router[:, :, :], w["router_w"].rearrange("(k p) e -> p k e", p=P)).then_inc(consts_in, 16)
            sp.dma_start(b1_rows[:, :], w["b1"].rearrange("e (f p) -> (e f) p", p=P)).then_inc(consts_in, 16)
            sp.dma_start(b2[:, :, :], w["b2"].unsqueeze(0).broadcast_to([ST, E, C])).then_inc(consts_in, 16)
            sp.wait_ge(consts, 1)
            sp.dma_start(expert_in[0:NT, :].rearrange("(j p) d -> p j d", p=TT),
                         zero[:, :].unsqueeze(1).broadcast_to([TT, NTILES, C])).then_inc(zeroed, 16)

            def weights(e, p):
                sp.dma_start(w1[p][:, :, :], w["w1"][bass.ds(e, 1)].rearrange("o (k p) f -> p (o k) f", p=P)).then_inc(w_in[p], 16)
                sp.dma_start(w2[p][:, :, :], w["w2"][bass.ds(e, 1)].rearrange("o (k p) d -> p (o k) d", p=P)).then_inc(w_in[p], 16)
            for p in range(2):
                weights(p, p)
            sp.wait_ge(scattered, 16 * NTILES)
            for p in range(2):
                sp.dma_start(ein[p][:, :, :], slots_of(expert_in, p)).then_inc(ein_in[p], 16)

            def body(i):
                for p in range(2):
                    e = 2 * i + p
                    sp.wait_ge(y_ready, 4 * (e + 1))
                    sp.dma_start(slots_of(expert_out, e), y[p][:, :, :]).then_inc(y_out[p], 16)
                    if isinstance(i, int) and i == E // 2 - 1:
                        continue
                    sp.wait_ge(ein_turned, e + 1)
                    sp.dma_start(ein[p][:, :, :], slots_of(expert_in, e + 2)).then_inc(ein_in[p], 16)
                    weights(e + 2, p)
            body(0)
            with sp.Fori(1, E // 2 - 1) as i:
                body(i)
            body(E // 2 - 1)
            for b in range(0, B, IMGS):
                sp.wait_ge(x_done, (b + IMGS) * HW // TT)
                for k in range(KC):
                    sp.dma_start(y_dram[b:b + IMGS, k * P:(k + 1) * P, :].rearrange("b p t -> p b t"),
                                 x[:, k, b * HW:(b + IMGS) * HW].rearrange("p (b t) -> p b t", b=IMGS)).then_inc(x_out, 16)
            sp.wait_ge(x_out, 16 * KC * B // IMGS)
            for p in range(2):
                sp.wait_ge(y_out[p], 16 * E // 2)

        @block.gpsimd
        def _(pool):
            nc.gpsimd.memset(zero[:, :], 0.0).then_inc(consts, 1)
            nc.gpsimd.memset(ones[:, :], 1.0).then_inc(consts, 1)
            nc.gpsimd.iota(e_num[:, :, :], [[0, NTILES], [1, E]], base=0, channel_multiplier=0,
                           allow_small_or_imprecise_dtypes=True).then_inc(consts, 1)
            nc.gpsimd.iota(spare[:, :], [[TT, NTILES]], base=NT, channel_multiplier=1,
                           allow_small_or_imprecise_dtypes=True).then_inc(consts, 1)
            pool.wait_ge(consts, 4)
            nc.gpsimd.affine_select(out=tri[:, :], in_=ones[:, :], compare_op=ALU.is_ge, fill=0.0,
                                    base=0, pattern=[[1, TT]], channel_multiplier=-1).then_inc(consts, 1)
            pool.wait_ge(slots_ready, 1)
            pool.wait_ge(zeroed, 16)
            for j in range(NTILES):
                pool.indirect_dma_start(expert_in[:, :], bass.IndirectOffsetOnAxis(ap=sent[:, j:j + 1], axis=0),
                                        rows[:, j, 0:C], None).then_inc(scattered, 16)
            pool.wait_ge(scattered, 16 * NTILES)
            for p in range(2):
                pool.wait_ge(y_out[p], 16 * E // 2)
            for i in range(NTILES // Q):
                for q in range(Q):
                    j = Q * i + q
                    pool.indirect_dma_start(rows[:, j, 0:C], None, expert_out[:, :],
                                            bass.IndirectOffsetOnAxis(ap=slot[:, j:j + 1], axis=0)).then_inc(gathered[i % 2], 16)
                if i > 0:
                    pool.wait_ge(gathered[(i - 1) % 2], 16 * Q * ((i - 1) // 2 + 1))
                    nc.gpsimd.memset(marks[:, i - 1:i], 0.0).then_inc(rows_back, 1)
            pool.wait_ge(gathered[(NTILES // Q - 1) % 2], 16 * Q * ((NTILES // Q - 1) // 2 + 1))
            nc.gpsimd.memset(marks[:, NTILES // Q - 1:NTILES // Q], 0.0).then_inc(rows_back, 1)

        @block.tensor
        def _(pe):
            pe.wait_ge(consts_in, 48)
            nc.tensor.transpose(y_ps[0][:, 0:E * KF], b1_rows[:, :], ident[0:E * KF, 0:E * KF]).then_inc(b1_turned, 1)

            def route(i):
                for q in range(Q):
                    j = Q * i + q
                    pe.wait_ge(copied, j + 1)
                    wait(pe, rows_ready, j - Q + 1)
                    for k in range(KC):
                        nc.tensor.transpose(a_ps[q][0:TT, k * P:(k + 1) * P], xs[q][:, k, :], ident[:, :])
                    for k in range(KC):
                        mm = nc.tensor.matmul(a_ps[q][0:TT, C:LW], xs[q][:, k, :], router[:, k, :], start=(k == 0), stop=(k == KC - 1))
                    mm.then_inc(turned, 1)
            steps(pe, NTILES // Q, route)
            pe.wait_ge(consts, 5)
            pe.wait_ge(onehot_ready, 1)
            oh = onehot[:, :, :].rearrange("p j e -> p (j e)")
            nc.tensor.matmul(t_ps[0][0:TT, 0:NTILES * E], tri[:, :], oh, start=True, stop=True)
            nc.tensor.matmul(t_ps[1][0:TT, 0:NTILES * E], ones[:, :], oh, start=True, stop=True).then_inc(counted, 1)

            def experts(i):
                for p in range(2):
                    e = 2 * i + p
                    pe.wait_ge(ein_in[p], 16 * (i + 1))
                    if isinstance(e, int) and e == 0:
                        pe.wait_ge(slots_ready, 1)
                        pe.wait_ge(b1_ready, 1)
                    else:
                        pe.wait_ge(ein_ready, e)
                    for k in range(KC):
                        for s in range(4):
                            mm = nc.tensor.transpose(t_ps[k][:, s * ST:(s + 1) * ST], ein[p][:, s, k * P:(k + 1) * P], ident[0:ST, 0:ST])
                    mm.then_inc(ein_turned, 1)
                    pe.wait_ge(w_in[p], 32 * (i + 1))
                    pe.wait_ge(ein_ready, e + 1)
                    for f in range(KF):
                        wait(pe, h_ready, KF * e + f - 3)
                        for k in range(KC):
                            mm = nc.tensor.matmul(a_ps[f % 4][:, 0:CAP], w1[p][:, k, f * P:(f + 1) * P], ein_t[p][:, k, :],
                                                  start=(k == 0), stop=(k == KC - 1))
                        mm.then_inc(h_done, 1)
                    for s in range(4):
                        wait(pe, y_ready, 4 * e + s - 1)
                        for f in range(KF):
                            if s == 0:
                                pe.wait_ge(h_ready, KF * e + f + 1)
                            mm = nc.tensor.matmul(y_ps[s % 2][0:ST, 0:C], h[p][:, f, s * ST:(s + 1) * ST], w2[p][:, f, :],
                                                  start=(f == 0), stop=(f == KF - 1))
                        mm.then_inc(y_done, 1)
            steps(pe, E // 2, experts)

            def back(i):
                for q in range(Q):
                    j = Q * i + q
                    pe.wait_ge(scaled_ready, j + 1)
                    wait(pe, x_done, j - Q + 1)
                    for k in range(KC):
                        mm = nc.tensor.transpose(a_ps[q][:, k * TT:(k + 1) * TT], scaled[q][:, k * P:(k + 1) * P], ident[0:TT, 0:TT])
                    mm.then_inc(back_turned, 1)
            steps(pe, NTILES // Q, back)

        @block.scalar
        def _(act):
            act.preload_act_table_set(LN_EXP)
            act.wait_ge(b1_turned, 1)
            nc.scalar.activation(b1[:, :], y_ps[0][:, 0:E * KF], ACT.Copy).then_inc(b1_ready, 1)
            act.wait_ge(dist_ready, 1)
            nc.scalar.activation(expd[:, :, :], dist[:, :, :], ACT.Exp).then_inc(exp_ready, 1)

            def experts(i):
                for p in range(2):
                    e = 2 * i + p
                    act.wait_ge(ein_turned, e + 1)
                    for k in range(KC):
                        ins = nc.scalar.activation(ein_t[p][:, k, :], t_ps[k][:, 0:CAP], ACT.Copy)
                    ins.then_inc(ein_ready, 1)
                    wait(act, y_done, 4 * (e - 1))
                    for f in range(KF):
                        act.wait_ge(h_done, KF * e + f + 1)
                        nc.scalar.activation(h[p][:, f, :], a_ps[f % 4][:, 0:CAP], ACT.Relu, bias=b1[:, bass.ds(e * KF + f, 1)]).then_inc(h_ready, 1)
            steps(act, E // 2, experts)

        @block.vector
        def _(dve):
            chain = Chain(dve, own)

            def copy_in(i):
                for q in range(Q):
                    j = Q * i + q
                    wait(dve, turned, j - Q + 1)
                    nc.vector.tensor_scalar(xs[q][:, :, :], xn[:, :, bass.ds(j * TT, TT)], 1.0, None, ALU.mult).then_inc(copied, 1)
                for q in range(Q):
                    j = Q * i + q
                    dve.wait_ge(turned, j + 1)
                    nc.vector.tensor_scalar(rows[:, bass.ds(j, 1), :].rearrange("p o c -> p (o c)"), a_ps[q][0:TT, 0:LW], 1.0, None,
                                            ALU.mult).then_inc(rows_ready, 1)
            steps(dve, NTILES // Q, copy_in)
            dve.wait_ge(consts, 5)
            dve.wait_ge(rows_ready, NTILES)
            logits = rows[:, :, C:LW]

            def each(t):
                return t[:, :].unsqueeze(2).broadcast_to([TT, NTILES, E])
            chain.step(nc.vector.tensor_reduce(best[:, :], logits, AX_X, ALU.max))
            chain.wait()
            nc.vector.tensor_tensor(dist[:, :, :], logits, each(best), ALU.subtract).then_inc(dist_ready, 1)
            dve.wait_ge(dist_ready, 1)
            chain.step(nc.vector.tensor_scalar(cand[:, :, :], dist[:, :, :], 0.0, -float(E), ALU.is_ge, ALU.mult))
            chain.wait()
            chain.step(nc.vector.tensor_tensor(cand[:, :, :], cand[:, :, :], e_num[:, :, :], ALU.add))
            chain.wait()
            chain.step(nc.vector.tensor_reduce(first[:, :], cand[:, :, :], AX_X, ALU.min))
            chain.wait()
            nc.vector.tensor_tensor(onehot[:, :, :], cand[:, :, :], each(first), ALU.is_equal).then_inc(onehot_ready, 1)
            dve.wait_ge(exp_ready, 1)
            chain.step(nc.vector.tensor_reduce(total[:, :], expd[:, :, :], AX_X, ALU.add))
            chain.wait()
            chain.step(nc.vector.reciprocal(gate[:, :], total[:, :]))
            dve.wait_ge(counted, 1)
            chain.step(nc.vector.tensor_copy(before[0][:, 1:NTILES, :],
                                             t_ps[1][0:TT, 0:(NTILES - 1) * E].rearrange("p (j e) -> p j e", e=E)))
            chain.step(nc.vector.memset(before[0][:, 0:1, :], 0.0))
            d, src = 1, 0
            while d < NTILES:
                chain.wait()
                a, b = before[src], before[1 - src]
                chain.step(nc.vector.tensor_tensor(b[:, d:NTILES, :], a[:, d:NTILES, :], a[:, 0:NTILES - d, :], ALU.add))
                chain.step(nc.vector.tensor_copy(b[:, 0:d, :], a[:, 0:d, :]))
                d, src = 2 * d, 1 - src
            chain.wait()
            chain.step(nc.vector.tensor_tensor(count[:, :, :], before[src][:, :, :],
                                               t_ps[0][0:TT, 0:NTILES * E].rearrange("p (j e) -> p j e", e=E), ALU.add))
            chain.wait()
            chain.step(nc.vector.tensor_tensor(count[:, :, :], count[:, :, :], onehot[:, :, :], ALU.mult))
            chain.wait()
            chain.step(nc.vector.tensor_reduce(picked[:, :], count[:, :, :], AX_X, ALU.add))
            chain.wait()
            chain.step(nc.vector.tensor_scalar(kept[:, :], picked[:, :], float(CAP), None, ALU.is_le))
            chain.step(nc.vector.tensor_scalar(slot_f[:, :], first[:, :], float(CAP), float(CAP * E - 1), ALU.mult, ALU.add))
            chain.wait()
            chain.step(nc.vector.tensor_tensor(slot_f[:, :], slot_f[:, :], picked[:, :], ALU.add))
            chain.step(nc.vector.tensor_tensor(gate[:, :], gate[:, :], kept[:, :], ALU.mult))
            chain.wait()
            chain.step(nc.vector.tensor_tensor(slot_f[:, :], slot_f[:, :], kept[:, :], ALU.mult))
            chain.step(nc.vector.tensor_tensor(kept[:, :], spare[:, :], kept[:, :], ALU.mult))
            chain.wait()
            chain.step(nc.vector.tensor_tensor(sent_f[:, :], slot_f[:, :], spare[:, :], ALU.add))
            chain.wait()
            chain.step(nc.vector.tensor_tensor(sent_f[:, :], sent_f[:, :], kept[:, :], ALU.subtract))
            chain.wait()
            chain.step(nc.vector.tensor_copy(slot[:, :], slot_f[:, :]))
            nc.vector.tensor_copy(sent[:, :], sent_f[:, :]).then_inc(slots_ready, 1)

            def experts(i):
                for p in range(2):
                    e = 2 * i + p
                    wait(dve, y_out[p], 16 * i)
                    for s in range(4):
                        dve.wait_ge(y_done, 4 * e + s + 1)
                        nc.vector.tensor_tensor(y[p][:, s, :], y_ps[s % 2][0:ST, 0:C], b2[:, bass.ds(e, 1), :].rearrange("p o c -> p (o c)"),
                                                ALU.add).then_inc(y_ready, 1)
            dve.wait_ge(consts_in, 48)
            steps(dve, E // 2, experts)

            def back(i):
                dve.wait_ge(rows_back, i + 1)
                for q in range(Q):
                    j = Q * i + q
                    wait(dve, back_turned, j - Q + 1)
                    nc.vector.tensor_scalar(scaled[q][:, :], rows[:, bass.ds(j, 1), 0:C].rearrange("p o c -> p (o c)"),
                                            gate[:, bass.ds(j, 1)], None, ALU.mult).then_inc(scaled_ready, 1)
                for q in range(Q):
                    j = Q * i + q
                    dve.wait_ge(back_turned, j + 1)
                    xt = x[:, :, bass.ds(j * TT, TT)]
                    nc.vector.tensor_tensor(xt, xt, a_ps[q][:, 0:KC * TT].rearrange("p (k t) -> p k t", k=KC), ALU.add).then_inc(x_done, 1)
            steps(dve, NTILES // Q, back)


def store_tokens(nc, xn, xn_dram):
    with Scope(nc, "spill") as S:
        stored = S.sem("stored")
        block = S.block()

        @block.sync
        def _(sp):
            for k in range(KC):
                sp.dma_start(xn_dram[k], xn[:, k, :]).then_inc(stored, 16)
            sp.wait_ge(stored, 16 * KC)


def network(nc, w, y_dram):
    with Scope(nc, "net") as S:
        ident, mean_w = constants(nc, S)
        x = S.sb("x", [P, KC, NT])
        l0_conv(nc, w["x"], part(w, "L0_conv_"), x, ident)
        l1_attention(nc, x, part(w, "L1_conv_"), ident)

        a = part(w, "L2_attn_")
        f = part(w, "L2_ffn_")
        xn_dram = nc.dram_tensor("xn_scratch", [KC, P, NT], F32, kind="Internal").ap()
        with Scope(nc, "l2") as T:
            xn = T.sb("xn", [P, KC, NT])
            layer_norm(nc, "ln_l2_attn", x, xn, mean_w, LN_EPS)
            attention(nc, "l2_attn", x, xn, ident, 16, True, 1.0, C ** -0.5, l2_weights(a["w_attn"]),
                      a["w_proj"], a["b_attn"], a["b_proj"])
            layer_norm(nc, "ln_l2_ffn", x, xn, mean_w, LN_EPS, f["norm_w"])
            store_tokens(nc, xn, xn_dram)
        peer_ffn(nc, x, xn_dram, f, ident)

        a = part(w, "L3_attn_")
        with Scope(nc, "l3") as T:
            xn = T.sb("xn", [P, KC, NT])
            layer_norm(nc, "ln_l3_attn", x, xn, mean_w, LN_EPS)
            attention(nc, "l3_attn", x, xn, ident, 8, False, 16 ** -0.5, 1.0, l3_weights(a["Wq"], a["Wk"], a["Wv"]),
                      a["Wout"], None, a["bout"])
            layer_norm(nc, "ln_l3_ffn", x, xn, mean_w, LN_EPS)
            moe_ffn(nc, x, xn, y_dram, part(w, "L3_ffn_"), ident)


def kernel(**inputs):
    import numpy as np
    import concourse.bacc as bacc
    from concourse.bass_utils import run_bass_kernel_spmd

    nc = bacc.Bacc("TRN2", target_bir_lowering=False, num_devices=1)
    arrays, drams = {}, {}
    for name, value in inputs.items():
        value = np.ascontiguousarray(value)
        if name == "x":
            value = value.reshape(B, C, HW)
        arrays[f"in_{name}_dram"] = value
        drams[name] = nc.dram_tensor(f"in_{name}_dram", value.shape, mybir.dt.from_np(value.dtype), kind="ExternalInput").ap()
    out = nc.dram_tensor("out_0_dram", [B, C, HW], F32, kind="ExternalOutput").ap()
    network(nc, drams, out)
    r = run_bass_kernel_spmd(nc, [arrays], core_ids=[0])
    return r.results[0]["out_0_dram"].reshape(B, C, HI, WI)
```

```python
import concourse.bass as bass
from concourse import mybir
from contextlib import ExitStack

F32 = mybir.dt.float32
BF16 = mybir.dt.bfloat16
U32 = mybir.dt.uint32
ALU = mybir.AluOpType
ACT = mybir.ActivationFunctionType
LN_EXP = "natural_log_exp_and_others"
AX_X = mybir.AxisListType.X

LN_EPS, RMS_EPS = 1e-5, 1e-5

P = 128
B, C, HI, WI = 16, 256, 14, 14
HW = HI * WI
NT = B * HW
KC = C // P
TH = HW // 2


def wait(eng, semaphore, value):
    if isinstance(value, int) and value <= 0:
        return
    eng.wait_ge(semaphore, value)


def steps(eng, n, body):
    body(0)
    if n > 1:
        with eng.Fori(1, n) as i:
            body(i)


class Chain:

    def __init__(self, eng, semaphore):
        self.eng, self.sem = eng, semaphore
        self.base, self.k, self.start, self.per = 0, 0, 0, None

    def turn(self, n, units=1):
        if isinstance(n, int) and n == 0:
            self.start, self.k = self.k, 0
            self.base = self.start
        else:
            if self.per is None:
                self.per = self.k
            assert self.k == self.per and self.per % units == 0
            self.base, self.k = self.start + n * (self.per // units), 0

    def step(self, ins):
        ins.then_inc(self.sem, 1)
        self.k += 1

    def wait(self, but=0):
        self.eng.wait_ge(self.sem, self.base + self.k - but)


class Scope:

    def __init__(self, nc, name):
        self.nc, self.name, self.ctx, self.sems = nc, name, ExitStack(), []

    def __enter__(self):
        self.ctx.__enter__()
        return self

    def __exit__(self, *e):
        self.ctx.__exit__(*e)
        if self.sems and e[0] is None:
            self.nc.clear_and_free_semaphores(self.sems)
            self.nc.all_engine_barrier()

    def sb(self, name, shape, dt=F32):
        return self.ctx.enter_context(self.nc.sbuf_tensor(f"{self.name}_{name}", shape, dt))

    def ps(self, name, shape=(P, 512), dt=F32):
        return self.ctx.enter_context(self.nc.psum_tensor(f"{self.name}_{name}_ps", list(shape), dt))

    def sem(self, name):
        s = self.nc.alloc_semaphore(f"{self.name}_{name}")
        self.sems.append(s)
        return s

    def block(self):
        return self.ctx.enter_context(self.nc.Block())


def part(w, prefix):
    return {name[len(prefix):]: dram for name, dram in w.items() if name.startswith(prefix)}


def constants(nc, S):
    ident = S.sb("ident", [P, P])
    mean_w = S.sb("mean_w", [P, P])
    filled, done = S.sem("filled"), S.sem("ident_done")
    with nc.Block() as block:
        @block.gpsimd
        def _(pool):
            nc.gpsimd.memset(ident[:, :], 0.0).then_inc(filled, 1)
            nc.gpsimd.memset(mean_w[:, :], 1.0 / C).then_inc(done, 1)
            pool.wait_ge(filled, 1)
            nc.gpsimd.affine_select(out=ident[:, :], in_=ident[:, :], compare_op=ALU.not_equal, fill=1.0,
                                    base=0, pattern=[[-1, P]], channel_multiplier=1).then_inc(done, 1)
            pool.wait_ge(done, 2)
    return ident, mean_w


def layer_norm(nc, name, x, xn, mean_w, eps, norm_w=None, rms_eps=None, copy_dram=None):
    N = 392
    var_scale = 1.0 if norm_w is None else 1.0 + rms_eps
    with Scope(nc, name) as S:
        eps_col = S.sb("eps", [P, 1])
        xs = [S.sb(f"xs{p}", [P, N]) for p in range(2)]
        sq = [S.sb(f"sq{p}", [P, KC, N]) for p in range(2)]
        ss = [S.sb(f"ss{p}", [P, N]) for p in range(2)]
        lnv = [S.sb(f"lnv{p}", [P, N]) for p in range(2)]
        rs = [S.sb(f"rs{p}", [P, N]) for p in range(2)]
        mean_ps = [S.ps(f"mean{p}") for p in range(2)]
        var_ps = [S.ps(f"var{p}") for p in range(2)]
        summed, mean_ready, centred, squared = S.sem("summed"), S.sem("mean_ready"), S.sem("centred"), S.sem("squared")
        sq_summed = S.sem("sq_summed")
        var_ready, ln_ready, rs_ready, normed = S.sem("var_ready"), S.sem("ln_ready"), S.sem("rs_ready"), S.sem("normed")
        stored, nw_loaded, consts = S.sem("stored"), S.sem("nw_loaded"), S.sem("consts")
        if norm_w is not None:
            nw = S.sb("nw", [P, KC])
        n_turns = NT // N // 2
        block = S.block()

        def tok(t, n):
            return t[:, :, bass.ds(n * N, N)] if not isinstance(n, int) else t[:, :, n * N:(n + 1) * N]

        @block.sync
        def _(sp):
            if norm_w is not None:
                sp.dma_start(nw[:, :], norm_w.rearrange("(k p) -> p k", p=P),
                             allow_slow_non_contiguous=True).then_inc(nw_loaded, 16)
            if copy_dram is not None:
                def body(n):
                    sp.wait_ge(normed, n + 1)
                    sp.dma_start(copy_dram[:, :, bass.ds(n * N, N)].rearrange("k p t -> p k t"), tok(xn, n)).then_inc(stored, 16)
                steps(sp, NT // N, body)
                sp.wait_ge(stored, 16 * (NT // N))

        @block.tensor
        def _(pe):
            def mean(n, p):
                pe.wait_ge(summed, n + 1)
                wait(pe, centred, n - 1)
                nc.tensor.matmul(mean_ps[p][:, 0:N], mean_w[:, :], xs[p][:, :], start=True, stop=True).then_inc(mean_ready, 1)

            def variance(n, p):
                pe.wait_ge(sq_summed, n + 1)
                wait(pe, ln_ready, n - 1)
                nc.tensor.matmul(var_ps[p][:, 0:N], mean_w[:, :], ss[p][:, :], start=True, stop=True).then_inc(var_ready, 1)

            for p in range(2):
                mean(p, p)

            def body(i):
                for p in range(2):
                    variance(2 * i + p, p)
                    mean(2 * i + p + 2, p)
            steps(pe, n_turns - 1, body)
            for p in range(2):
                variance(NT // N - 2 + p, p)

        @block.scalar
        def _(act):
            act.preload_act_table_set(LN_EXP)

            def body(i):
                for p in range(2):
                    n = 2 * i + p
                    act.wait_ge(centred, n + 1)
                    wait(act, sq_summed, n - 1)
                    nc.scalar.activation(sq[p][:, :, :], tok(xn, n), ACT.Square).then_inc(squared, 1)
                for p in range(2):
                    n = 2 * i + p
                    act.wait_ge(consts, 1)
                    act.wait_ge(var_ready, n + 1)
                    nc.scalar.activation(lnv[p][:, :], var_ps[p][:, 0:N], ACT.Ln, scale=var_scale,
                                         bias=eps_col[:, 0:1]).then_inc(ln_ready, 1)
                    act.wait_ge(ln_ready, n + 1)
                    wait(act, normed, n - 1)
                    nc.scalar.activation(rs[p][:, :], lnv[p][:, :], ACT.Exp, scale=-0.5).then_inc(rs_ready, 1)
            steps(act, n_turns, body)

        @block.vector
        def _(dve):
            nc.vector.memset(eps_col[:, :], eps if norm_w is None else eps * rms_eps).then_inc(consts, 1)
            if norm_w is not None:
                dve.wait_ge(nw_loaded, 16)

            def add_halves(n, p):
                wait(dve, mean_ready, n - 1)
                xc = tok(x, n)
                nc.vector.tensor_tensor(xs[p][:, :], xc[:, 0, :], xc[:, 1, :], ALU.add).then_inc(summed, 1)

            def centre(n, p):
                dve.wait_ge(mean_ready, n + 1)
                nc.vector.tensor_tensor(tok(xn, n), tok(x, n), mean_ps[p][:, 0:N].unsqueeze(1).broadcast_to([P, KC, N]),
                                        ALU.subtract).then_inc(centred, 1)

            def add_squares(n, p):
                dve.wait_ge(squared, n + 1)
                wait(dve, var_ready, n - 1)
                nc.vector.tensor_tensor(ss[p][:, :], sq[p][:, 0, :], sq[p][:, 1, :], ALU.add).then_inc(sq_summed, 1)

            def scale(n, p):
                dve.wait_ge(rs_ready, n + 1)
                for k in range(KC):
                    xk = tok(xn, n)[:, k, :]
                    if norm_w is None:
                        ins = nc.vector.tensor_tensor(xk, xk, rs[p][:, :], ALU.mult)
                    else:
                        ins = nc.vector.scalar_tensor_tensor(xk, xk, nw[:, k:k + 1], rs[p][:, :], ALU.mult, ALU.mult)
                ins.then_inc(normed, 1)

            for p in range(2):
                add_halves(p, p)
            for p in range(2):
                centre(p, p)

            def body(i):
                for p in range(2):
                    n = 2 * i + p
                    add_halves(n + 2, p)
                    add_squares(n, p)
                for p in range(2):
                    n = 2 * i + p
                    centre(n + 2, p)
                    scale(n, p)
            steps(dve, n_turns - 1, body)
            for p in range(2):
                add_squares(NT // N - 2 + p, p)
            for p in range(2):
                scale(NT // N - 2 + p, p)


def l0_conv(nc, x_dram, w, x, ident):
    MID = 64
    IPC = 2
    NCH = B // IPC
    N = IPC * HW
    PW = WI + 2
    EPS = 1e-5
    N_COL = 16
    with Scope(nc, "l0") as S:
        w1n, w3n = S.sb("w1n", [MID, C]), S.sb("w3n", [P, KC, MID])
        w2n = S.sb("w2n", [MID, 9 * MID])
        w2r = S.sb("w2r", [MID, 9, MID])
        w1t = S.sb("w1t", [P, KC, P])
        w2t = S.sb("w2t", [P, 3, P])
        w2s = S.sb("w2s", [MID, 3, P])
        w3t = S.sb("w3t", [MID, C])
        bias1, gam1, bet1 = S.sb("b1", [P, 1]), S.sb("g1", [P, 1]), S.sb("be1", [P, 1])
        bias2, gam2, bet2 = S.sb("b2", [P, 1]), S.sb("g2", [P, 1]), S.sb("be2", [P, 1])
        bias3, gam3, bet3 = S.sb("b3", [P, KC]), S.sb("g3", [P, KC]), S.sb("be3", [P, KC])
        rsc = S.sb("rsc", [P, 5])
        eps_col = S.sb("eps", [P, 1])
        y1 = S.sb("y1", [P, NT])
        ypad = S.sb("ypad", [P, B, PW, PW])
        y2 = S.sb("y2", [MID, NT])
        y3 = S.sb("y3", [P, KC, NT])
        stats = S.sb("stats", [P, 4, NCH, 6])
        mv = S.sb("mv", [P, 4, 2])
        lnv, rstd = S.sb("lnv", [P, 4]), S.sb("rstd", [P, 4])
        scale, shift, mscale = S.sb("scale", [P, 4]), S.sb("shift", [P, 4]), S.sb("mscale", [P, 4])
        scale3, shift3 = S.sb("scale3", [P, KC]), S.sb("shift3", [P, KC])
        wps = [S.ps(f"w{p}") for p in range(2)]
        cps = [S.ps(f"c{p}") for p in range(4)]
        col_in = S.sem("col_in")
        w_in, x_in = S.sem("w_in"), [S.sem(f"x_in{c}") for c in range(NCH)]
        w_turned, w_ready, cleared = S.sem("w_turned"), S.sem("w_ready"), S.sem("cleared")
        conv1_done, conv2_done, conv3_done = S.sem("conv1_done"), S.sem("conv2_done"), S.sem("conv3_done")
        y1_ready, y2_ready, y3_ready = S.sem("y1_ready"), S.sem("y2_ready"), S.sem("y3_ready")
        var_ready, ln_ready, rstd_ready, aff_ready = S.sem("var_ready"), S.sem("ln_ready"), S.sem("rstd_ready"), S.sem("aff_ready")
        padded, act2_done, sum_done, res_done = S.sem("padded"), S.sem("act2_done"), S.sem("sum_done"), S.sem("res_done")
        soft_in, w2_ordered, dve_link = S.sem("soft_in"), S.sem("w2_ordered"), S.sem("dve_link")
        block = S.block()
        HALF = [slice(0, MID), slice(MID, P)]

        def chunk(t, c):
            return t[:, bass.ds(c * N, N)]

        @block.sync
        def _(sp):
            sp.dma_start(w1n[:, :], w["w1"].rearrange("o c h w -> o (c h w)")).then_inc(w_in, 16)
            sp.dma_start(w2n[:, :], w["w2"].rearrange("o i h w -> o (i h w)")).then_inc(w_in, 16)
            sp.dma_start(w3n[:, :, :], w["w3"].rearrange("(k o) c h w -> o k (c h w)", k=KC)).then_inc(w_in, 16)
            for c in range(NCH):
                for k in range(KC):
                    sp.dma_start(x[:, k, c * N:(c + 1) * N].rearrange("p (b t) -> p b t", b=IPC),
                                 x_dram[c * IPC:(c + 1) * IPC, k * P:(k + 1) * P].rearrange("b p t -> p b t")).then_inc(x_in[c], 16)

        @block.gpsimd
        def _(pool):
            def column(dst, src):
                pool.dma_start(dst, src.rearrange("(p a) -> p a", a=1)).then_inc(col_in, 16)
            for dst, v in ((bias1, "b1"), (gam1, "g1"), (bet1, "be1")):
                for h in HALF:
                    column(dst[h, 0:1], w[v])
            for dst, v in ((bias2, "b2"), (gam2, "g2"), (bet2, "be2")):
                column(dst[0:MID, 0:1], w[v])
            for dst, v in ((bias3, "b3"), (gam3, "g3"), (bet3, "be3")):
                for k in range(KC):
                    column(dst[:, k:k + 1], w[v][k * P:(k + 1) * P])
            pool.dma_start(rsc[:, 0:1], w["residual_scale"].partition_broadcast(P)).then_inc(col_in, 16)
            nc.gpsimd.memset(eps_col[:, :], EPS).then_inc(cleared, 1)
            nc.gpsimd.memset(ypad[:, :, :, :], 0.0).then_inc(cleared, 1)

        @block.tensor
        def _(pe):
            pe.wait_ge(w_in, 16 * 3)
            for k in range(KC):
                for h in range(2):
                    nc.tensor.transpose(wps[0][:, (2 * k + h) * MID:(2 * k + h + 1) * MID], w1n[:, k * P:(k + 1) * P],
                                        ident[0:MID, 0:MID])
            for k in range(KC):
                mm = nc.tensor.transpose(wps[0][0:MID, 256 + k * P:256 + (k + 1) * P], w3n[:, k, :], ident[:, :])
            mm.then_inc(w_turned, 1)
            pe.wait_ge(w2_ordered, 1)
            for ky in range(3):
                nc.tensor.transpose(wps[1][:, ky * MID:(ky + 1) * MID], w2r[:, 3 * ky:3 * ky + 2, :].rearrange("o t i -> o (t i)"), ident[0:MID, 0:MID])
            for ky in range(3):
                mm = nc.tensor.transpose(wps[1][0:MID, (3 + ky) * MID:(4 + ky) * MID], w2r[:, 3 * ky + 2, :], ident[0:MID, 0:MID])
            mm.then_inc(w_turned, 1)
            pe.wait_ge(w_ready, 1)
            for c in range(NCH):
                pe.wait_ge(x_in[c], 32)
                wait(pe, y1_ready, c - 3)
                for k in range(KC):
                    mm = nc.tensor.matmul(cps[c % 4][:, 0:N], w1t[:, k, :], x[:, k, c * N:(c + 1) * N],
                                          start=(k == 0), stop=(k == KC - 1))
                mm.then_inc(conv1_done, 1)
            pe.wait_ge(w_ready, 2)
            pe.wait_ge(y1_ready, NCH)

            def conv2(i):
                for p in range(2):
                    c = 2 * i + p
                    pe.wait_ge(padded, c + 1)
                    wait(pe, y2_ready, c - 1)
                    src = ypad[:, bass.ds(c * IPC, IPC), :, :]
                    out = cps[p][:, 0:N].rearrange("o (b h w) -> o b h w", b=IPC, h=HI)
                    for ky in range(3):
                        nc.tensor.matmul(out, w2t[:, ky, :], src[:, :, ky:ky + HI, 0:WI], start=(ky == 0), stop=False)
                        mm = nc.tensor.matmul(out, w2s[:, ky, :], src[0:MID, :, ky:ky + HI, 2:2 + WI], start=False, stop=(ky == 2))
                    mm.then_inc(conv2_done, 1)
            steps(pe, NCH // 2, conv2)
            pe.wait_ge(y2_ready, NCH)

            def conv3(i):
                for p in range(2):
                    c = 2 * i + p
                    pe.wait_ge(act2_done, c + 1)
                    wait(pe, y3_ready, 2 * c - 2)
                    for k in range(KC):
                        nc.tensor.matmul(cps[2 * p + k][:, 0:N], w3t[:, k * P:(k + 1) * P], chunk(y2, c),
                                         start=True, stop=True).then_inc(conv3_done, 1)
            steps(pe, NCH // 2, conv3)

        @block.scalar
        def _(act):
            act.preload_act_table_set(LN_EXP)
            act.wait_ge(col_in, 16 * N_COL)
            act.wait_ge(cleared, 2)
            nc.scalar.activation(rsc[:, 1:2], rsc[:, 0:1], ACT.Abs).then_inc(soft_in, 1)
            act.wait_ge(soft_in, 1)
            nc.scalar.activation(rsc[:, 2:3], rsc[:, 1:2], ACT.Exp, scale=-1.0).then_inc(soft_in, 1)
            act.wait_ge(soft_in, 2)
            nc.scalar.activation(rsc[:, 3:4], rsc[:, 2:3], ACT.Ln, bias=1.0).then_inc(soft_in, 1)
            for c in range(NCH):
                act.wait_ge(conv1_done, c + 1)
                nc.scalar.activation(y1[:, c * N:(c + 1) * N], cps[c % 4][:, 0:N], ACT.Identity, bias=bias1[:, 0:1]).then_inc(y1_ready, 1)

            def rstd_of(n, s, h):
                act.wait_ge(var_ready, n + 1)
                nc.scalar.activation(lnv[0:h, s], mv[0:h, s, 1], ACT.Ln, bias=eps_col[0:h, 0:1]).then_inc(ln_ready, 1)
                act.wait_ge(ln_ready, n + 1)
                nc.scalar.activation(rstd[0:h, s], lnv[0:h, s], ACT.Exp, scale=-0.5).then_inc(rstd_ready, 1)
                act.wait_ge(aff_ready, n + 1)

            rstd_of(0, slice(0, 1), P)

            def pad(c):
                for h, off in ((0, 1), (1, 0)):
                    dst = ypad[HALF[h], bass.ds(c * IPC, IPC), 1:1 + HI, off:off + WI]
                    ins = nc.scalar.activation(dst, chunk(y1, c)[HALF[h], :].rearrange("p (b h w) -> p b h w", b=IPC, h=HI),
                                               ACT.Relu, scale=scale[HALF[h], 0:1], bias=shift[HALF[h], 0:1])
                ins.then_inc(padded, 1)
            steps(act, NCH, pad)

            def out2(i):
                for p in range(2):
                    c = 2 * i + p
                    act.wait_ge(conv2_done, c + 1)
                    nc.scalar.activation(chunk(y2, c), cps[p][0:MID, 0:N], ACT.Identity, bias=bias2[0:MID, 0:1]).then_inc(y2_ready, 1)
            steps(act, NCH // 2, out2)
            rstd_of(1, slice(1, 2), MID)

            def relu2(c):
                nc.scalar.activation(chunk(y2, c), chunk(y2, c), ACT.Relu, scale=scale[0:MID, 1:2], bias=shift[0:MID, 1:2]).then_inc(act2_done, 1)
            steps(act, NCH, relu2)

            def out3(i):
                for p in range(2):
                    c = 2 * i + p
                    for k in range(KC):
                        act.wait_ge(conv3_done, 2 * c + k + 1)
                        nc.scalar.activation(chunk(y3[:, k, :], c), cps[2 * p + k][:, 0:N], ACT.Identity, bias=bias3[:, k:k + 1]).then_inc(y3_ready, 1)
            steps(act, NCH // 2, out3)
            rstd_of(2, slice(2, 4), P)

            def relu3(c):
                act.wait_ge(sum_done, c + 1)
                for k in range(KC):
                    nc.scalar.activation(chunk(x[:, k, :], c), chunk(y3[:, k, :], c), ACT.Relu, bias=shift3[:, k:k + 1]).then_inc(res_done, 1)
            steps(act, NCH, relu3)

        @block.vector
        def _(dve):
            links = [0]

            def link(ins):
                links[0] += 1
                ins.then_inc(dve_link, 1)
                dve.wait_ge(dve_link, links[0])

            dve.wait_ge(w_in, 16 * 3)
            dve.wait_ge(col_in, 16 * N_COL)
            nc.vector.tensor_copy(w2r[:, :, :], w2n[:, :].rearrange("o (i t) -> o t i", t=9)).then_inc(w2_ordered, 1)
            dve.wait_ge(w_turned, 1)
            nc.vector.tensor_copy(w1t[:, :, :], wps[0][:, 0:256].rearrange("p (k m) -> p k m", k=KC))
            nc.vector.tensor_copy(w3t[:, :], wps[0][0:MID, 256:512]).then_inc(w_ready, 1)
            dve.wait_ge(w_turned, 2)
            for h in HALF:
                nc.vector.tensor_copy(w2t[:, :, h], wps[1][:, 0:3 * MID].rearrange("p (y m) -> p y m", y=3))
                ins = nc.vector.tensor_copy(w2s[:, :, h], wps[1][0:MID, 3 * MID:6 * MID].rearrange("p (y m) -> p y m", y=3))
            ins.then_inc(w_ready, 1)

            def affine(n, s, h, g, b):
                dve.wait_ge(rstd_ready, n + 1)
                link(nc.vector.tensor_tensor(scale[0:h, s], g[0:h, :], rstd[0:h, s], ALU.mult))
                link(nc.vector.tensor_tensor(mscale[0:h, s], mv[0:h, s, 0], scale[0:h, s], ALU.mult))
                return nc.vector.tensor_tensor(shift[0:h, s], b[0:h, :], mscale[0:h, s], ALU.subtract)

            for c in range(NCH):
                dve.wait_ge(y1_ready, c + 1)
                ins = nc.vector.bn_stats(stats[:, 0, c, :], y1[:, c * N:(c + 1) * N])
            link(ins)
            nc.vector.bn_aggr(mv[:, 0, :], stats[:, 0, :, :]).then_inc(var_ready, 1)
            affine(0, slice(0, 1), P, gam1, bet1).then_inc(aff_ready, 1)
            for c in range(NCH):
                dve.wait_ge(y2_ready, c + 1)
                ins = nc.vector.bn_stats(stats[0:MID, 1, c, :], y2[:, c * N:(c + 1) * N])
            link(ins)
            nc.vector.bn_aggr(mv[0:MID, 1, :], stats[0:MID, 1, :, :]).then_inc(var_ready, 1)
            affine(1, slice(1, 2), MID, gam2, bet2).then_inc(aff_ready, 1)
            for c in range(NCH):
                for k in range(KC):
                    dve.wait_ge(y3_ready, 2 * c + k + 1)
                    ins = nc.vector.bn_stats(stats[:, 2 + k, c, :], y3[:, k, c * N:(c + 1) * N])
            link(ins)
            for k in range(KC):
                ins = nc.vector.bn_aggr(mv[:, 2 + k, :], stats[:, 2 + k, :, :])
            ins.then_inc(var_ready, 1)
            link(affine(2, slice(2, 4), P, gam3, bet3))
            dve.wait_ge(soft_in, 3)
            link(nc.vector.scalar_tensor_tensor(rsc[:, 4:5], rsc[:, 0:1], 0.0, rsc[:, 3:4], ALU.max, ALU.add))
            nc.vector.tensor_scalar(scale3[:, :], scale[:, 2:4], rsc[:, 4:5], None, ALU.mult)
            nc.vector.tensor_scalar(shift3[:, :], shift[:, 2:4], rsc[:, 4:5], None, ALU.mult).then_inc(aff_ready, 1)
            dve.wait_ge(aff_ready, 3)

            def residual(c):
                for k in range(KC):
                    ins = nc.vector.scalar_tensor_tensor(chunk(y3[:, k, :], c), chunk(y3[:, k, :], c), scale3[:, k:k + 1],
                                                         chunk(x[:, k, :], c), ALU.mult, ALU.add)
                ins.then_inc(sum_done, 1)
            steps(dve, NCH, residual)


def l1_attention(nc, x, w, ident):
    MID = 64
    EPS = 1e-5
    SCALE = MID ** -0.5
    with Scope(nc, "l1") as S:
        wn = S.sb("wn", [MID, 3, C])
        wvn = S.sb("wvn", [P, KC, MID])
        wt = S.sb("wt", [P, KC, 3, MID])
        wvt = S.sb("wvt", [MID, C])
        col = S.sb("col", [MID, 2, 5])
        bh = S.sb("bh", [MID, 1])
        bv = S.sb("bv", [P, KC])
        eps_col = S.sb("eps", [MID, 1])
        lnv, rstd = S.sb("lnv", [MID, 2]), S.sb("rstd", [MID, 2])
        scale, shift, tmp = S.sb("scale", [MID, 2]), S.sb("shift", [MID, 2]), S.sb("tmp", [MID, 2])
        xi = [S.sb(f"xi{p}", [P, KC, HW]) for p in range(2)]
        fg = [S.sb(f"fg{p}", [MID, 2, HW]) for p in range(2)]
        ht = [S.sb(f"ht{p}", [TH, 2, MID]) for p in range(2)]
        nm = [S.sb(f"nm{p}", [TH, 2]) for p in range(2)]
        ex = [S.sb(f"ex{p}", [TH, 2, HW]) for p in range(2)]
        total = [S.sb(f"total{p}", [TH, 2]) for p in range(2)]
        inv = [S.sb(f"inv{p}", [TH, 2]) for p in range(2)]
        pn = [S.sb(f"pn{p}", [TH, 2, HW]) for p in range(2)]
        pt = [S.sb(f"pt{p}", [TH, 2, HW]) for p in range(2)]
        z = [S.sb(f"z{p}", [MID, HW]) for p in range(2)]
        a_ps = [S.ps(f"a{p}") for p in range(2)]
        s_ps = [S.ps(f"s{p}") for p in range(2)]
        h_ps, pt_ps = S.ps("h"), [S.ps(f"pt{p}") for p in range(2)]
        z_ps = S.ps("z")
        w_in, consts, w_turned, w_ready = S.sem("w_in"), S.sem("consts"), S.sem("w_turned"), S.sem("w_ready")
        ln_ready, rstd_ready, aff_ready, link_s = S.sem("ln_ready"), S.sem("rstd_ready"), S.sem("aff_ready"), S.sem("link")
        xi_in = [S.sem(f"xi_in{p}") for p in range(2)]
        fg_done, h_done, fg_ready, h_ready = S.sem("fg_done"), S.sem("h_done"), S.sem("fg_ready"), S.sem("h_ready")
        s_done, max_done, exp_done, inv_done, pn_ready = S.sem("s_done"), S.sem("max_done"), S.sem("exp_done"), S.sem("inv_done"), S.sem("pn_ready")
        t_done, pt_ready, z_done, z_ready, o_done, x_done = S.sem("t_done"), S.sem("pt_ready"), S.sem("z_done"), S.sem("z_ready"), S.sem("o_done"), S.sem("x_done")
        N_W = 4 + 10 + 2
        block = S.block()

        def image(t, n):
            return t[:, :, bass.ds(n * HW, HW)]

        def pairs(eng, body):
            def both(i):
                for p in range(2):
                    body(2 * i + p, p)
            steps(eng, B // 2, both)

        def loop(eng, both):
            both(0, False)
            with eng.Fori(1, B // 2 - 1) as i:
                both(i, False)
            both(B // 2 - 1, True)

        @block.sync
        def _(sp):
            for j, v in enumerate(("Wf", "Wg", "Wh")):
                sp.dma_start(wn[:, j, :], w[v]).then_inc(w_in, 16)
            sp.dma_start(wvn[:, :, :], w["Wv"].rearrange("(k p) c -> p k c", p=P)).then_inc(w_in, 16)
            for j, s in enumerate("fg"):
                for n, v in enumerate(("b", "g", "bt", "m", "v")):
                    sp.dma_start(col[:, j, n:n + 1], w[v + s].rearrange("(p a) -> p a", a=1)).then_inc(w_in, 16)
            sp.dma_start(bh[:, :], w["bh"].rearrange("(p a) -> p a", a=1)).then_inc(w_in, 16)
            sp.dma_start(bv[:, :], w["bv"].rearrange("(k p) -> p k", p=P), allow_slow_non_contiguous=True).then_inc(w_in, 16)

            def body(n, p):
                wait(sp, h_done, n - 1)
                sp.dma_start(xi[p][:, :, :], image(x, n)).then_inc(xi_in[p], 16)
            pairs(sp, body)

        @block.gpsimd
        def _(pool):
            nc.gpsimd.memset(eps_col[:, :], EPS).then_inc(consts, 1)

        @block.tensor
        def _(pe):
            pe.wait_ge(w_in, 16 * N_W)
            for j in range(3):
                for k in range(KC):
                    mm = nc.tensor.transpose(a_ps[0][:, (3 * k + j) * MID:(3 * k + j + 1) * MID], wn[:, j, k * P:(k + 1) * P], ident[0:MID, 0:MID])
            for k in range(KC):
                mm = nc.tensor.transpose(a_ps[1][0:MID, k * P:(k + 1) * P], wvn[:, k, :], ident[:, :])
            mm.then_inc(w_turned, 1)
            pe.wait_ge(w_ready, 1)

            def project_in(n, p):
                pe.wait_ge(xi_in[p], 8 * (n - p) + 16)
                wait(pe, fg_ready, n - 1)
                for j in range(2):
                    for k in range(KC):
                        mm = nc.tensor.matmul(a_ps[p][0:MID, j * HW:(j + 1) * HW], wt[:, k, j, :], xi[p][:, k, :],
                                              start=(k == 0), stop=(k == KC - 1))
                mm.then_inc(fg_done, 1)
                wait(pe, h_ready, n - p)
                for t in range(2):
                    for k in range(KC):
                        mm = nc.tensor.matmul(h_ps[0:TH, (2 * p + t) * MID:(2 * p + t + 1) * MID], xi[p][:, k, t * TH:(t + 1) * TH], wt[:, k, 2, :],
                                              start=(k == 0), stop=(k == KC - 1))
                mm.then_inc(h_done, 1)

            def scores(n, p):
                pe.wait_ge(fg_ready, n + 1)
                wait(pe, x_done, n - 1)
                for t in range(2):
                    mm = nc.tensor.matmul(s_ps[p][0:TH, t * HW:(t + 1) * HW], fg[p][:, 0, t * TH:(t + 1) * TH], fg[p][:, 1, :],
                                          start=True, stop=True)
                mm.then_inc(s_done, 1)

            def turn(n, p):
                pe.wait_ge(pn_ready, n + 1)
                wait(pe, pt_ready, n - 1)
                for t in range(2):
                    for u in range(2):
                        mm = nc.tensor.transpose(pt_ps[p][0:TH, u * HW + t * TH:u * HW + (t + 1) * TH], pn[p][:, t, u * TH:(u + 1) * TH],
                                                 ident[0:TH, 0:TH])
                mm.then_inc(t_done, 1)

            def mix(n, p):
                pe.wait_ge(pt_ready, n + 1)
                pe.wait_ge(h_ready, n + 1)
                wait(pe, z_ready, n)
                for u in range(2):
                    mm = nc.tensor.matmul(z_ps[0:MID, 0:HW], ht[p][:, u, :], pt[p][:, u, :], start=(u == 0), stop=(u == 1))
                mm.then_inc(z_done, 1)

            def project_out(n, p):
                pe.wait_ge(z_ready, n + 1)
                for k in range(KC):
                    mm = nc.tensor.matmul(s_ps[p][:, k * HW:(k + 1) * HW], wvt[:, k * P:(k + 1) * P], z[p][:, :], start=True, stop=True)
                mm.then_inc(o_done, 1)

            def both(i, last):
                for stage in (scores, project_in, turn, mix, project_out):
                    for p in range(2):
                        if stage is not project_in:
                            stage(2 * i + p, p)
                        elif not last:
                            stage(2 * i + 2 + p, p)
            for p in range(2):
                project_in(p, p)
            loop(pe, both)

        @block.scalar
        def _(act):
            act.preload_act_table_set(LN_EXP)
            act.wait_ge(w_in, 16 * N_W)
            act.wait_ge(consts, 1)
            nc.scalar.activation(lnv[:, :], col[:, :, 4], ACT.Ln, bias=eps_col[:, 0:1]).then_inc(ln_ready, 1)
            act.wait_ge(ln_ready, 1)
            nc.scalar.activation(rstd[:, :], lnv[:, :], ACT.Exp, scale=-0.5).then_inc(rstd_ready, 1)
            act.wait_ge(aff_ready, 1)

            def inputs_out(n, p):
                act.wait_ge(fg_done, n + 1)
                wait(act, s_done, n - 1)
                for j in range(2):
                    ins = nc.scalar.activation(fg[p][:, j, :], a_ps[p][0:MID, j * HW:(j + 1) * HW], ACT.Relu,
                                               scale=scale[:, j:j + 1], bias=shift[:, j:j + 1])
                ins.then_inc(fg_ready, 1)

            def mixed_out(n, p):
                act.wait_ge(h_done, n - p + 2)
                wait(act, z_done, n - 1)
                nc.scalar.activation(ht[p][:, :, :], h_ps[0:TH, 2 * p * MID:(2 * p + 2) * MID].rearrange("q (t m) -> q t m", t=2),
                                     ACT.Copy).then_inc(h_ready, 1)

            for stage in (inputs_out, mixed_out):
                for p in range(2):
                    stage(p, p)

            def both(i, last):
                for p in range(2):
                    n = 2 * i + p
                    act.wait_ge(max_done, n + 1)
                    wait(act, pn_ready, n - 1)
                    for t in range(2):
                        ins = nc.scalar.activation(ex[p][:, t, :], s_ps[p][0:TH, t * HW:(t + 1) * HW], ACT.Exp, scale=SCALE,
                                                   bias=nm[p][:, t:t + 1], accum_out=total[p][:, t:t + 1])
                    ins.then_inc(exp_done, 1)
                if not last:
                    for p in range(2):
                        inputs_out(2 * i + 2 + p, p)
                for p in range(2):
                    n = 2 * i + p
                    act.wait_ge(t_done, n + 1)
                    wait(act, z_done, n - 1)
                    nc.scalar.activation(pt[p][:, :, :], pt_ps[p][0:TH, 0:2 * HW].rearrange("p (u t) -> p u t", u=2), ACT.Copy).then_inc(pt_ready, 1)
                for p in range(2):
                    n = 2 * i + p
                    act.wait_ge(z_done, n + 1)
                    wait(act, o_done, n - 1)
                    nc.scalar.activation(z[p][:, :], z_ps[0:MID, 0:HW], ACT.Identity, bias=bh[:, 0:1]).then_inc(z_ready, 1)
                if not last:
                    for p in range(2):
                        mixed_out(2 * i + 2 + p, p)
            loop(act, both)

        @block.vector
        def _(dve):
            dve.wait_ge(w_turned, 1)
            nc.vector.tensor_copy(wt[:, :, :, :], a_ps[0][:, 0:KC * 3 * MID].rearrange("p (k j m) -> p k j m", k=KC, j=3))
            nc.vector.tensor_copy(wvt[:, :], a_ps[1][0:MID, 0:C]).then_inc(w_ready, 1)
            dve.wait_ge(w_in, 16 * N_W)
            dve.wait_ge(rstd_ready, 1)
            nc.vector.tensor_tensor(scale[:, :], col[:, :, 1], rstd[:, :], ALU.mult).then_inc(link_s, 1)
            nc.vector.tensor_tensor(tmp[:, :], col[:, :, 0], col[:, :, 3], ALU.subtract).then_inc(link_s, 1)
            dve.wait_ge(link_s, 2)
            nc.vector.tensor_tensor(tmp[:, :], tmp[:, :], scale[:, :], ALU.mult).then_inc(link_s, 1)
            dve.wait_ge(link_s, 3)
            nc.vector.tensor_tensor(shift[:, :], tmp[:, :], col[:, :, 2], ALU.add).then_inc(aff_ready, 1)

            def both(i):
                for p in range(2):
                    n = 2 * i + p
                    dve.wait_ge(s_done, n + 1)
                    nc.vector.tensor_reduce(inv[p][:, :], s_ps[p][0:TH, 0:2 * HW].rearrange("p (t j) -> p t j", t=2), AX_X, ALU.max).then_inc(link_s, 1)
                    dve.wait_ge(link_s, n + 4)
                    nc.vector.tensor_scalar(nm[p][:, :], inv[p][:, :], -SCALE, None, ALU.mult).then_inc(max_done, 1)
                for p in range(2):
                    n = 2 * i + p
                    dve.wait_ge(exp_done, n + 1)
                    nc.vector.reciprocal(inv[p][:, :], total[p][:, :]).then_inc(inv_done, 1)
                    dve.wait_ge(inv_done, n + 1)
                    wait(dve, t_done, n - 1)
                    for t in range(2):
                        ins = nc.vector.tensor_scalar(pn[p][:, t, :], ex[p][:, t, :], inv[p][:, t:t + 1], None, ALU.mult)
                    ins.then_inc(pn_ready, 1)
                for p in range(2):
                    n = 2 * i + p
                    dve.wait_ge(o_done, n + 1)
                    for k in range(KC):
                        ins = nc.vector.scalar_tensor_tensor(image(x, n)[:, k, :], s_ps[p][:, k * HW:(k + 1) * HW], bv[:, k:k + 1],
                                                             image(x, n)[:, k, :], ALU.add, ALU.add)
                    ins.then_inc(x_done, 1)
            steps(dve, B // 2, both)


def attention(nc, name, x, xn, ident, heads, causal, q_scale, out_scale, load_w, w_out, b_qkv, b_out):
    D = 16
    NPIECE = 3
    PAIRS = [(0, 0), (0, 1), (1, 0), (1, 1), (0, 2), (2, 0)]
    KS = len(PAIRS) * D
    HR = 32
    G = heads * HR // P
    OB = G // 2
    INNER = heads * D
    MT = INNER // P
    GH = P // D
    SW = 3 * TH if causal else 4 * TH
    blocks = [(0, 0, 0), (1, 0, 1), (1, 1, 2)] if causal else [(0, 0, 0), (0, 1, 1), (1, 0, 2), (1, 1, 3)]
    rows = [(0, 0, 1), (1, 1, 2)] if causal else [(0, 0, 2), (1, 2, 2)]
    with Scope(nc, name) as S:
        w_qkv = S.sb("w_qkv", [P, KC, 3 * INNER])
        w_o = S.sb("w_o", [P, G, C])
        pick_sum = S.sb("pick_sum", [P, P])
        bq, bk = S.sb("bq", [P, MT]), S.sb("bk", [P, MT])
        bv = S.sb("bv", [1, INNER])
        bo = S.sb("bo", [P, KC])
        ones = S.sb("ones", [1, TH])
        pieces_dram = [nc.dram_tensor(f"{name}_pieces_{s}_dram", [NPIECE, P, MT, HW], BF16, kind="Internal").ap() for s in "qk"]
        ident_b, mask_b = S.sb("ident_b", [TH, TH], BF16), S.sb("mask_b", [TH, 2, TH], BF16)
        xi = S.sb("xi", [P, KC, HW])
        full = [S.sb(f"full_{s}", [P, MT, HW]) for s in "qk"]
        rest = S.sb("rest", [P, MT, HW])
        pieces = [S.sb(f"pieces_{s}", [P, NPIECE, MT, HW], BF16) for s in "qk"]
        stacks = [[S.sb(f"stack_{s}{p}", [KS, heads, HW], BF16) for s in "qk"] for p in range(2)]
        va = [S.sb(f"va{p}", [TH, 2, heads, HR]) for p in range(2)]
        ex = [S.sb(f"ex{p}", [TH, SW]) for p in range(4)]
        pt = [S.sb(f"pt{p}", [TH, SW]) for p in range(4)]
        mn = S.sb("mn", [TH, heads, 2])
        o = S.sb("o", [P, OB, 2 * HW])
        lns, rinv = S.sb("lns", [P, OB, 2 * HW]), S.sb("rinv", [P, OB, 2 * HW])
        io_ps = S.ps("io")
        pt_ps = [S.ps(f"pt{p}") for p in range(2)]
        s_ps = [S.ps(f"s{p}") for p in range(3)]
        o_ps = [S.ps(f"o{b}") for b in range(2)]
        w_in, c_in, consts, masked = S.sem("w_in"), S.sem("c_in"), S.sem("consts"), S.sem("masked")
        xi_in, q_done, k_done, v_done = S.sem("xi_in"), S.sem("q_done"), S.sem("k_done"), S.sem("v_done")
        full_ready, own, v_ready = [S.sem("q_full"), S.sem("k_full")], S.sem("own"), S.sem("v_ready")
        cut, dumped, stacked = ([S.sem(f"{s}_{what}") for s in "qk"] for what in ("cut", "dumped", "stacked"))
        s_done, min_done, exp_done, t_done = S.sem("s_done"), S.sem("min_done"), S.sem("exp_done"), S.sem("t_done")
        pt_ready = [S.sem(f"pt_ready{p}") for p in range(2)]
        pv_done, o_out, o_ready = S.sem("pv_done"), S.sem("o_out"), S.sem("o_ready")
        spread, ln_done, rinv_ready, w_cleared = S.sem("spread"), S.sem("ln_done"), S.sem("rinv_ready"), S.sem("w_cleared")
        bias_scaled = S.sem("bias_scaled")
        proj_done, x_done = S.sem("proj_done"), S.sem("x_done")
        n_w = load_w(None, None, None)
        n_c = (3 if b_qkv is not None else 0) + 1
        block = S.block()

        def bank_of(p, h):
            return s_ps[(p * heads + h) % 3]

        def bank_used(n, p, h):
            if p * heads + h >= 3:
                return n * heads + h - 2
            return (n - 2) * heads + max(j for j in range(2 * heads) if j % 3 == h) + 1

        def behind(n, p, h):
            if h >= 0:
                return n, p, h
            if isinstance(n, int) and n == 0:
                return None
            return n - 1, 1 - p, heads + h

        def out_bank(p, b):
            return o_ps[b if OB == 2 else p]

        def image(t, n):
            return t[:, :, bass.ds(n * HW, HW)]

        def loop(eng, body):
            for p in range(2):
                body(p, p, False)
            with eng.Fori(1, B // 2 - 1) as i:
                for p in range(2):
                    body(2 * i + p, p, False)
            for p in range(2):
                body(B - 2 + p, p, p == 1)

        @block.sync
        def _(sp):
            load_w(sp, w_qkv, w_in)
            sp.wait_ge(w_cleared, 1)
            for j in range(P // HR):
                sp.dma_start(w_o[j * HR:j * HR + D, :, :], w_out.rearrange("(g j d) c -> j d g c", j=P // HR, d=D)[j]).then_inc(w_in, 16)
            if b_qkv is not None:
                for j, dst in ((0, bq), (1, bk)):
                    sp.dma_start(dst[:, :], b_qkv[j * INNER:(j + 1) * INNER].rearrange("(m p) -> p m", p=P),
                                 allow_slow_non_contiguous=True).then_inc(c_in, 16)
                sp.dma_start(bv[:, :], b_qkv[2 * INNER:3 * INNER].rearrange("(a n) -> a n", a=1)).then_inc(c_in, 16)
            sp.dma_start(bo[:, :], b_out.rearrange("(k p) -> p k", p=P), allow_slow_non_contiguous=True).then_inc(c_in, 16)

            def stack(n, p):
                for s in range(2):
                    sp.wait_ge(cut[s], n + 1)
                    sp.dma_start(pieces_dram[s].rearrange("j p m t -> p j m t"), pieces[s][:, :, :, :]).then_inc(dumped[s], 16)
                for s in range(2):
                    sp.wait_ge(dumped[s], 16 * (n + 1))
                    for g, pair in enumerate(PAIRS):
                        for m in range(MT):
                            sp.dma_start(stacks[p][s][g * D:(g + 1) * D, m * GH:(m + 1) * GH, :],
                                         pieces_dram[s][pair[s], :, m, :].rearrange("(h d) t -> d h t", d=D)).then_inc(stacked[s], 16)

            sp.dma_start(xi[:, :, :], image(xn, 0)).then_inc(xi_in, 16)
            stack(0, 0)
            sp.wait_ge(v_done, 1)
            sp.dma_start(xi[:, :, :], image(xn, 1)).then_inc(xi_in, 16)

            def body(n, p, last):
                if last:
                    return
                stack(n + 1, 1 - p)
                if isinstance(n, int) and n + 2 >= B:
                    return
                sp.wait_ge(v_done, n + 2)
                sp.dma_start(xi[:, :, :], image(xn, n + 2)).then_inc(xi_in, 16)
            loop(sp, body)

        @block.gpsimd
        def _(pool):
            nc.gpsimd.memset(w_o[:, :, :], 0.0).then_inc(w_cleared, 1)
            nc.gpsimd.memset(ones[:, :], 1.0).then_inc(consts, 1)
            for p in range(2):
                nc.gpsimd.memset(va[p][:, :, :, :], 1.0).then_inc(consts, 1)
            nc.gpsimd.tensor_copy(ident_b[:, :], ident[0:TH, 0:TH]).then_inc(consts, 1)
            nc.gpsimd.memset(mask_b[:, :, :], 0.0).then_inc(masked, 1)
            nc.gpsimd.memset(pick_sum[:, :], 0.0).then_inc(masked, 1)
            pool.wait_ge(masked, 2)
            nc.gpsimd.affine_select(out=pick_sum[:, :], in_=pick_sum[:, :], compare_op=ALU.not_equal, fill=1.0,
                                    base=-D, pattern=[[-HR, P // HR], [0, HR]], channel_multiplier=1).then_inc(consts, 1)
            nc.gpsimd.affine_select(out=mask_b[:, :, :], in_=mask_b[:, :, :], compare_op=ALU.is_ge, fill=1e30,
                                    base=0, pattern=[[0, 2], [-1, TH]], channel_multiplier=1).then_inc(consts, 1)

        @block.tensor
        def _(pe):
            def project_in(n, s):
                if s == 0:
                    pe.wait_ge(xi_in, 16 * n + 16)
                    wait(pe, v_ready, n)
                    wait(pe, x_done, n - 2)
                else:
                    pe.wait_ge(full_ready[0], n + 1)
                for m in range(MT):
                    for k in range(KC):
                        mm = nc.tensor.matmul(io_ps[:, m * HW:(m + 1) * HW], w_qkv[:, k, s * INNER + m * P:s * INNER + (m + 1) * P],
                                              xi[:, k, :], start=(k == 0), stop=(k == KC - 1))
                mm.then_inc((q_done, k_done)[s], 1)

            def values_in(n):
                pe.wait_ge(full_ready[1], n + 1)
                for t in range(2):
                    for k in range(KC):
                        mm = nc.tensor.matmul(io_ps[0:TH, t * INNER:(t + 1) * INNER], xi[:, k, t * TH:(t + 1) * TH],
                                              w_qkv[:, k, 2 * INNER:3 * INNER], start=(k == 0),
                                              stop=(k == KC - 1 and b_qkv is None))
                    if b_qkv is not None:
                        mm = nc.tensor.matmul(io_ps[0:TH, t * INNER:(t + 1) * INNER], ones[0:1, :], bv[0:1, :], start=False, stop=True)
                mm.then_inc(v_done, 1)

            def scores(n, p, h):
                wait(pe, exp_done, bank_used(n, p, h))
                if h == 0:
                    for s in range(2):
                        pe.wait_ge(stacked[s], 16 * MT * len(PAIRS) * (n + 1))
                for j, (t, b, nb) in enumerate(rows):
                    mm = nc.tensor.matmul(bank_of(p, h)[0:TH, b * TH:(b + nb) * TH], stacks[p][0][:, h, t * TH:(t + 1) * TH],
                                          stacks[p][1][:, h, 0:nb * TH], start=(j == 0), stop=(not causal and j == 1),
                                          skip_group_check=True)
                if causal:
                    out = bank_of(p, h)[0:TH, 0:2 * 2 * TH].rearrange("p (a c) -> p a c", a=2)[:, :, 0:TH]
                    mm = nc.tensor.matmul(out, ident_b[:, :], mask_b[:, :, :], start=False, stop=True, skip_group_check=True)
                mm.then_inc(s_done, 1)

            def turn(n, h):
                pe.wait_ge(exp_done, n * heads + h + 1)
                wait(pe, pt_ready[h % 2], n * (heads // 2) + h // 2)
                for t, u, b in blocks:
                    mm = nc.tensor.transpose(pt_ps[h % 2][0:TH, b * TH:(b + 1) * TH], ex[h % 4][:, b * TH:(b + 1) * TH], ident[0:TH, 0:TH])
                mm.then_inc(t_done, 1)

            def values(n, p, h):
                pe.wait_ge(pt_ready[h % 2], n * (heads // 2) + h // 2 + 1)
                if h == 0:
                    pe.wait_ge(v_ready, n + 1)
                if h % 8 == 0:
                    wait(pe, o_out, 2 * n - 1 + h // 8 if OB == 2 else n - 1)
                row, col = h % 4 * HR, h // 4 % 2 * HW
                for t, u, b in blocks:
                    last = u == (t if causal else 1)
                    mm = nc.tensor.matmul(out_bank(p, h // 8)[row:row + HR, col + t * TH:col + (t + 1) * TH], va[p][:, u, h, :],
                                          pt[h % 4][:, b * TH:(b + 1) * TH], start=(u == 0), stop=last)
                mm.then_inc(pv_done, 1)

            def spread_sums(n, b):
                pe.wait_ge(o_out, OB * n + b + 1)
                if b > 0:
                    pe.wait_ge(ln_done, OB * n + b)
                nc.tensor.matmul(io_ps[:, 0:2 * HW], pick_sum[:, :], o[:, b, :], start=True, stop=True).then_inc(spread, 1)

            def project_out(n):
                pe.wait_ge(ln_done, OB * (n + 1))
                pe.wait_ge(o_ready, n + 1)
                for k in range(KC):
                    for g in range(G):
                        mm = nc.tensor.matmul(io_ps[:, k * HW:(k + 1) * HW], w_o[:, g, k * P:(k + 1) * P],
                                              o[:, g // 2, g % 2 * HW:(g % 2 + 1) * HW], start=(g == 0), stop=(g == G - 1))
                mm.then_inc(proj_done, 1)

            pe.wait_ge(w_in, 16 * (n_w + P // HR))
            pe.wait_ge(c_in, 16 * n_c)
            pe.wait_ge(consts, 6)
            for s in range(2):
                project_in(0, s)
            values_in(0)

            def steps_behind(n, p, s):
                b = behind(n, p, s - 2)
                if b is not None:
                    turn(b[0], b[2])
                b = behind(n, p, s - 4)
                if b is not None:
                    values(*b)

            def body(n, p, last):
                for s in range(heads):
                    scores(n, p, s)
                    steps_behind(n, p, s)
                    if s in (0, 2) and not last:
                        project_in(n + 1, s // 2)
                    if s == 4 and not last:
                        values_in(n + 1)
                    if not (isinstance(n, int) and n == 0):
                        if s == 5:
                            pe.wait_ge(v_ready, n + 1 if last else n + 2)
                        if 5 <= s < 5 + OB:
                            spread_sums(n - 1, s - 5)
                        if s == 6 + OB:
                            project_out(n - 1)
            loop(pe, body)
            for s in range(2):
                turn(B - 1, heads - 2 + s)
                values(B - 1, 1, heads - 4 + s)
            for s in range(2):
                values(B - 1, 1, heads - 2 + s)
            pe.wait_ge(x_done, B - 1)
            for b in range(OB):
                spread_sums(B - 1, b)
            project_out(B - 1)

        @block.scalar
        def _(act):
            act.preload_act_table_set(LN_EXP)

            def projected(n, s):
                act.wait_ge((q_done, k_done)[s], n + 1)
                wait(act, cut[s], n)
                scale = (-q_scale, 1.0)[s]
                for m in range(MT):
                    if b_qkv is not None:
                        ins = nc.scalar.activation(full[s][:, m, :], io_ps[:, m * HW:(m + 1) * HW], ACT.Identity, scale=scale,
                                                   bias=(bq, bk)[s][:, m:m + 1])
                    else:
                        ins = nc.scalar.activation(full[s][:, m, :], io_ps[:, m * HW:(m + 1) * HW], ACT.Copy, scale=scale)
                ins.then_inc(full_ready[s], 1)

            def values_out(n, p):
                act.wait_ge(v_done, n + 1)
                wait(act, pv_done, (n - 1) * heads)
                for t in range(2):
                    ins = nc.scalar.activation(va[p][:, t, :, 0:D], io_ps[0:TH, t * INNER:(t + 1) * INNER].rearrange("p (h d) -> p h d", d=D),
                                               ACT.Copy)
                ins.then_inc(v_ready, 1)

            def outputs_out(n, p, b):
                act.wait_ge(pv_done, n * heads + 8 * (b + 1))
                wait(act, proj_done, n)
                nc.scalar.activation(o[:, b, :], out_bank(p, b)[:, 0:2 * HW], ACT.Copy).then_inc(o_out, 1)

            def log_sums(n, b):
                act.wait_ge(spread, OB * n + b + 1)
                wait(act, rinv_ready, n)
                nc.scalar.activation(lns[:, b, :], io_ps[:, 0:2 * HW], ACT.Ln).then_inc(ln_done, 1)

            def inverse_sums(n):
                act.wait_ge(ln_done, OB * (n + 1))
                wait(act, o_ready, n)
                nc.scalar.activation(rinv[:, :, :], lns[:, :, :], ACT.Exp, scale=-1.0).then_inc(rinv_ready, 1)

            def turned_out(n, h):
                act.wait_ge(t_done, n * heads + h + 1)
                wait(act, pv_done, n * heads + h - 3)
                nc.scalar.activation(pt[h % 4][:, :], pt_ps[h % 2][0:TH, 0:SW], ACT.Copy).then_inc(pt_ready[h % 2], 1)

            def exps(n, p, h):
                act.wait_ge(min_done, n * heads + h + 1)
                wait(act, t_done, n * heads + h - 3)
                for t, b, nb in rows:
                    ins = nc.scalar.activation(ex[h % 4][:, b * TH:(b + nb) * TH], bank_of(p, h)[0:TH, b * TH:(b + nb) * TH],
                                               ACT.Exp, scale=-1.0, bias=mn[:, h, t:t + 1])
                ins.then_inc(exp_done, 1)

            act.wait_ge(c_in, 16 * n_c)
            act.wait_ge(consts, 6)
            act.wait_ge(bias_scaled, 1)
            for s in range(2):
                projected(0, s)
            values_out(0, 0)

            def body(n, p, last):
                for s in range(heads):
                    exps(n, p, s)
                    b = behind(n, p, s - 2)
                    if s % 2 == 1 and b is not None:
                        turned_out(b[0], b[2])
                    if s in (0, 2) and not last:
                        projected(n + 1, s // 2)
                    if s == 4 and not last:
                        values_out(n + 1, 1 - p)
                    if s == 12:
                        outputs_out(n, p, 0)
                    if not (isinstance(n, int) and n == 0):
                        if s == 4:
                            outputs_out(n - 1, 1 - p, OB - 1)
                        if 5 <= s < 5 + OB:
                            log_sums(n - 1, s - 5)
                        if s == 4 + OB:
                            inverse_sums(n - 1)
            loop(act, body)
            turned_out(B - 1, heads - 1)
            outputs_out(B - 1, 1, OB - 1)
            for b in range(OB):
                log_sums(B - 1, b)
            inverse_sums(B - 1)

        @block.vector
        def _(dve):
            chain = Chain(dve, own)

            def cut_up(n, s):
                dve.wait_ge(full_ready[s], n + 1)
                wait(dve, dumped[s], 16 * n)
                chain.step(nc.vector.tensor_copy(pieces[s][:, 0, :, :], full[s][:, :, :]))
                chain.wait()
                chain.step(nc.vector.tensor_tensor(rest[:, :, :], full[s][:, :, :], pieces[s][:, 0, :, :], ALU.subtract))
                chain.wait()
                chain.step(nc.vector.tensor_copy(pieces[s][:, 1, :, :], rest[:, :, :]))
                chain.wait()
                last = nc.vector.tensor_tensor(pieces[s][:, 2, :, :], rest[:, :, :], pieces[s][:, 1, :, :], ALU.subtract)
                last.then_inc(cut[s], 1)

            def row_min(n, p, h):
                dve.wait_ge(s_done, n * heads + h + 1)
                if causal:
                    for t, b, nb in rows:
                        ins = nc.vector.tensor_reduce(mn[:, h, t:t + 1], bank_of(p, h)[0:TH, b * TH:(b + nb) * TH], AX_X, ALU.min)
                else:
                    ins = nc.vector.tensor_reduce(mn[:, h, :], bank_of(p, h)[0:TH, 0:SW].rearrange("p (t j) -> p t j", t=2), AX_X, ALU.min)
                ins.then_inc(min_done, 1)

            def turned_out(n, h):
                dve.wait_ge(t_done, n * heads + h + 1)
                wait(dve, pv_done, n * heads + h - 3)
                nc.vector.tensor_copy(pt[h % 4][:, :], pt_ps[h % 2][0:TH, 0:SW]).then_inc(pt_ready[h % 2], 1)

            def normalize(n):
                dve.wait_ge(rinv_ready, n + 1)
                nc.vector.scalar_tensor_tensor(o[:, :, :], o[:, :, :], out_scale, rinv[:, :, :], ALU.mult, ALU.mult).then_inc(o_ready, 1)

            def add_out(n):
                dve.wait_ge(proj_done, n + 1)
                for k in range(KC):
                    ins = nc.vector.scalar_tensor_tensor(image(x, n)[:, k, :], io_ps[:, k * HW:(k + 1) * HW], bo[:, k:k + 1],
                                                         image(x, n)[:, k, :], ALU.add, ALU.add)
                ins.then_inc(x_done, 1)

            dve.wait_ge(c_in, 16 * n_c)
            if b_qkv is not None:
                nc.vector.tensor_scalar(bq[:, :], bq[:, :], -q_scale, None, ALU.mult).then_inc(bias_scaled, 1)
            else:
                nc.vector.memset(mn[:, 0, 0:1], 0.0).then_inc(bias_scaled, 1)
            for s in range(2):
                cut_up(0, s)

            def body(n, p, last):
                if p == 0:
                    chain.turn(n, 2)
                for s in range(heads):
                    row_min(n, p, s)
                    b = behind(n, p, s - 2)
                    if s % 2 == 0 and b is not None:
                        turned_out(b[0], b[2])
                    if s in (1, 3) and not last:
                        cut_up(n + 1, s // 2)
                    if not (isinstance(n, int) and n == 0):
                        if s == 5 + OB:
                            normalize(n - 1)
                        if s == (9 if OB == 2 else 7):
                            add_out(n - 1)
            loop(dve, body)
            turned_out(B - 1, heads - 2)
            normalize(B - 1)
            add_out(B - 1)


def l2_weights(w_attn):
    def load(sp, w_qkv, w_in):
        if sp is None:
            return 1
        sp.dma_start(w_qkv[:, :, :], w_attn.rearrange("(k p) n -> p k n", p=P)).then_inc(w_in, 16)
    return load


def l3_weights(wq, wk, wv):
    def load(sp, w_qkv, w_in):
        if sp is None:
            return 3
        n = wq.shape[1]
        for j, w in enumerate((wq, wk, wv)):
            sp.dma_start(w_qkv[:, :, j * n:(j + 1) * n], w.rearrange("(k p) n -> p k n", p=P)).then_inc(w_in, 16)
    return load


def peer_ffn(nc, x, xn_dram, w, ident):
    NH, NK, DK, TOP = 8, 64, 32, 16
    G16 = 2 * NH
    NP = NH * TOP
    TT = 112
    NTILE = 2
    CT = NTILE * TT
    NCHUNK = NT // CT
    HH, PP = NTILE * NH, NTILE * NP
    J = 32
    HT = TT // 2
    NHB = 2 * NTILE
    LATE = NHB // 2
    GT = HT // 4
    LOWEST = -3.4028235e38
    CAND = [(0, 1, 16), (1, 3, 8), (4, 4, 4), (8, 8, 1)]
    row_start = [off for a0, na, nb, o in ((0, 1, 16, 0), (1, 3, 8, 16), (4, 4, 4, 40), (8, 8, 1, 56)) for off in range(o, o + na * nb, nb)]
    with Scope(nc, "peer") as S:
        up = S.sb("up", [P, J, C])
        dt = S.sb("dt", [P, KC, J, P])
        g = S.sb("g", [P, J, CT])
        oh_a = [S.sb(f"oh_a{p}", [P, P, HT], BF16) for p in range(2)]
        oh_h = [S.sb(f"oh_h{p}", [P, J, HT], BF16) for p in range(2)]
        oh_l = [S.sb(f"oh_l{p}", [P, J, HT], BF16) for p in range(2)]
        iota_f = S.sb("iota_f", [P, P, GT], BF16)
        wq = S.sb("wq", [P, KC, 2 * NH * DK])
        keys_b = S.sb("keys_b", [P, 4, 4 * NK])
        xc = [S.sb(f"xc{p}", [P, KC, CT]) for p in range(2)]
        qt = S.sb("qt", [P, 4, CT])
        m_copy = [qt[:, 2 * p:2 * p + 2, :].rearrange("p m t -> p (m t)") for p in range(2)]
        sc = [S.sb(f"sc{p}", [TT, G16, NK]) for p in range(NTILE)]
        keys_n = sc[1][0:NK, 0:NH, :].rearrange("k h r -> k (h r)")
        v16, i16 = S.sb("v16", [TT, NTILE * G16, TOP]), S.sb("i16", [TT, NTILE * G16, TOP], U32)
        i16f, step16 = S.sb("i16f", [TT, NTILE * G16, TOP]), S.sb("step16", [TT, 2, TOP, HH], BF16)
        cv = sc[0]
        f16, p16 = S.sb("f16", [TT, HH, TOP]), S.sb("p16", [TT, HH, TOP], U32)
        pos_b, col_b = S.sb("pos_b", [TT, PP], BF16), S.sb("col_b", [TT, PP], BF16)
        t1, t2, t3 = S.sb("t1", [TT, PP]), S.sb("t2", [TT, PP]), S.sb("t3", [TT, PP])
        bits, col = S.sb("bits", [TT, PP], U32), S.sb("col", [TT, PP], U32)
        starts_b, ranks_b = S.sb("starts_b", [TT, TOP, TOP], BF16), S.sb("ranks_b", [TT, TOP, TOP], BF16)
        sel = [oh_a[p][0:TT, :, :].rearrange("t r k -> t (r k)")[:, 0:TOP * PP].rearrange("t (a k) -> t a k", a=TOP) for p in range(2)]
        i1, i2 = t2, t3
        codes = S.sb("codes", [TT, 3, PP])
        a_t = S.sb("a_t", [P, CT], BF16)
        b_t = S.sb("b_t", [P, CT], BF16)
        wh_t, wl_t = S.sb("wh_t", [P, CT], BF16), S.sb("wl_t", [P, CT], BF16)
        x_ps = [S.ps(f"x{p}") for p in range(4)]
        sim_ps = [S.ps(f"sim{p}") for p in range(2)]
        tr_ps, out_ps = S.ps("tr"), S.ps("out")
        w_in, d_in, w_turned = S.sem("w_in"), S.sem("d_in"), S.sem("w_turned")
        w_out = S.sem("w_out")
        xc_in = [S.sem(f"xc_in{p}") for p in range(2)]
        q_done, q_ready, sim_done, sim_ready = S.sem("q_done"), S.sem("q_ready"), S.sem("sim_done"), S.sem("sim_ready")
        codes_ready, tr_done, tr_ready, wl_ready = S.sem("codes_ready"), S.sem("tr_done"), S.sem("tr_ready"), S.sem("wl_ready")
        oh_ready, h_done, gelu_done, m_done, g_done = S.sem("oh_ready"), S.sem("h_done"), S.sem("gelu_done"), S.sem("m_done"), S.sem("g_done")
        g_done_late, m_copied = S.sem("g_done_late"), S.sem("m_copied")
        out_done, x_done, own, keys_ready = S.sem("out_done"), S.sem("x_done"), S.sem("own"), S.sem("keys_ready")
        iota_done = S.sem("iota_done")
        pad = S.sb("pad", [1, 1 + NTILE])
        block = S.block()
        NPAIR = J // 2
        EARLY = 10
        JS = 8
        stage = [g[:, 0:10, :].rearrange("p j t -> p (j t)")[:, 0:JS * C], g[:, 10:20, :].rearrange("p j t -> p (j t)")[:, 0:JS * C]]

        def by_halves(dram, h):
            return dram.rearrange("(i h j) d -> h i j d", h=2, j=J)[h]

        def chunks(eng, chunk):
            for p in range(2):
                chunk(p, p, False)
            with eng.Fori(1, NCHUNK // 2 - 1) as i:
                for p in range(2):
                    chunk(2 * i + p, p, False)
            for p in range(2):
                chunk(NCHUNK - 2 + p, p, p == 1)

        @block.sync
        def _(sp):
            sp.dma_start(wq[:, :, :], w["wq"].rearrange("(k p) n -> p k n", p=P)).then_inc(w_in, 16)
            sp.dma_start(keys_n.rearrange("k (h r) -> k h r", h=NH), w["keys"].rearrange("h k p d -> k h (p d)")).then_inc(w_in, 16)
            for p in range(2):
                sp.dma_start(xc[p][:, :, :], xn_dram[:, :, p * CT:(p + 1) * CT].rearrange("k p t -> p k t")).then_inc(xc_in[p], 16)
            for s in range(J // JS):
                if s >= 2:
                    sp.wait_ge(w_turned, 4 * (s - 1) + 1)
                for h in range(2):
                    sp.dma_start(stage[s % 2][64 * h:64 * h + 64, :].rearrange("p (j d) -> p j d", j=JS),
                                 by_halves(w["expert_down"], h)[:, s * JS:(s + 1) * JS, :]).then_inc(d_in, 16)
                sp.wait_ge(d_in, 32 * (s + 1))
            for h in range(2):
                sp.dma_start(up[64 * h:64 * h + 64, :, :], by_halves(w["expert_up"], h)).then_inc(w_in, 16)

            def body(i):
                for p in range(2):
                    n = 2 * i + p
                    sp.wait_ge(h_done, NPAIR * (n + 1))
                    sp.dma_start(xc[p][:, :, :], xn_dram[:, :, bass.ds((n + 2) * CT, CT)].rearrange("k p t -> p k t")).then_inc(xc_in[p], 16)
            steps(sp, NCHUNK // 2 - 1, body)

        @block.gpsimd
        def _(pool):
            nc.gpsimd.iota(iota_f[:, :, :], [[1, P], [0, GT]], base=0, channel_multiplier=0,
                           allow_small_or_imprecise_dtypes=True).then_inc(iota_done, 1)
            nc.gpsimd.iota(ranks_b[:, :, :], [[1, TOP], [0, TOP]], base=0, channel_multiplier=0,
                           allow_small_or_imprecise_dtypes=True).then_inc(iota_done, 1)
            for a in range(TOP):
                nc.gpsimd.memset(starts_b[:, a, :], float(row_start[a])).then_inc(iota_done, 1)
            nc.gpsimd.memset(keys_b[:, :, :], 0.0).then_inc(iota_done, 1)

            def chunk(n, p, last):
                for hb in range(LATE, NHB):
                    for q in range(4):
                        pool.wait_ge(m_copied, 4 * (NHB - LATE) * n + 4 * (hb - LATE) + q + 1)
                        ts = slice(hb * HT + q * GT, hb * HT + (q + 1) * GT)
                        nc.gpsimd.tensor_tensor(g[:, :, ts], g[:, :, ts], m_copy[q % 2].rearrange("p (t j) -> p j t", j=J),
                                                ALU.mult).then_inc(g_done_late, 1)
            chunks(pool, chunk)

        @block.tensor
        def _(pe):
            def queries(n, p):
                pe.wait_ge(xc_in[p], 8 * (n - p) + 16)
                wait(pe, sim_ready, NTILE * n)
                for m in range(4):
                    for k in range(KC):
                        mm = nc.tensor.matmul(sim_ps[m // 2][:, (m % 2) * CT:(m % 2 + 1) * CT], wq[:, k, m * P:(m + 1) * P],
                                              xc[p][:, k, :], start=(k == 0), stop=(k == KC - 1))
                mm.then_inc(q_done, 1)

            def scores(n, t):
                pe.wait_ge(q_ready, n + 1)
                if t > 0:
                    pe.wait_ge(sim_ready, NTILE * n + t)
                for m in range(4):
                    mm = nc.tensor.matmul(sim_ps[m // 2][0:TT, (m % 2) * 4 * NK:(m % 2 + 1) * 4 * NK], qt[:, m, t * TT:(t + 1) * TT],
                                          keys_b[:, m, :], start=True, stop=True)
                mm.then_inc(sim_done, 1)

            def hidden(n, p, pairs):
                for jp in pairs:
                    b = jp % 4
                    if jp < 4:
                        wait(pe, m_copied, 4 * (NHB - LATE) * n - 3 + jp)
                    else:
                        pe.wait_ge(gelu_done, NPAIR * n + jp - 3)
                    for jj in range(2):
                        for k in range(KC):
                            mm = nc.tensor.matmul(x_ps[b][:, jj * CT:(jj + 1) * CT], dt[:, k, 2 * jp + jj, :], xc[p][:, k, :],
                                                  start=(k == 0), stop=(k == KC - 1))
                    mm.then_inc(h_done, 1)

            def turn(n, t):
                pe.wait_ge(codes_ready, n + 1)
                wait(pe, tr_ready, NTILE * n + t)
                wait(pe, wl_ready, NTILE * n + t)
                for s in range(3):
                    mm = nc.tensor.transpose(tr_ps[:, s * TT:(s + 1) * TT], codes[:, s, t * NP:(t + 1) * NP], ident[0:TT, 0:TT])
                mm.then_inc(tr_done, 1)

            def scatter(n, hb):
                pe.wait_ge(oh_ready, NHB * n + hb + 1)
                for q in range(4):
                    if hb == 0:
                        pe.wait_ge(gelu_done, NPAIR * (n + 1))
                    elif hb < LATE + 1:
                        pe.wait_ge(g_done, 4 * LATE * n + 4 * (hb - 1) + q + 1)
                    else:
                        pe.wait_ge(m_copied, 4 * (NHB - LATE) * n + 4 * (hb - 1 - LATE) + q + 1)
                    for i in range(GT):
                        t = q * GT + i
                        nc.tensor.matmul(x_ps[q][:, i * J:(i + 1) * J], oh_a[hb % 2][:, :, t], oh_h[hb % 2][:, :, t], start=True, stop=False)
                        mm = nc.tensor.matmul(x_ps[q][:, i * J:(i + 1) * J], oh_a[hb % 2][:, :, t], oh_l[hb % 2][:, :, t], start=False, stop=True)
                    mm.then_inc(m_done, 1)

            def experts_out(n):
                pe.wait_ge(g_done, 4 * LATE * (n + 1))
                pe.wait_ge(g_done_late, 4 * (NHB - LATE) * (n + 1))
                wait(pe, x_done, n)
                for m in range(KC):
                    for j in range(J):
                        mm = nc.tensor.matmul(out_ps[:, m * CT:(m + 1) * CT], up[:, j, m * P:(m + 1) * P], g[:, j, :],
                                              start=(j == 0), stop=(j == J - 1))
                mm.then_inc(out_done, 1)

            pe.wait_ge(w_in, 16 * 2)
            for m in range(4):
                mm = nc.tensor.transpose(tr_ps[:, m * NK:(m + 1) * NK], keys_n[:, m * P:(m + 1) * P], ident[0:NK, 0:NK])
            mm.then_inc(w_turned, 1)
            pe.wait_ge(keys_ready, 1)
            queries(0, 0)
            for t in range(NTILE):
                scores(0, t)
            for s in range(J // JS):
                pe.wait_ge(d_in, 32 * (s + 1))
                for r in range(4):
                    i = 4 * s + r
                    if i >= 4:
                        pe.wait_ge(w_out, i - 3)
                    for jj in range(2):
                        for k in range(KC):
                            j = 2 * r + jj
                            mm = nc.tensor.transpose(x_ps[i % 4][:, (2 * jj + k) * P:(2 * jj + k + 1) * P],
                                                     stage[s % 2][:, j * C + k * P:j * C + (k + 1) * P], ident[:, :])
                    mm.then_inc(w_turned, 1)
            pe.wait_ge(w_out, 16)
            pe.wait_ge(w_in, 16 * 4)

            def chunk(n, p, last):
                hidden(n, p, range(EARLY))
                for t in range(NTILE):
                    turn(n, t)
                hidden(n, p, range(EARLY, NPAIR))
                if not last:
                    queries(n + 1, 1 - p)
                for hb in range(NHB):
                    scatter(n, hb)
                    if hb < NTILE and not last:
                        scores(n + 1, hb)
                experts_out(n)
            chunks(pe, chunk)

        @block.scalar
        def _(act):
            act.preload_act_table(ACT.Gelu)
            def query_out(n):
                act.wait_ge(q_done, n + 1)
                for b in range(2):
                    ins = nc.scalar.activation(qt[:, 2 * b:2 * b + 2, :], sim_ps[b][:, 0:2 * CT].rearrange("p (m t) -> p m t", m=2), ACT.Copy)
                ins.then_inc(q_ready, 1)

            def score_out(n, t):
                act.wait_ge(sim_done, NTILE * n + t + 1)
                for b in range(2):
                    ins = nc.scalar.activation(sc[t][:, 8 * b:8 * b + 8, :], sim_ps[b][0:TT, :].rearrange("p (g k) -> p g k", g=8), ACT.Copy)
                ins.then_inc(sim_ready, 1)

            query_out(0)
            for t in range(NTILE):
                score_out(0, t)
            for i in range(16):
                act.wait_ge(w_turned, i + 2)
                nc.scalar.activation(dt[:, :, 2 * i:2 * i + 2, :].rearrange("p k j e -> p j k e"),
                                     x_ps[i % 4][:, :].rearrange("p (j k e) -> p j k e", j=2, k=KC), ACT.Copy).then_inc(w_out, 1)

            def hidden_out(n, pairs):
                for jp in pairs:
                    act.wait_ge(h_done, NPAIR * n + jp + 1)
                    nc.scalar.activation(g[:, 2 * jp:2 * jp + 2, :], x_ps[jp % 4][:, 0:2 * CT].rearrange("p (j t) -> p j t", j=2),
                                         ACT.Gelu).then_inc(gelu_done, 1)

            def chunk(n, p, last):
                wait(act, out_done, n)
                hidden_out(n, range(EARLY))
                for t in range(NTILE):
                    act.wait_ge(tr_done, NTILE * n + t + 1)
                    ts = slice(t * TT, (t + 1) * TT)
                    if t == 0:
                        wait(act, oh_ready, NHB * n)
                    nc.scalar.activation(wh_t[:, ts], tr_ps[:, 2 * TT:3 * TT], ACT.Copy)
                    nc.scalar.activation(a_t[:, ts], tr_ps[:, 0:TT], ACT.Copy)
                    nc.scalar.activation(b_t[:, ts], tr_ps[:, TT:2 * TT], ACT.Copy).then_inc(tr_ready, 1)
                hidden_out(n, range(EARLY, NPAIR))
                if not last:
                    query_out(n + 1)
                    for t in range(NTILE):
                        score_out(n + 1, t)
                for k in range(4 * (NHB - LATE)):
                    act.wait_ge(m_done, 4 * NHB * n + 4 * LATE + k + 1)
                    wait(act, g_done_late, 4 * (NHB - LATE) * n + k - 1)
                    nc.scalar.activation(m_copy[k % 2], x_ps[k % 4][:, 0:GT * J], ACT.Copy).then_inc(m_copied, 1)
            chunks(act, chunk)

        @block.vector
        def _(dve):
            dve.wait_ge(w_turned, 1)
            dve.wait_ge(iota_done, TOP + 3)
            for q in range(4):
                rows = slice(32 * q, 32 * q + 32)
                ins = nc.vector.tensor_copy(keys_b[rows, :, q * NK:(q + 1) * NK], tr_ps[rows, 0:4 * NK].rearrange("p (m k) -> p m k", m=4))
            ins.then_inc(keys_ready, 1)
            chain = Chain(dve, own)

            def top16(values, indices, sources):
                for half in range(2):
                    r = slice(8 * half, 8 * half + 8)
                    for q, source in enumerate(sources):
                        ins = nc.vector.max(values[:, q, r], source)
                    chain.step(ins)
                    chain.wait()
                    nc.vector.memset(pad[:, 0:1], 0.0)
                    for q, source in enumerate(sources):
                        last = nc.vector.max_index(indices[:, q, r], values[:, q, r], source)
                        if half == 0:
                            ins = nc.vector.match_replace(source, values[:, q, r], source, LOWEST)
                    if half == 1:
                        ins = last
                    chain.step(ins)
                    if half == 0:
                        chain.wait()
                        nc.vector.memset(pad[:, 0:1], 0.0)

            H = TOP // 2
            parts = [(slice(0, H), slice(0, TOP)), (slice(H, TOP), slice(H, TOP))]
            by_entry = [m.rearrange("t a (k h) -> t a k h", h=HH) for m in sel]

            def reached(which, places, table):
                for entries, ranks in parts:
                    shape = [TT, H, ranks.stop - ranks.start, HH]
                    ins = nc.vector.tensor_tensor(by_entry[which][:, entries, ranks, :],
                                                  places[:, :].rearrange("t (k h) -> t k h", h=HH)[:, ranks, :].unsqueeze(1).broadcast_to(shape),
                                                  table[:, entries, :].unsqueeze(2).broadcast_to(shape), ALU.is_ge)
                chain.step(ins)

            def times_steps(which):
                for entries, ranks in parts:
                    shape = [TT, H, ranks.stop - ranks.start, HH]
                    m = by_entry[which][:, entries, ranks, :]
                    ins = nc.vector.tensor_tensor(m, m, step16[:, which, entries, :].unsqueeze(2).broadcast_to(shape), ALU.mult)
                chain.step(ins)

            def fold(which, n, out=None):
                m = sel[which]
                if n == H:
                    low, high = (by_entry[which][:, e, H:TOP, :] for e in (slice(0, H), slice(H, TOP)))
                    chain.step(nc.vector.tensor_tensor(low, low, high, ALU.add))
                elif n > 1:
                    chain.step(nc.vector.tensor_tensor(m[:, 0:n, :], m[:, 0:n, :], m[:, n:2 * n, :], ALU.add))
                else:
                    chain.step(nc.vector.tensor_tensor(out[:, :], m[:, 0, :], m[:, 1, :], ALU.add))

            def top_halves(n, t):
                dve.wait_ge(sim_ready, NTILE * n + t + 1)
                nc.vector.memset(pad[:, 1 + t:2 + t], 0.0)
                groups = slice(t * G16, (t + 1) * G16)
                top16(v16[:, groups, :], i16[:, groups, :], [sc[t][:, q, :] for q in range(G16)])

            def make_codes(n):
                v = v16[:, :, :].rearrange("t (h w) a -> t w h a", w=2)
                o = 0
                chain.wait()
                for a0, na, nb in CAND:
                    out = cv[:, :, o:o + na * nb]
                    v1, v2 = v[:, 0, :, a0:a0 + na], v[:, 1, :, 0:nb]
                    if na == 1:
                        v1 = v1.broadcast_to([TT, HH, nb])
                    elif nb == 1:
                        v2 = v2.broadcast_to([TT, HH, na])
                    else:
                        out = out.rearrange("t h (a b) -> t h a b", a=na)
                        v1 = v1.unsqueeze(3).broadcast_to([TT, HH, na, nb])
                        v2 = v2.unsqueeze(2).broadcast_to([TT, HH, na, nb])
                    ins = nc.vector.tensor_tensor(out, v1, v2, ALU.add)
                    o += na * nb
                chain.step(ins)
                chain.step(nc.vector.tensor_copy(i16f[:, :, :], i16[:, :, :]))
                chain.wait()
                for half in range(2):
                    entries = i16f[:, :, :].rearrange("t (h w) a -> t w a h", w=2)[:, half, :, :]
                    nc.vector.tensor_tensor(step16[:, half, 1:TOP, :], entries[:, 1:TOP, :], entries[:, 0:TOP - 1, :], ALU.subtract)
                    ins = nc.vector.tensor_copy(step16[:, half, 0, :], entries[:, 0, :])
                chain.step(ins)
                top16(f16, p16, [cv[:, h, :] for h in range(HH)])
                fv = f16[:, :, :].rearrange("t h k -> t (h k)")
                pv = p16[:, :, :].rearrange("t h k -> t k h")

                def by_rank(m):
                    return m.rearrange("t (k h) -> t k h", h=HH)
                chain.wait()
                wait(dve, tr_done, NTILE * n)
                chain.step(nc.vector.tensor_scalar(codes[:, 2, :], fv, 0.0, None, ALU.max))
                chain.step(nc.vector.tensor_copy(by_rank(pos_b[:, :]), pv))
                chain.wait()
                wait(dve, m_done, 4 * NHB * n)
                chain.step(nc.vector.tensor_scalar(t1[:, :], pos_b[:, :], 16.0, -8.0, ALU.is_ge, ALU.mult))
                chain.step(nc.vector.tensor_scalar(t2[:, :], pos_b[:, :], 40.0, -4.0, ALU.is_ge, ALU.mult))
                chain.step(nc.vector.tensor_scalar(t3[:, :], pos_b[:, :], 56.0, -3.0, ALU.is_ge, ALU.mult))
                reached(0, pos_b, starts_b)
                chain.wait(but=1)
                chain.step(nc.vector.tensor_tensor(t1[:, :], t1[:, :], t2[:, :], ALU.add))
                chain.wait(but=1)
                times_steps(0)
                chain.wait(but=1)
                chain.step(nc.vector.scalar_tensor_tensor(bits[:, :], t1[:, :], 15.0, t3[:, :], ALU.add, ALU.add))
                chain.wait(but=1)
                fold(0, H)
                chain.wait(but=1)
                chain.step(nc.vector.tensor_tensor(by_rank(col[:, :]), pv, by_rank(bits[:, :]), ALU.bitwise_and))
                chain.wait(but=1)
                fold(0, H // 2)
                chain.wait(but=1)
                chain.step(nc.vector.tensor_copy(col_b[:, :], col[:, :]))
                chain.wait(but=1)
                fold(0, H // 4)
                chain.wait(but=1)
                reached(1, col_b, ranks_b)
                chain.wait(but=1)
                fold(0, 1, i1)
                chain.wait(but=1)
                times_steps(1)
                for size in (H, H // 2, H // 4, 1):
                    chain.wait()
                    fold(1, size, i2)
                chain.wait()
                chain.step(nc.vector.tensor_scalar(t1[:, :], i2[:, :], 32.0, 64.0, ALU.is_ge, ALU.mult))
                chain.wait()
                row, column = (codes[:, c, :].rearrange("t (h k) -> t k h", k=TOP) for c in range(2))
                nc.vector.tensor_tensor(row, by_rank(t1[:, :]), by_rank(i1[:, :]), ALU.add)
                nc.vector.scalar_tensor_tensor(column, by_rank(t1[:, :]), -0.5, by_rank(i2[:, :]), ALU.mult, ALU.add).then_inc(codes_ready, 1)

            def low_weights(n, t):
                dve.wait_ge(tr_ready, NTILE * n + t + 1)
                ts = slice(t * TT, (t + 1) * TT)
                nc.vector.tensor_tensor(wl_t[:, ts], tr_ps[:, 2 * TT:3 * TT], wh_t[:, ts], ALU.subtract).then_inc(wl_ready, 1)

            def one_hots(n, hb):
                q = hb % 2
                wait(dve, m_done, 16 * n + 4 * (hb - 1))
                if hb % 2 == 0:
                    dve.wait_ge(wl_ready, NTILE * n + hb // 2 + 1)
                ts = slice(hb * HT, (hb + 1) * HT)

                def spread(v, rows):
                    return v[:, ts].rearrange("p (a b) -> p a b", b=GT).unsqueeze(1).broadcast_to([P, rows, HT // GT, GT])

                def number(rows):
                    return iota_f[:, 0:rows, :].unsqueeze(2).broadcast_to([P, rows, HT // GT, GT])

                def view(m):
                    return m[:, :, :].rearrange("p r (a b) -> p r a b", b=GT)
                nc.vector.tensor_tensor(view(oh_a[q]), spread(a_t, P), number(P), ALU.is_equal)
                chain.step(nc.vector.tensor_tensor(view(oh_l[q]), spread(b_t, J), number(J), ALU.is_equal))
                chain.wait()
                for dst, wt in ((oh_h, wh_t), (oh_l, wl_t)):
                    ins = nc.vector.tensor_tensor(dst[q][:, :, :], oh_l[q][:, :, :], wt[:, ts].unsqueeze(1).broadcast_to([P, J, HT]), ALU.mult)
                ins.then_inc(oh_ready, 1)

            def weigh(n, hb):
                for q in range(4):
                    dve.wait_ge(m_done, 4 * NHB * n + 4 * hb + q + 1)
                    ts = slice(hb * HT + q * GT, hb * HT + (q + 1) * GT)
                    nc.vector.tensor_tensor(g[:, :, ts], g[:, :, ts], x_ps[q][:, 0:GT * J].rearrange("p (t j) -> p j t", j=J),
                                            ALU.mult).then_inc(g_done, 1)

            for t in range(NTILE):
                top_halves(0, t)
            make_codes(0)

            def chunk(n, p, last):
                if p == 0:
                    chain.turn(n, 2)
                low_weights(n, 0)
                one_hots(n, 0)
                low_weights(n, 1)
                for hb in range(NHB - 1):
                    one_hots(n, hb + 1)
                    if hb < LATE:
                        weigh(n, hb)
                if not last:
                    for t in range(NTILE):
                        top_halves(n + 1, t)
                    make_codes(n + 1)
                dve.wait_ge(out_done, n + 1)
                xs = x[:, :, bass.ds(n * CT, CT)]
                nc.vector.tensor_tensor(xs, xs, out_ps[:, 0:KC * CT].rearrange("p (k t) -> p k t", k=KC), ALU.add).then_inc(x_done, 1)
            chunks(dve, chunk)


def moe_ffn(nc, x, xn, y_dram, w, ident):
    E, F = 8, 1024
    CAP = NT // E
    TT = 112
    NTILES = NT // TT
    Q = 4
    QT = Q * TT
    KF = F // P
    ST = CAP // 4
    IMGS = 4
    with Scope(nc, "moe") as S:
        expert_in = nc.dram_tensor("moe_expert_in", [2 * NT, C], F32, kind="Internal").ap()
        expert_out = nc.dram_tensor("moe_expert_out", [NT, C], F32, kind="Internal").ap()
        router = S.sb("router", [P, KC, E])
        xs = [S.sb(f"xs{q}", [P, KC, TT]) for q in range(Q)]
        logits_t = S.sb("logits_t", [E, NT])
        logits, rows = S.sb("logits", [TT, NTILES, E]), S.sb("rows", [TT, NTILES, C])
        marks = S.sb("marks", [1, NTILES // Q])
        zero = S.sb("zero", [TT, C])
        tri, ones = S.sb("tri", [TT, TT]), S.sb("ones", [TT, TT])
        e_num, spare = S.sb("e_num", [TT, NTILES, E]), S.sb("spare", [TT, NTILES])
        best, dist, expd = S.sb("best", [TT, NTILES]), S.sb("dist", [TT, NTILES, E]), S.sb("expd", [TT, NTILES, E])
        total, gate = S.sb("total", [TT, NTILES]), S.sb("gate", [TT, NTILES])
        cand, first, onehot = S.sb("cand", [TT, NTILES, E]), S.sb("first", [TT, NTILES]), S.sb("onehot", [TT, NTILES, E])
        before = [S.sb(f"before{p}", [TT, NTILES, E]) for p in range(2)]
        count, picked = S.sb("count", [TT, NTILES, E]), S.sb("picked", [TT, NTILES])
        kept, slot_f, sent_f = S.sb("kept", [TT, NTILES]), S.sb("slot_f", [TT, NTILES]), S.sb("sent_f", [TT, NTILES])
        slot, sent = S.sb("slot", [TT, NTILES], U32), S.sb("sent", [TT, NTILES], U32)
        w1 = [S.sb(f"w1_{p}", [P, KC, F]) for p in range(2)]
        w2 = [S.sb(f"w2_{p}", [P, KF, C]) for p in range(2)]
        b1_rows, b1, b2 = S.sb("b1_rows", [E * KF, P]), S.sb("b1", [P, E * KF]), S.sb("b2", [ST, E, C])
        ein = [S.sb(f"ein{p}", [ST, 4, C]) for p in range(2)]
        ein_t = [S.sb(f"ein_t{p}", [P, KC, CAP]) for p in range(2)]
        h = [S.sb(f"h{p}", [P, KF, CAP]) for p in range(2)]
        y = [S.sb(f"y{p}", [ST, 4, C]) for p in range(2)]
        scaled = [S.sb(f"scaled{q}", [TT, C]) for q in range(Q)]
        a_ps = [S.ps(f"a{q}") for q in range(4)]
        t_ps = [S.ps(f"t{k}") for k in range(2)]
        y_ps = [S.ps(f"y{k}") for k in range(2)]
        consts_in, consts = S.sem("consts_in"), S.sem("consts")
        w_in = [S.sem(f"w_in{p}") for p in range(2)]
        ein_in = [S.sem(f"ein_in{p}") for p in range(2)]
        y_out = [S.sem(f"y_out{p}") for p in range(2)]
        zeroed, scattered, x_out = S.sem("zeroed"), S.sem("scattered"), S.sem("x_out")
        copied, turned, rows_ready = S.sem("copied"), S.sem("turned"), S.sem("rows_ready")
        scored_out = S.sem("scored_out")
        scored, logits_ready = S.sem("scored"), S.sem("logits_ready")
        b1_turned, b1_ready = S.sem("b1_turned"), S.sem("b1_ready")
        own, dist_ready, exp_ready = S.sem("own"), S.sem("dist_ready"), S.sem("exp_ready")
        onehot_ready, counted, slots_ready = S.sem("onehot_ready"), S.sem("counted"), S.sem("slots_ready")
        ein_turned, ein_ready, h_done, h_ready = S.sem("ein_turned"), S.sem("ein_ready"), S.sem("h_done"), S.sem("h_ready")
        y_done, y_ready = S.sem("y_done"), S.sem("y_ready")
        gathered = [S.sem(f"gathered{p}") for p in range(2)]
        rows_back, scaled_ready, back_turned, x_done = S.sem("rows_back"), S.sem("scaled_ready"), S.sem("back_turned"), S.sem("x_done")
        block = S.block()

        def slots_of(dram, e):
            return dram[bass.ds(e * CAP, CAP), :].rearrange("(s p) d -> p s d", p=ST)

        @block.sync
        def _(sp):
            sp.dma_start(router[:, :, :], w["router_w"].rearrange("(k p) e -> p k e", p=P)).then_inc(consts_in, 16)
            sp.dma_start(b1_rows[:, :], w["b1"].rearrange("e (f p) -> (e f) p", p=P)).then_inc(consts_in, 16)
            sp.dma_start(b2[:, :, :], w["b2"].unsqueeze(0).broadcast_to([ST, E, C])).then_inc(consts_in, 16)
            sp.wait_ge(consts, 1)
            sp.dma_start(expert_in[0:NT, :].rearrange("(j p) d -> p j d", p=TT),
                         zero[:, :].unsqueeze(1).broadcast_to([TT, NTILES, C])).then_inc(zeroed, 16)

            def weights(e, p):
                sp.dma_start(w1[p][:, :, :], w["w1"][bass.ds(e, 1)].rearrange("o (k p) f -> p (o k) f", p=P)).then_inc(w_in[p], 16)
                sp.dma_start(w2[p][:, :, :], w["w2"][bass.ds(e, 1)].rearrange("o (k p) d -> p (o k) d", p=P)).then_inc(w_in[p], 16)
            for p in range(2):
                weights(p, p)
            sp.wait_ge(scattered, 16 * NTILES)
            for p in range(2):
                sp.dma_start(ein[p][:, :, :], slots_of(expert_in, p)).then_inc(ein_in[p], 16)

            def body(i):
                for p in range(2):
                    e = 2 * i + p
                    sp.wait_ge(y_ready, 4 * (e + 1))
                    sp.dma_start(slots_of(expert_out, e), y[p][:, :, :]).then_inc(y_out[p], 16)
                    if isinstance(i, int) and i == E // 2 - 1:
                        continue
                    sp.wait_ge(ein_turned, e + 1)
                    sp.dma_start(ein[p][:, :, :], slots_of(expert_in, e + 2)).then_inc(ein_in[p], 16)
                    weights(e + 2, p)
            body(0)
            with sp.Fori(1, E // 2 - 1) as i:
                body(i)
            body(E // 2 - 1)
            for b in range(0, B, IMGS):
                sp.wait_ge(x_done, (b + IMGS) * HW // TT)
                for k in range(KC):
                    sp.dma_start(y_dram[b:b + IMGS, k * P:(k + 1) * P, :].rearrange("b p t -> p b t"),
                                 x[:, k, b * HW:(b + IMGS) * HW].rearrange("p (b t) -> p b t", b=IMGS)).then_inc(x_out, 16)
            sp.wait_ge(x_out, 16 * KC * B // IMGS)
            for p in range(2):
                sp.wait_ge(y_out[p], 16 * E // 2)

        @block.gpsimd
        def _(pool):
            nc.gpsimd.memset(zero[:, :], 0.0).then_inc(consts, 1)
            nc.gpsimd.memset(ones[:, :], 1.0).then_inc(consts, 1)
            nc.gpsimd.iota(e_num[:, :, :], [[0, NTILES], [1, E]], base=0, channel_multiplier=0,
                           allow_small_or_imprecise_dtypes=True).then_inc(consts, 1)
            nc.gpsimd.iota(spare[:, :], [[TT, NTILES]], base=NT, channel_multiplier=1,
                           allow_small_or_imprecise_dtypes=True).then_inc(consts, 1)
            pool.wait_ge(consts, 4)
            nc.gpsimd.affine_select(out=tri[:, :], in_=ones[:, :], compare_op=ALU.is_ge, fill=0.0,
                                    base=0, pattern=[[1, TT]], channel_multiplier=-1).then_inc(consts, 1)
            pool.wait_ge(slots_ready, 1)
            pool.wait_ge(zeroed, 16)
            for j in range(NTILES):
                pool.wait_ge(rows_ready, j + 1)
                pool.indirect_dma_start(expert_in[:, :], bass.IndirectOffsetOnAxis(ap=sent[:, j:j + 1], axis=0),
                                        rows[:, j, :], None).then_inc(scattered, 16)
            pool.wait_ge(scattered, 16 * NTILES)
            for p in range(2):
                pool.wait_ge(y_out[p], 16 * E // 2)
            for i in range(NTILES // Q):
                for q in range(Q):
                    j = Q * i + q
                    pool.indirect_dma_start(rows[:, j, :], None, expert_out[:, :],
                                            bass.IndirectOffsetOnAxis(ap=slot[:, j:j + 1], axis=0)).then_inc(gathered[i % 2], 16)
                if i > 0:
                    pool.wait_ge(gathered[(i - 1) % 2], 16 * Q * ((i - 1) // 2 + 1))
                    nc.gpsimd.memset(marks[:, i - 1:i], 0.0).then_inc(rows_back, 1)
            pool.wait_ge(gathered[(NTILES // Q - 1) % 2], 16 * Q * ((NTILES // Q - 1) // 2 + 1))
            nc.gpsimd.memset(marks[:, NTILES // Q - 1:NTILES // Q], 0.0).then_inc(rows_back, 1)

        @block.tensor
        def _(pe):
            pe.wait_ge(consts_in, 48)
            nc.tensor.transpose(y_ps[0][:, 0:E * KF], b1_rows[:, :], ident[0:E * KF, 0:E * KF]).then_inc(b1_turned, 1)

            for i in range(NT // QT):
                wait(pe, scored_out, i - 3)
                for k in range(KC):
                    mm = nc.tensor.matmul(a_ps[i % 4][0:E, 0:QT], router[:, k, :], xn[:, k, i * QT:(i + 1) * QT], start=(k == 0), stop=(k == KC - 1))
                mm.then_inc(scored, 1)
            for j in range(NTILES):
                pe.wait_ge(scored_out, j // Q + 1)
                mm = nc.tensor.transpose(y_ps[1][0:TT, j * E:(j + 1) * E], logits_t[:, j * TT:(j + 1) * TT], ident[0:E, 0:E])
            mm.then_inc(logits_ready, 1)
            pe.wait_ge(consts, 5)
            pe.wait_ge(onehot_ready, 1)
            oh = onehot[:, :, :].rearrange("p j e -> p (j e)")
            nc.tensor.matmul(t_ps[0][0:TT, 0:NTILES * E], tri[:, :], oh, start=True, stop=True)
            nc.tensor.matmul(t_ps[1][0:TT, 0:NTILES * E], ones[:, :], oh, start=True, stop=True).then_inc(counted, 1)

            def to_rows(i):
                for q in range(Q):
                    j = Q * i + q
                    pe.wait_ge(copied, j + 1)
                    wait(pe, rows_ready, j - Q + 1)
                    for k in range(KC):
                        mm = nc.tensor.transpose(a_ps[q][0:TT, k * P:(k + 1) * P], xs[q][:, k, :], ident[:, :])
                    mm.then_inc(turned, 1)
            steps(pe, NTILES // Q, to_rows)

            def experts(i):
                for p in range(2):
                    e = 2 * i + p
                    pe.wait_ge(ein_in[p], 16 * (i + 1))
                    if isinstance(e, int) and e == 0:
                        pe.wait_ge(slots_ready, 1)
                        pe.wait_ge(b1_ready, 1)
                    else:
                        pe.wait_ge(ein_ready, e)
                    for k in range(KC):
                        for s in range(4):
                            mm = nc.tensor.transpose(t_ps[k][:, s * ST:(s + 1) * ST], ein[p][:, s, k * P:(k + 1) * P], ident[0:ST, 0:ST])
                    mm.then_inc(ein_turned, 1)
                    pe.wait_ge(w_in[p], 32 * (i + 1))
                    pe.wait_ge(ein_ready, e + 1)
                    for f in range(KF):
                        wait(pe, h_ready, KF * e + f - 3)
                        for k in range(KC):
                            mm = nc.tensor.matmul(a_ps[f % 4][:, 0:CAP], w1[p][:, k, f * P:(f + 1) * P], ein_t[p][:, k, :],
                                                  start=(k == 0), stop=(k == KC - 1))
                        mm.then_inc(h_done, 1)
                    for s in range(4):
                        wait(pe, y_ready, 4 * e + s - 1)
                        for f in range(KF):
                            if s == 0:
                                pe.wait_ge(h_ready, KF * e + f + 1)
                            mm = nc.tensor.matmul(y_ps[s % 2][0:ST, 0:C], h[p][:, f, s * ST:(s + 1) * ST], w2[p][:, f, :],
                                                  start=(f == 0), stop=(f == KF - 1))
                        mm.then_inc(y_done, 1)
            steps(pe, E // 2, experts)

            def back(i):
                for q in range(Q):
                    j = Q * i + q
                    pe.wait_ge(scaled_ready, j + 1)
                    wait(pe, x_done, j - Q + 1)
                    for k in range(KC):
                        mm = nc.tensor.transpose(a_ps[q][:, k * TT:(k + 1) * TT], scaled[q][:, k * P:(k + 1) * P], ident[0:TT, 0:TT])
                    mm.then_inc(back_turned, 1)
            steps(pe, NTILES // Q, back)

        @block.scalar
        def _(act):
            act.preload_act_table_set(LN_EXP)
            act.wait_ge(b1_turned, 1)
            nc.scalar.activation(b1[:, :], y_ps[0][:, 0:E * KF], ACT.Copy).then_inc(b1_ready, 1)
            act.wait_ge(dist_ready, 1)
            nc.scalar.activation(expd[:, :, :], dist[:, :, :], ACT.Exp).then_inc(exp_ready, 1)

            def experts(i):
                for p in range(2):
                    e = 2 * i + p
                    act.wait_ge(ein_turned, e + 1)
                    for k in range(KC):
                        ins = nc.scalar.activation(ein_t[p][:, k, :], t_ps[k][:, 0:CAP], ACT.Copy)
                    ins.then_inc(ein_ready, 1)
                    wait(act, y_done, 4 * (e - 1))
                    for f in range(KF):
                        act.wait_ge(h_done, KF * e + f + 1)
                        nc.scalar.activation(h[p][:, f, :], a_ps[f % 4][:, 0:CAP], ACT.Relu, bias=b1[:, bass.ds(e * KF + f, 1)]).then_inc(h_ready, 1)
            steps(act, E // 2, experts)

        @block.vector
        def _(dve):
            chain = Chain(dve, own)

            def copy_in(j, q):
                nc.vector.tensor_scalar(xs[q][:, :, :], xn[:, :, bass.ds(j * TT, TT)], 1.0, None, ALU.mult).then_inc(copied, 1)

            for i in range(NT // QT):
                dve.wait_ge(scored, i + 1)
                nc.vector.tensor_copy(logits_t[:, i * QT:(i + 1) * QT], a_ps[i % 4][0:E, 0:QT]).then_inc(scored_out, 1)
            dve.wait_ge(consts, 5)
            dve.wait_ge(logits_ready, 1)
            chain.step(nc.vector.tensor_copy(logits[:, :, :], y_ps[1][0:TT, 0:NTILES * E].rearrange("p (j e) -> p j e", e=E)))
            chain.wait()

            def each(t):
                return t[:, :].unsqueeze(2).broadcast_to([TT, NTILES, E])
            chain.step(nc.vector.tensor_reduce(best[:, :], logits[:, :, :], AX_X, ALU.max))
            chain.wait()
            nc.vector.tensor_tensor(dist[:, :, :], logits[:, :, :], each(best), ALU.subtract).then_inc(dist_ready, 1)
            dve.wait_ge(dist_ready, 1)
            chain.step(nc.vector.tensor_scalar(cand[:, :, :], dist[:, :, :], 0.0, -float(E), ALU.is_ge, ALU.mult))
            chain.wait()
            chain.step(nc.vector.tensor_tensor(cand[:, :, :], cand[:, :, :], e_num[:, :, :], ALU.add))
            chain.wait()
            chain.step(nc.vector.tensor_reduce(first[:, :], cand[:, :, :], AX_X, ALU.min))
            chain.wait()
            nc.vector.tensor_tensor(onehot[:, :, :], cand[:, :, :], each(first), ALU.is_equal).then_inc(onehot_ready, 1)
            dve.wait_ge(exp_ready, 1)
            chain.step(nc.vector.tensor_reduce(total[:, :], expd[:, :, :], AX_X, ALU.add))
            chain.wait()
            chain.step(nc.vector.reciprocal(gate[:, :], total[:, :]))
            dve.wait_ge(counted, 1)
            chain.step(nc.vector.tensor_copy(before[0][:, 1:NTILES, :],
                                             t_ps[1][0:TT, 0:(NTILES - 1) * E].rearrange("p (j e) -> p j e", e=E)))
            chain.step(nc.vector.memset(before[0][:, 0:1, :], 0.0))
            d, src = 1, 0
            while d < NTILES:
                chain.wait()
                a, b = before[src], before[1 - src]
                chain.step(nc.vector.tensor_tensor(b[:, d:NTILES, :], a[:, d:NTILES, :], a[:, 0:NTILES - d, :], ALU.add))
                chain.step(nc.vector.tensor_copy(b[:, 0:d, :], a[:, 0:d, :]))
                d, src = 2 * d, 1 - src
            chain.wait()
            chain.step(nc.vector.tensor_tensor(count[:, :, :], before[src][:, :, :],
                                               t_ps[0][0:TT, 0:NTILES * E].rearrange("p (j e) -> p j e", e=E), ALU.add))
            chain.wait()
            chain.step(nc.vector.tensor_tensor(count[:, :, :], count[:, :, :], onehot[:, :, :], ALU.mult))
            chain.wait()
            chain.step(nc.vector.tensor_reduce(picked[:, :], count[:, :, :], AX_X, ALU.add))
            chain.wait()
            chain.step(nc.vector.tensor_scalar(kept[:, :], picked[:, :], float(CAP), None, ALU.is_le))
            chain.step(nc.vector.tensor_scalar(slot_f[:, :], first[:, :], float(CAP), float(CAP * E - 1), ALU.mult, ALU.add))
            chain.wait()
            chain.step(nc.vector.tensor_tensor(slot_f[:, :], slot_f[:, :], picked[:, :], ALU.add))
            chain.step(nc.vector.tensor_tensor(gate[:, :], gate[:, :], kept[:, :], ALU.mult))
            chain.wait()
            chain.step(nc.vector.tensor_tensor(slot_f[:, :], slot_f[:, :], kept[:, :], ALU.mult))
            chain.step(nc.vector.tensor_tensor(kept[:, :], spare[:, :], kept[:, :], ALU.mult))
            chain.wait()
            chain.step(nc.vector.tensor_tensor(sent_f[:, :], slot_f[:, :], spare[:, :], ALU.add))
            chain.wait()
            chain.step(nc.vector.tensor_tensor(sent_f[:, :], sent_f[:, :], kept[:, :], ALU.subtract))
            chain.wait()
            chain.step(nc.vector.tensor_copy(slot[:, :], slot_f[:, :]))
            nc.vector.tensor_copy(sent[:, :], sent_f[:, :]).then_inc(slots_ready, 1)

            def to_rows(i):
                for q in range(Q):
                    wait(dve, turned, Q * i + q - Q + 1)
                    copy_in(Q * i + q, q)
                for q in range(Q):
                    j = Q * i + q
                    dve.wait_ge(turned, j + 1)
                    nc.vector.tensor_scalar(rows[:, bass.ds(j, 1), :].rearrange("p o c -> p (o c)"), a_ps[q][0:TT, 0:C], 1.0, None,
                                            ALU.mult).then_inc(rows_ready, 1)
            steps(dve, NTILES // Q, to_rows)

            def experts(i):
                for p in range(2):
                    e = 2 * i + p
                    wait(dve, y_out[p], 16 * i)
                    for s in range(4):
                        dve.wait_ge(y_done, 4 * e + s + 1)
                        nc.vector.tensor_tensor(y[p][:, s, :], y_ps[s % 2][0:ST, 0:C], b2[:, bass.ds(e, 1), :].rearrange("p o c -> p (o c)"),
                                                ALU.add).then_inc(y_ready, 1)
            dve.wait_ge(consts_in, 48)
            steps(dve, E // 2, experts)

            def back(i):
                dve.wait_ge(rows_back, i + 1)
                for q in range(Q):
                    j = Q * i + q
                    wait(dve, back_turned, j - Q + 1)
                    nc.vector.tensor_scalar(scaled[q][:, :], rows[:, bass.ds(j, 1), :].rearrange("p o c -> p (o c)"),
                                            gate[:, bass.ds(j, 1)], None, ALU.mult).then_inc(scaled_ready, 1)
                for q in range(Q):
                    j = Q * i + q
                    dve.wait_ge(back_turned, j + 1)
                    xt = x[:, :, bass.ds(j * TT, TT)]
                    nc.vector.tensor_tensor(xt, xt, a_ps[q][:, 0:KC * TT].rearrange("p (k t) -> p k t", k=KC), ALU.add).then_inc(x_done, 1)
            steps(dve, NTILES // Q, back)


def network(nc, w, y_dram):
    with Scope(nc, "net") as S:
        ident, mean_w = constants(nc, S)
        x = S.sb("x", [P, KC, NT])
        l0_conv(nc, w["x"], part(w, "L0_conv_"), x, ident)
        l1_attention(nc, x, part(w, "L1_conv_"), ident)

        a = part(w, "L2_attn_")
        f = part(w, "L2_ffn_")
        xn_dram = nc.dram_tensor("xn_scratch", [KC, P, NT], F32, kind="Internal").ap()
        with Scope(nc, "l2") as T:
            xn = T.sb("xn", [P, KC, NT])
            layer_norm(nc, "ln_l2_attn", x, xn, mean_w, LN_EPS)
            attention(nc, "l2_attn", x, xn, ident, 16, True, 1.0, C ** -0.5, l2_weights(a["w_attn"]),
                      a["w_proj"], a["b_attn"], a["b_proj"])
            layer_norm(nc, "ln_l2_ffn", x, xn, mean_w, LN_EPS, f["norm_w"], RMS_EPS, xn_dram)
        peer_ffn(nc, x, xn_dram, f, ident)

        a = part(w, "L3_attn_")
        with Scope(nc, "l3") as T:
            xn = T.sb("xn", [P, KC, NT])
            layer_norm(nc, "ln_l3_attn", x, xn, mean_w, LN_EPS)
            attention(nc, "l3_attn", x, xn, ident, 8, False, 16 ** -0.5, 1.0, l3_weights(a["Wq"], a["Wk"], a["Wv"]),
                      a["Wout"], None, a["bout"])
            layer_norm(nc, "ln_l3_ffn", x, xn, mean_w, LN_EPS)
            moe_ffn(nc, x, xn, y_dram, part(w, "L3_ffn_"), ident)


def kernel(**inputs):
    import numpy as np
    import concourse.bacc as bacc
    from concourse.bass_utils import run_bass_kernel_spmd

    nc = bacc.Bacc("TRN2", target_bir_lowering=False, num_devices=1)
    arrays, drams = {}, {}
    for name, value in inputs.items():
        value = np.ascontiguousarray(value)
        if name == "x":
            value = value.reshape(B, C, HW)
        arrays[f"in_{name}_dram"] = value
        drams[name] = nc.dram_tensor(f"in_{name}_dram", value.shape, mybir.dt.from_np(value.dtype), kind="ExternalInput").ap()
    out = nc.dram_tensor("out_0_dram", [B, C, HW], F32, kind="ExternalOutput").ap()
    network(nc, drams, out)
    r = run_bass_kernel_spmd(nc, [arrays], core_ids=[0])
    return r.results[0]["out_0_dram"].reshape(B, C, HI, WI)
```
